# Optimizing a Trainium2 kernel written in Bass

```python
import numpy as np
import jax
import jax.numpy as jnp

def _softmax(x, axis=-1):
    return jax.nn.softmax(x, axis=axis)

def _gelu(x):
    return jax.nn.gelu(x, approximate=True)

def _silu(x):
    return jax.nn.silu(x)

def _sigmoid(x):
    return jax.nn.sigmoid(x)

def _layernorm(x, axis=-1, eps=1e-05):
    m = jnp.mean(x, axis=axis, keepdims=True)
    v = jnp.var(x, axis=axis, keepdims=True)
    return (x - m) / jnp.sqrt(v + eps)

def _scatter_add(tgt, idx, src, axis=0):
    return tgt.at[idx].add(src)

def _segment_sum(src, seg, n):
    return jax.ops.segment_sum(src, seg, n)
kernel_name = 'mk_gnn_preln_d4_gnn_r32_ed919b'

def setup_inputs(seed: int=0):
    np.random.seed(seed)
    _w = jnp.asarray

    def _rec_inputs():
        import jax
        import jax.numpy as jnp
        _gk = jax.random.key(seed)
        x = -0.0003713 + 1 * jax.random.normal(jax.random.fold_in(_gk, 1), (3125, 128), jnp.float32)
        src = jax.random.randint(jax.random.fold_in(_gk, 2), (50000,), 0, 3125, jnp.int32)
        dst = jax.random.randint(jax.random.fold_in(_gk, 3), (50000,), 0, 3125, jnp.int32)
        _o = jnp.argsort(dst, stable=True)
        src = src[_o]
        dst = dst[_o]
        edge_weight = jax.random.uniform(jax.random.fold_in(_gk, 13), (50000,), jnp.float32, 0.0, 0.999998)
        return (x, src, dst, edge_weight)
    x, src, dst, edge_weight = _rec_inputs()

    def _L0_gnn_setup():
        import jax, jax.numpy as jnp
        import numpy as np
        N = 3125
        E = 50000
        D_IN = 128
        D_OUT = 128
        ALPHA = 0.2
        EPS = 1e-08
        key = jax.random.key(seed)
        kx, kr, kc, kW, ka = jax.random.split(key, 5)
        x = jax.random.normal(kx, (N, D_IN), dtype=jnp.float32)
        row = jax.random.randint(kr, (E,), 0, N)
        col = jax.random.randint(kc, (E,), 0, N)
        stdv_w = 1.0 / np.sqrt(D_OUT)
        W = jax.random.uniform(kW, (D_IN, D_OUT), jnp.float32, -stdv_w, stdv_w)
        stdv_a = 1.0 / np.sqrt(2 * D_OUT)
        a = jax.random.uniform(ka, (2 * D_OUT, 1), jnp.float32, -stdv_a, stdv_a)
        return {'x': x, 'row': row, 'col': col, 'W': W, 'a': a}
    _L0_gnn_all = _L0_gnn_setup()
    _L0_gnn_in = {k: v for k, v in _L0_gnn_all.items() if k in ('W', 'a')}
    del _L0_gnn_all

    def _L1_gnn_setup():
        import jax, jax.numpy as jnp
        import numpy as np
        N_NODES, N_EDGES, D, N_LAYERS = (50000, 25000, 128, 3)
        LN_EPS = 1e-05

        def _layer_norm(h):
            mu = jnp.mean(h, axis=-1, keepdims=True)
            var = jnp.var(h, axis=-1, keepdims=True)
            return (h - mu) * jax.lax.rsqrt(var + LN_EPS)
        key = jax.random.key(seed)
        k0, k1, k2 = jax.random.split(key, 3)
        x = jax.random.normal(k0, (N_NODES, D), dtype=jnp.float32)
        edge_index = jax.random.randint(k1, (2, N_EDGES), 0, N_NODES, dtype=jnp.int64)
        W = jax.random.normal(k2, (N_LAYERS, D, D), dtype=jnp.float32) * (1.0 / np.sqrt(D))
        b = jnp.zeros((N_LAYERS, D), dtype=jnp.float32)
        return {'x': x, 'edge_index': edge_index, 'W': W, 'b': b}
    _L1_gnn_all = _L1_gnn_setup()
    _L1_gnn_in = {k: v for k, v in _L1_gnn_all.items() if k in ('W', 'b')}
    del _L1_gnn_all

    def _L2_gnn_setup():
        import jax, jax.numpy as jnp
        import numpy as np
        N = 3125
        E = 50000
        ANN = 128
        HID = 128
        S = ANN + HID
        L = 5
        MLP_H = 256
        OUT = 128

        def _forward(x, edge_index, W, w_ih, w_hh, b_ih, b_hh, l0_w, l0_b, l1_w, l1_b):
            n = x.shape[0]
            s = W.shape[-1]
            src, dst = (edge_index[0], edge_index[1])
            h = jnp.pad(x, ((0, 0), (0, s - x.shape[-1])))

            def step(h, Wl):
                m = h @ Wl
                agg = jax.ops.segment_sum(m[src], dst, num_segments=n)
                gi = agg @ w_ih.T + b_ih
                gh = h @ w_hh.T + b_hh
                ir, iz, in_ = jnp.split(gi, 3, axis=-1)
                hr, hz, hn = jnp.split(gh, 3, axis=-1)
                r = jax.nn.sigmoid(ir + hr)
                z = jax.nn.sigmoid(iz + hz)
                ng = jnp.tanh(in_ + r * hn)
                h_new = (1.0 - z) * ng + z * h
                return (h_new, None)
            h, _ = jax.lax.scan(step, h, W)
            cat = jnp.concatenate([h, x], axis=-1)
            y = jax.nn.relu(cat @ l0_w.T + l0_b)
            y = jax.nn.relu(y @ l1_w.T + l1_b)
            return y
        key = jax.random.key(seed)
        ks = jax.random.split(key, 12)
        sc = 0.05
        return {'x': jax.random.normal(ks[0], (N, ANN), dtype=jnp.float32), 'edge_index': jax.random.randint(ks[1], (2, E), 0, N, dtype=jnp.int64), 'W': jax.random.normal(ks[2], (L, S, S), dtype=jnp.float32) * sc, 'w_ih': jax.random.normal(ks[3], (3 * S, S), dtype=jnp.float32) * sc, 'w_hh': jax.random.normal(ks[4], (3 * S, S), dtype=jnp.float32) * sc, 'b_ih': jax.random.normal(ks[5], (3 * S,), dtype=jnp.float32) * sc, 'b_hh': jax.random.normal(ks[6], (3 * S,), dtype=jnp.float32) * sc, 'l0_w': jax.random.normal(ks[7], (MLP_H, S + ANN), dtype=jnp.float32) * sc, 'l0_b': jax.random.normal(ks[8], (MLP_H,), dtype=jnp.float32) * sc, 'l1_w': jax.random.normal(ks[9], (OUT, MLP_H), dtype=jnp.float32) * sc, 'l1_b': jax.random.normal(ks[10], (OUT,), dtype=jnp.float32) * sc}
    _L2_gnn_all = _L2_gnn_setup()
    _L2_gnn_in = {k: v for k, v in _L2_gnn_all.items() if k in ('W', 'w_ih', 'w_hh', 'b_ih', 'b_hh', 'l0_w', 'l0_b', 'l1_w', 'l1_b')}
    del _L2_gnn_all

    def _L3_gnn_setup():
        import jax, jax.numpy as jnp
        import numpy as np
        N = 3125
        D = 128
        E = 18750
        key = jax.random.key(seed)
        k = jax.random.split(key, 7)
        x = jax.random.normal(k[0], (N, D), dtype=jnp.float32)
        edge_index = jax.random.randint(k[1], (2, E), 0, N, dtype=jnp.int32)
        edge_weight = jax.random.uniform(k[2], (E,), dtype=jnp.float32)
        s = 1.0 / np.sqrt(D)
        W1 = jax.random.uniform(k[3], (D, D), minval=-s, maxval=s, dtype=jnp.float32)
        b1 = jax.random.uniform(k[4], (D,), minval=-s, maxval=s, dtype=jnp.float32)
        W2 = jax.random.uniform(k[5], (D, D), minval=-s, maxval=s, dtype=jnp.float32)
        b2 = jax.random.uniform(k[6], (D,), minval=-s, maxval=s, dtype=jnp.float32)
        return {'x': x, 'edge_index': edge_index, 'edge_weight': edge_weight, 'W1': W1, 'b1': b1, 'W2': W2, 'b2': b2}
    _L3_gnn_all = _L3_gnn_setup()
    _L3_gnn_in = {k: v for k, v in _L3_gnn_all.items() if k in ('W1', 'b1', 'W2', 'b2')}
    del _L3_gnn_all
    return {'x': x, 'src': src, 'dst': dst, 'edge_weight': edge_weight, 'L0_gnn_W': _L0_gnn_in['W'], 'L0_gnn_a': _L0_gnn_in['a'], 'L1_gnn_W': _L1_gnn_in['W'], 'L1_gnn_b': _L1_gnn_in['b'], 'L2_gnn_W': _L2_gnn_in['W'], 'L2_gnn_w_ih': _L2_gnn_in['w_ih'], 'L2_gnn_w_hh': _L2_gnn_in['w_hh'], 'L2_gnn_b_ih': _L2_gnn_in['b_ih'], 'L2_gnn_b_hh': _L2_gnn_in['b_hh'], 'L2_gnn_l0_w': _L2_gnn_in['l0_w'], 'L2_gnn_l0_b': _L2_gnn_in['l0_b'], 'L2_gnn_l1_w': _L2_gnn_in['l1_w'], 'L2_gnn_l1_b': _L2_gnn_in['l1_b'], 'L3_gnn_W1': _L3_gnn_in['W1'], 'L3_gnn_b1': _L3_gnn_in['b1'], 'L3_gnn_W2': _L3_gnn_in['W2'], 'L3_gnn_b2': _L3_gnn_in['b2']}

def reference(x, src, dst, edge_weight, L0_gnn_W, L0_gnn_a, L1_gnn_W, L1_gnn_b, L2_gnn_W, L2_gnn_w_ih, L2_gnn_w_hh, L2_gnn_b_ih, L2_gnn_b_hh, L2_gnn_l0_w, L2_gnn_l0_b, L2_gnn_l1_w, L2_gnn_l1_b, L3_gnn_W1, L3_gnn_b1, L3_gnn_W2, L3_gnn_b2):
    import jax
    import jax.numpy as jnp

    def _L0_gnn_ref(x, row, col, W, a):
        import jax, jax.numpy as jnp
        import numpy as np
        N = 3125
        E = 50000
        D_IN = 128
        D_OUT = 128
        ALPHA = 0.2
        EPS = 1e-08
        h = x @ W
        n = x.shape[0]
        s_src = h @ a[:D_OUT, 0]
        s_dst = h @ a[D_OUT:, 0]
        e = s_src[row] + s_dst[col]
        e = jnp.where(e > 0, e, ALPHA * e)
        row_max = jax.ops.segment_max(e, row, num_segments=n)
        e_exp = jnp.exp(e - row_max[row])
        row_sum = jax.ops.segment_sum(e_exp, row, num_segments=n)
        row_sum = jnp.maximum(row_sum, EPS)
        att = e_exp / row_sum[row]
        h_prime = jax.ops.segment_sum(att[:, None] * h[col], row, num_segments=n)
        return jax.nn.elu(h_prime)

    def _L1_gnn_ref(x, edge_index, W, b):
        import jax, jax.numpy as jnp
        import numpy as np
        N_NODES, N_EDGES, D, N_LAYERS = (50000, 25000, 128, 3)
        LN_EPS = 1e-05

        def _layer_norm(h):
            mu = jnp.mean(h, axis=-1, keepdims=True)
            var = jnp.var(h, axis=-1, keepdims=True)
            return (h - mu) * jax.lax.rsqrt(var + LN_EPS)
        N = x.shape[0]
        loop = jnp.arange(N, dtype=edge_index.dtype)
        src = jnp.concatenate([edge_index[0], loop])
        dst = jnp.concatenate([edge_index[1], loop])
        deg = jax.ops.segment_sum(jnp.ones_like(src, dtype=x.dtype), dst, num_segments=N)
        dinv = jnp.where(deg > 0, jax.lax.rsqrt(jnp.maximum(deg, 1.0)), 0.0)
        norm = dinv[src] * dinv[dst]
        for l in range(N_LAYERS):
            x_raw = x
            h = x @ W[l]
            msg = h[src] * norm[:, None]
            agg = jax.ops.segment_sum(msg, dst, num_segments=N) + b[l]
            h = jax.nn.relu(agg)
            h = _layer_norm(h)
            x = h + x_raw
        return x

    def _L2_gnn_ref(x, edge_index, W, w_ih, w_hh, b_ih, b_hh, l0_w, l0_b, l1_w, l1_b):
        import jax, jax.numpy as jnp
        import numpy as np
        N = 3125
        E = 50000
        ANN = 128
        HID = 128
        S = ANN + HID
        L = 5
        MLP_H = 256
        OUT = 128

        def _forward(x, edge_index, W, w_ih, w_hh, b_ih, b_hh, l0_w, l0_b, l1_w, l1_b):
            n = x.shape[0]
            s = W.shape[-1]
            src, dst = (edge_index[0], edge_index[1])
            h = jnp.pad(x, ((0, 0), (0, s - x.shape[-1])))

            def step(h, Wl):
                m = h @ Wl
                agg = jax.ops.segment_sum(m[src], dst, num_segments=n)
                gi = agg @ w_ih.T + b_ih
                gh = h @ w_hh.T + b_hh
                ir, iz, in_ = jnp.split(gi, 3, axis=-1)
                hr, hz, hn = jnp.split(gh, 3, axis=-1)
                r = jax.nn.sigmoid(ir + hr)
                z = jax.nn.sigmoid(iz + hz)
                ng = jnp.tanh(in_ + r * hn)
                h_new = (1.0 - z) * ng + z * h
                return (h_new, None)
            h, _ = jax.lax.scan(step, h, W)
            cat = jnp.concatenate([h, x], axis=-1)
            y = jax.nn.relu(cat @ l0_w.T + l0_b)
            y = jax.nn.relu(y @ l1_w.T + l1_b)
            return y
        return _forward(x, edge_index, W, w_ih, w_hh, b_ih, b_hh, l0_w, l0_b, l1_w, l1_b)

    def _L3_gnn_ref(x, edge_index, edge_weight, W1, b1, W2, b2):
        import jax, jax.numpy as jnp
        import numpy as np
        N = 3125
        D = 128
        E = 18750
        row, col = (edge_index[0], edge_index[1])
        msgs = edge_weight[:, None] * x[row]
        agg = jax.ops.segment_sum(msgs, col, num_segments=x.shape[0])
        h = (agg + x) @ W1.T + b1 + agg * x @ W2.T + b2
        out = jax.nn.leaky_relu(h, negative_slope=0.2)
        return out
    edge_index = jnp.stack([src, dst])
    h = jnp.maximum(_layernorm(x, axis=-1), 0.0)
    x = x + _L0_gnn_ref(h, src, dst, L0_gnn_W, L0_gnn_a)
    h = jnp.maximum(_layernorm(x, axis=-1), 0.0)
    x = x + _L1_gnn_ref(h, edge_index, L1_gnn_W, L1_gnn_b)
    h = jnp.maximum(_layernorm(x, axis=-1), 0.0)
    x = x + _L2_gnn_ref(h, edge_index, L2_gnn_W, L2_gnn_w_ih, L2_gnn_w_hh, L2_gnn_b_ih, L2_gnn_b_hh, L2_gnn_l0_w, L2_gnn_l0_b, L2_gnn_l1_w, L2_gnn_l1_b)
    h = jnp.maximum(_layernorm(x, axis=-1), 0.0)
    x = x + _L3_gnn_ref(h, edge_index, edge_weight, L3_gnn_W1, L3_gnn_b1, L3_gnn_W2, L3_gnn_b2)
    return x

_drawn_inputs = setup_inputs


def setup_inputs(seed=0):
    import zlib

    import numpy as np

    out = dict(_drawn_inputs(seed))
    spreads = {'L1_gnn_b': (0.0, 0.1)}
    factors = {'L0_gnn_a': 4.663,
     'L2_gnn_b_ih': 2.756,
     'L2_gnn_b_hh': 3.807,
     'L2_gnn_l0_b': 8.0,
     'L2_gnn_l1_b': 3.418,
     'L3_gnn_b1': 7.652,
     'L3_gnn_b2': 7.212}
    for name, (base, spread) in spreads.items():
        noise = np.random.default_rng([zlib.crc32(name.encode()), seed]).standard_normal(out[name].shape)
        drawn = base * np.exp(spread * noise) if base else spread * noise
        out[name] = jnp.asarray(drawn.astype(out[name].dtype))
    for name, factor in factors.items():
        out[name] = (out[name] * factor).astype(out[name].dtype)
    return out
```

```python
import concourse.bass as bass
from concourse import mybir
from concourse.alu_op_type import AluOpType as ALU
from contextlib import ExitStack

N, D, E = 3125, 128, 50000
P = 125
T = N // P
CH = 500
NQ = CH // P
NC = N // CH
LANE = 128
ET = -(-E // LANE)
EG = 4
MID = N // 2
S2 = 256
GL, CL = 5, 3
GATES = 3 * S2
UP = 256.0
EPS = 1e-5
ALPHA = 0.2
BIG = 60000.0
SLOTS = 4
PAD_SRC = N + 1
BATCH = 4
NBATCH = -(-ET // BATCH)
assert NBATCH % 2 == 0 and NBATCH * BATCH <= EG * LANE
ZF = 11
ZW = 6944
TABLE = ZF * LANE * ZW
DUMP = N * N + 8192
FAR = 1000.0
SPLIT = 20
assert TABLE >= DUMP + LANE and TABLE >= (N + 3) * N and PAD_SRC * N < DUMP

f32, f16, i32 = mybir.dt.float32, mybir.dt.float16, mybir.dt.int32
ACT = mybir.ActivationFunctionType
X = mybir.AxisListType.X


def gnn_kernel(nc, x, src, dst, ew, aW, aA, cW, cB, gW, wih, whh, bih, bhh, l0w, l0b, l1w, l1b,
               w1, b1, w2, b2, out):
    ctx = ExitStack()

    def dram(name, shape, dt=f32):
        return nc.dram_tensor(name, shape, dt).ap()

    CT = dram("CT", (T, LANE, N), f16)
    WT = dram("WT", (TABLE, 1))
    keyD = dram("keyD", (EG * LANE, LANE))
    ewD = dram("ewD", (EG * LANE, LANE))
    scatD = dram("scatD", (NBATCH, LANE, 2 * BATCH), i32)
    VD = dram("VD", (GL, LANE, 2 * GATES))
    whhD = dram("whhD", (LANE, 2 * GATES))
    l0D = dram("l0D", (LANE, 3 * 256))
    l1D = dram("l1D", (LANE, 2 * LANE))
    w12D = dram("w12D", (LANE, 2 * LANE))
    rowD = dram("rowD", (2, N))
    xhD = dram("xhD", (P, T, 2, D), f16)
    xh1D = dram("xh1D", (P, T, D))
    hnD = dram("hnD", (P, T, 2, S2), f16)
    hTD = dram("hTD", (128, 2, N))
    xhTD = dram("xhTD", (128, N))
    x1D = dram("x1D", (P, T, D))
    x2D = dram("x2D", (P, T, D))
    colD = dram("colD", (P, 4 * T))

    with ctx:
        def sem(name):
            return ctx.enter_context(nc.semaphore(name))

        PS = [ctx.enter_context(nc.psum_tensor(f"PS{i}", [128, 512], f32)) for i in range(8)]

        setup(nc, sem, PS, x, src, dst, ew, aW, aA, gW, wih, whh, l0w, l1w, w1, w2,
              keyD, ewD, scatD, VD, whhD, l0D, l1D, w12D, xhD, colD, WT, CT, rowD)
        layers(nc, sem, PS, x, aW, cW, cB, bih, bhh, l0b, l1b, b1, b2, out, CT, WT, scatD, VD, whhD, l0D, l1D, w12D,
               rowD, xhD, xh1D, x1D, x2D, colD, hnD, hTD, xhTD)


def setup(nc, sem, PS, x, src, dst, ew, aW, aA, gW, wih, whh, l0w, l1w, w1, w2,
          keyD, ewD, scatD, VD, whhD, l0D, l1D, w12D, xhD, colD, WT, CT, rowD):
    with ExitStack() as c:
        def sb(name, shape, dt=f32):
            return c.enter_context(nc.sbuf_tensor(name, shape, dt))

        srcf = sb("srcf", [128, EG * LANE])
        dstf = sb("dstf", [128, EG * LANE])
        iota = sb("iota", [128, N + 3], f16)
        visits = sb("visits", [1, 3 * 32], i32)
        tcol = sb("tcol", [P, T])
        scol = sb("scol", [P, T])
        ident = sb("ident", [128, 128])
        prepare(nc, sem, PS, x, src, dst, ew, aW, aA, gW, wih, whh, l0w, l1w, w1, w2,
                keyD, ewD, scatD, VD, whhD, l0D, l1D, w12D, xhD, colD,
                srcf, dstf, iota, visits, tcol, scol, ident)
        counts(nc, sem, PS, srcf, dstf, iota, visits, tcol, scol, ident, WT, CT, colD, rowD)


def newton(V_, done, y, v, tmp):
    done(V_.tensor_tensor(tmp, y, y, ALU.mult))
    done(V_.tensor_tensor(tmp, tmp, v, ALU.mult))
    done(V_.tensor_scalar(tmp, tmp, -0.5, 1.5, ALU.mult, ALU.add))
    done(V_.tensor_tensor(y, y, tmp, ALU.mult))


def prepare(nc, sem, PS, x, src, dst, ew, aW, aA, gW, wih, whh, l0w, l1w, w1, w2,
            keyD, ewD, scatD, VD, whhD, l0D, l1D, w12D, xhD, colD,
            srcf, dstf, iota, visits, tcol, scol, ident):
    with ExitStack() as c:
        def sb(name, shape, dt=f32):
            return c.enter_context(nc.sbuf_tensor(name, shape, dt))

        ei = sb("ei", [128, 2, EG, LANE], i32)
        ef = sb("ef", [128, 2, EG, LANE])
        we = sb("we", [128, EG, LANE])
        key = sb("key", [128, EG, LANE])
        near = sb("near", [128, EG, LANE])
        dmin = sb("dmin", [128, EG])
        dmax = sb("dmax", [128, EG])
        tile_no = sb("tile_no", [128, EG])
        base = sb("base", [128, T])
        over = sb("over", [128, EG, 3, T])
        cand = sb("cand", [128, 2, T])
        ends = sb("ends", [T, 2])
        vis = sb("vis", [1, 8, 32])
        keyc = sb("keyc", [128, EG * LANE])
        wc = sb("wc", [128, EG * LANE])
        dump = sb("dump", [128, 1])
        lower = sb("lower", [128, LANE])
        krow = sb("krow", [128, 8, LANE])
        wrow = sb("wrow", [128, 8, LANE])
        junk = sb("junk", [128, 4 * BATCH, LANE])
        wsum = sb("wsum", [128, EG * LANE])
        rank = sb("rank", [128, EG * LANE])
        scat = sb("scat", [128, NBATCH, 2, BATCH], i32)
        xn = sb("xn", [P, T, D])
        sq = sb("sq", [P, T, D])
        pair = sb("pair", [P, T, 2, D], f16)
        st = sb("st", [P, 4, T])
        eps = sb("eps", [128, 1])
        uT = sb("uT", [P, 2, D])
        acol = sb("acol", [128, 2])
        abc = sb("abc", [128, 2, P])
        wihN, whhN = sb("wihN", [128, 6, S2]), sb("whhN", [128, 6, S2])
        l0N, l1N = sb("l0N", [128, 2, 384]), sb("l1N", [128, 1, S2])
        w12N, aWN = sb("w12N", [128, 2, D]), sb("aWN", [128, 1, D])
        gWN = sb("gWN", [128, 2 * GL, S2])
        wihT, whhT = sb("wihT", [128, 2, GATES]), sb("whhT", [128, 2, GATES])
        l0T, l1T = sb("l0T", [128, 3, 256]), sb("l1T", [128, 2, 128])
        w12T, aWT = sb("w12T", [128, 1, 256]), sb("aWT", [128, 1, 128])
        gWT = sb("gWT", [128, 2, GL * S2])
        V = sb("V", [128, 2, 2 * GATES])

        loaded, eloaded, padded, made, chain = (sem(s) for s in ("loaded", "eloaded", "padded", "made", "chain"))
        edge_t, edge_c, w_t, w_c, v_t, v_c, v_st = (
            sem(s) for s in ("edge_t", "edge_c", "w_t", "w_c", "v_t", "v_c", "v_st"))
        keys_out, rows_in, rows_free, eps_r, rstd, u_t = (
            sem(s) for s in ("keys_out", "rows_in", "rows_free", "eps_r", "rstd", "u_t"))
        var_r, root_r, st_out, cand_r, cand_t, ends_r, ends_t = (
            sem(s) for s in ("var_r", "root_r", "st_out", "cand_r", "cand_t", "ends_r", "ends_t"))
        abc_r, outs, edges_r, rows_in2, scat_r = (sem(s) for s in ("abc_r", "outs", "edges_r", "rows_in2", "scat_r"))
        rows_sem = [rows_in, rows_in2]

        def runs(nat, rows, cols, tr, per=4):
            r = []
            for b in range(cols):
                for a in range(0, rows, per):
                    r.append((nat, tr, b, a, min(per, rows - a)))
            return r
        jobs = (runs(aWN, 1, 1, aWT) + runs(wihN, 6, 2, wihT, 3) + runs(gWN, 2 * GL, 2, gWT)
                + runs(whhN, 6, 2, whhT, 3) + runs(l0N, 2, 3, l0T) + runs(l1N, 1, 2, l1T) + runs(w12N, 2, 1, w12T))
        full = (E // (LANE * LANE))
        rest = E - full * LANE * LANE
        rt, rl = rest // LANE, rest % LANE
        edge_dmas = 3 * 3 if rl else 3 * 2
        HALF = 2 * GATES // 4

        with nc.Block() as block:
            @block.gpsimd
            def _(pool):
                nc.gpsimd.memset(ei[:, 0], PAD_SRC).then_inc(padded, 1)
                nc.gpsimd.memset(ei[:, 1], -1).then_inc(padded, 1)
                nc.gpsimd.memset(we[:], 0.0).then_inc(padded, 1)
                nc.gpsimd.memset(eps[:], EPS).then_inc(made, 1)
                nc.gpsimd.iota(iota[:], [[1, N + 3]], base=-MID, channel_multiplier=0,
                               allow_small_or_imprecise_dtypes=True).then_inc(made, 1)
                nc.gpsimd.iota(base[:], [[P, T]], base=0, channel_multiplier=0,
                               allow_small_or_imprecise_dtypes=True).then_inc(made, 1)
                nc.gpsimd.iota(tile_no[:], [[LANE, EG]], base=0, channel_multiplier=1,
                               allow_small_or_imprecise_dtypes=True).then_inc(made, 1)
                nc.gpsimd.iota(dump[:], [[0, 1]], base=DUMP, channel_multiplier=1,
                               allow_small_or_imprecise_dtypes=True).then_inc(made, 1)
                nc.gpsimd.memset(ident[:], 0.0).then_inc(made, 1)
                nc.gpsimd.memset(lower[:], 0.0).then_inc(made, 1)
                pool.wait_ge(made, 7)
                nc.gpsimd.affine_select(out=ident[:], in_=ident[:], compare_op=ALU.not_equal, fill=1.0,
                                        base=0, pattern=[[-1, 128]], channel_multiplier=1).then_inc(made, 1)
                nc.gpsimd.affine_select(out=lower[:], in_=lower[:], compare_op=ALU.is_ge, fill=1.0,
                                        base=0, pattern=[[1, 128]], channel_multiplier=-1).then_inc(made, 1)

            @block.sync
            def _(sp):
                sp.wait_ge(padded, 3)
                for n, (arr, to) in enumerate(((src, ei[:, 0]), (dst, ei[:, 1]), (ew, we))):
                    m = full * LANE * LANE
                    sp.dma_start(to[:, 0:full, :], arr[0:m].rearrange("(g t e) -> t g e", t=LANE, e=LANE)).then_inc(eloaded, 16)
                    sp.dma_start(to[0:rt, full, :], arr[m:m + rt * LANE].rearrange("(t e) -> t e", e=LANE)).then_inc(eloaded, 16)
                    if rl:
                        m += rt * LANE
                        sp.dma_start(to[rt:rt + 1, full, 0:rl], arr[m:E].rearrange("(t e) -> t e", t=1)).then_inc(eloaded, 16)
                sp.wait_ge(edges_r, 1)
                sp.dma_start(keyD.rearrange("(g t) e -> t g e", g=EG), key[:]).then_inc(keys_out, 16)
                sp.dma_start(ewD.rearrange("(g t) e -> t g e", g=EG), we[:]).then_inc(keys_out, 16)
                sp.wait_ge(keys_out, 32)
                with sp.Fori(0, NBATCH // 2) as i:
                    for h in range(2):
                        sp.wait_ge(rows_free, 2 * i + h + 1)
                        for d_, s_ in ((krow, keyD), (wrow, ewD)):
                            rows = s_[bass.ds((2 * i + h) * BATCH, BATCH), :].rearrange("(o t) e -> o (t e)", o=1)
                            sp.dma_start(d_[:, h * BATCH:(h + 1) * BATCH, :].rearrange("p t e -> p (t e)"),
                                         rows.to_broadcast([128, BATCH * LANE])).then_inc(rows_sem[h], 16)
                sp.wait_ge(scat_r, 2)
                sp.dma_start(scatD.rearrange("b p c -> p b c"), scat[:].rearrange("p b k c -> p b (k c)")).then_inc(outs, 16)
                sp.wait_ge(st_out, 1)
                sp.dma_start(xhD, pair[:]).then_inc(outs, 16)
                sp.wait_ge(w_c, len(jobs))
                for d_, s_ in ((whhD, whhT), (l0D, l0T), (l1D, l1T), (w12D, w12T)):
                    sp.dma_start(d_, s_[:].rearrange("p a b -> p (a b)")).then_inc(outs, 16)
                sp.wait_ge(outs, 16 * 6)

            @block.tensor
            def _(pe):
                pe.wait_ge(made, 9)
                n = [0]

                def bank():
                    i = n[0]
                    if i >= 6:
                        pe.wait_ge(w_c, i - 5)
                    n[0] += 1
                    return PS[i % 6]
                pe.wait_ge(loaded, 16 * 9)
                for nat, tr, b, a, m in jobs:
                    ps = bank()
                    for q in range(m):
                        last = nc.tensor.transpose(ps[:, q * 128:(q + 1) * 128], nat[:, a + q, b * 128:(b + 1) * 128], ident[:])
                    last.then_inc(w_t, 1)
                pe.wait_ge(abc_r, 1)
                pe.wait_ge(w_c, len(jobs))
                for h in range(2):
                    last = nc.tensor.matmul(PS[0][0:P, h * 128:(h + 1) * 128], abc[:, h, :], aWT[:, 0, :], start=True, stop=True)
                last.then_inc(u_t, 1)
                pe.wait_ge(edges_r, 1)
                for g in range(EG):
                    if g:
                        pe.wait_ge(edge_c, g)
                    for q, a in enumerate((ef[:, 0, g], ef[:, 1, g], key[:, g], we[:, g])):
                        last = nc.tensor.transpose(PS[6][:, q * 128:(q + 1) * 128], a, ident[:])
                    last.then_inc(edge_t, 1)
                pe.wait_ge(cand_r, 1)
                for h in range(2):
                    last = nc.tensor.transpose(PS[7][0:T, h * 128:(h + 1) * 128], cand[:, h, :], ident[:])
                last.then_inc(cand_t, 1)
                pe.wait_ge(ends_r, 1)
                for h in range(2):
                    last = nc.tensor.transpose(PS[7][0:1, 256 + 32 * h:256 + 32 * h + T], ends[:, h:h + 1], ident[0:T, 0:T])
                last.then_inc(ends_t, 1)
                pe.wait_ge(u_t, 1)
                for l in range(GL):
                    for kt in range(2):
                        for h in range(2):
                            i = (l * 2 + kt) * 2 + h
                            if i >= 4:
                                pe.wait_ge(v_c, i - 3)
                            for mt in range(2):
                                last = nc.tensor.matmul(PS[1 + i % 4][:, 0:HALF],
                                                        gWT[:, mt, l * S2 + kt * 128:l * S2 + (kt + 1) * 128],
                                                        wihT[:, mt, h * HALF:(h + 1) * HALF], start=(mt == 0), stop=(mt == 1))
                            last.then_inc(v_t, 1)

            @block.scalar
            def _(act):
                act.dma_start(aWN[:, 0, :], aW).then_inc(loaded, 16)
                act.dma_start(wihN[:], wih.rearrange("(a p) m -> p a m", p=128)).then_inc(loaded, 16)
                act.dma_start(gWN[:], gW.rearrange("l (a p) m -> p (l a) m", p=128)).then_inc(loaded, 16)
                act.dma_start(whhN[:], whh.rearrange("(a p) m -> p a m", p=128)).then_inc(loaded, 16)
                act.dma_start(l0N[:], l0w.rearrange("(a p) m -> p a m", p=128)).then_inc(loaded, 16)
                act.dma_start(l1N[:, 0, :], l1w).then_inc(loaded, 16)
                act.dma_start(w12N[:, 0, :], w1).then_inc(loaded, 16)
                act.dma_start(w12N[:, 1, :], w2).then_inc(loaded, 16)
                act.dma_start(acol[:], aA.rearrange("(h p) o -> p (h o)", p=128), allow_slow_non_contiguous=True).then_inc(loaded, 16)
                act.dma_start(xn[:], x.rearrange("(k p) d -> p k d", p=P)).then_inc(rstd, 16)
                for i, (nat, tr, b, a, m) in enumerate(jobs):
                    act.wait_ge(w_t, i + 1)
                    nc.scalar.copy(tr[:, b, a * 128:(a + m) * 128], PS[i % 6][:, 0:m * 128]).then_inc(w_c, 1)
                act.wait_ge(var_r, 1)
                act.wait_ge(made, 1)
                nc.scalar.activation(st[:, 1, :], st[:, 0, :], ACT.Sqrt, bias=eps[0:P, :], scale=1.0 / D).then_inc(root_r, 1)
                for i in range(4 * GL):
                    l, j = i // 4, i % 4
                    act.wait_ge(v_t, i + 1)
                    if l >= 2 and j == 0:
                        act.wait_ge(v_st, 16 * (l - 1))
                    nc.scalar.copy(V[:, l % 2, (j // 2) * GATES + (j % 2) * HALF:(j // 2) * GATES + (j % 2 + 1) * HALF],
                                   PS[1 + i % 4][:, 0:HALF]).then_inc(v_c, 1)
                    if j == 3:
                        act.wait_ge(v_c, i + 1)
                        if l:
                            act.wait_ge(v_st, 16 * l)
                        act.dma_start(VD[l], V[:, l % 2, :]).then_inc(v_st, 16)
                act.wait_ge(v_st, 16 * GL)

            @block.vector
            def _(dve):
                n = [0]

                def done(ins):
                    n[0] += 1
                    ins.then_inc(chain, 1)
                    dve.wait_ge(chain, n[0])
                V_ = nc.vector
                dve.wait_ge(loaded, 16 * 9)
                last = V_.tensor_copy(abc[:], acol[:, :, None].to_broadcast([128, 2, P]))
                last.then_inc(abc_r, 1)
                dve.wait_ge(eloaded, 16 * edge_dmas)
                done(V_.tensor_copy(ef[:], ei[:]))
                V_.scalar_tensor_tensor(key[:], ef[:, 0], float(N), ef[:, 1], ALU.mult, ALU.add).then_inc(edges_r, 1)
                dve.wait_ge(edges_r, 1)
                for g in range(EG):
                    dve.wait_ge(edge_t, g + 1)
                    cols = slice(g * LANE, (g + 1) * LANE)
                    V_.tensor_scalar(srcf[:, cols], PS[6][:, 0:128], -float(MID), None, ALU.add)
                    V_.tensor_scalar(dstf[:, cols], PS[6][:, 128:256], -float(MID), None, ALU.add)
                    V_.tensor_copy(keyc[:, cols], PS[6][:, 256:384])
                    V_.tensor_copy(wc[:, cols], PS[6][:, 384:512]).then_inc(edge_c, 1)
                done(V_.tensor_scalar(near[:], ef[:, 1], 0.0, 1e5, ALU.is_lt, ALU.mult))
                done(V_.tensor_tensor(near[:], near[:], ef[:, 1], ALU.add))
                V_.tensor_reduce(dmin[:], near[:], X, ALU.min)
                done(V_.tensor_reduce(dmax[:], ef[:, 1], X, ALU.max))
                done(V_.tensor_scalar(dmin[:], dmin[:], -float(P - 1), None, ALU.add))
                dve.wait_ge(made, 9)
                for g in range(EG):
                    done(V_.tensor_scalar(over[:, g, 1, :], base[:], dmax[:, g:g + 1], None, ALU.is_le))
                    done(V_.scalar_tensor_tensor(over[:, g, 0, :], base[:], dmin[:, g:g + 1], over[:, g, 1, :], ALU.is_ge, ALU.mult))
                    done(V_.tensor_scalar(over[:, g, 1, :], over[:, g, 0, :], tile_no[:, g:g + 1], None, ALU.mult))
                    V_.tensor_tensor(over[:, g, 2, :], over[:, g, 1, :], over[:, g, 0, :], ALU.add)
                    done(V_.scalar_tensor_tensor(over[:, g, 1, :], over[:, g, 0, :], -FAR, over[:, g, 1, :], ALU.mult, ALU.add))
                for g in range(1, EG):
                    a = (cand[:, 0, :], cand[:, 1, :]) if g > 1 else (over[:, 0, 1, :], over[:, 0, 2, :])
                    V_.tensor_tensor(cand[:, 0, :], a[0], over[:, g, 1, :], ALU.min)
                    done(V_.tensor_tensor(cand[:, 1, :], a[1], over[:, g, 2, :], ALU.max))
                V_.tensor_copy(cand[:, 0, :], cand[:, 0, :]).then_inc(cand_r, 1)
                dve.wait_ge(cand_t, 1)
                V_.tensor_reduce(ends[:, 0:1], PS[7][0:T, 0:128], X, ALU.min)
                done(V_.tensor_reduce(ends[:, 1:2], PS[7][0:T, 128:256], X, ALU.max))
                done(V_.tensor_scalar(ends[:, 0:1], ends[:, 0:1], FAR, float(ET - 1), ALU.add, ALU.min))
                V_.scalar_tensor_tensor(ends[:, 1:2], ends[:, 0:1], 4.0, ends[:, 1:2], ALU.add, ALU.max).then_inc(ends_r, 1)
                dve.wait_ge(ends_t, 1)
                done(V_.memset(vis[:], 0.0))
                done(V_.tensor_copy(vis[:, 0:2, 0:T], PS[7][0:1, 256:320].rearrange("p (h c) -> p h c", h=2)[:, :, 0:T]))
                done(V_.tensor_tensor(vis[:, 2, 0:T], vis[:, 1, 0:T], vis[:, 0, 0:T], ALU.subtract))
                done(V_.tensor_tensor_scan(vis[:, 3, 0:T], vis[:, 2, 0:T], vis[:, 7, 0:T], 0.0, ALU.add, ALU.add))
                done(V_.tensor_tensor(vis[:, 4, 0:T], vis[:, 3, 0:T], vis[:, 2, 0:T], ALU.subtract))
                done(V_.scalar_tensor_tensor(vis[:, 5, 0:T], vis[:, 0, 0:T], FAR, vis[:, 4, 0:T], ALU.add, ALU.subtract))
                V_.tensor_copy(visits[:, 0:32], vis[:, 4, :])
                V_.tensor_copy(visits[:, 32:64], vis[:, 3, :])
                done(V_.tensor_copy(visits[:, 64:96], vis[:, 5, :]))
                dve.wait_ge(rstd, 16)
                bc = lambda a: a[:, :, None].to_broadcast([P, T, D])
                done(V_.tensor_reduce(st[:, 2, :], xn[:], X, ALU.add))
                done(V_.tensor_scalar(st[:, 3, :], st[:, 2, :], 1.0 / D, None, ALU.mult))
                done(V_.tensor_tensor(xn[:], xn[:], bc(st[:, 3, :]), ALU.subtract))
                done(V_.tensor_tensor(sq[:], xn[:], xn[:], ALU.mult))
                V_.tensor_reduce(st[:, 0, :], sq[:], X, ALU.add).then_inc(var_r, 1)
                dve.wait_ge(root_r, 1)
                done(V_.reciprocal(st[:, 2, :], st[:, 1, :]))
                done(V_.tensor_scalar(st[:, 0, :], st[:, 0, :], 1.0 / D, EPS, ALU.mult, ALU.add))
                newton(V_, done, st[:, 2, :], st[:, 0, :], st[:, 1, :])
                done(V_.tensor_tensor(xn[:], xn[:], bc(st[:, 2, :]), ALU.mult))
                done(V_.tensor_scalar(sq[:], xn[:], 0.0, None, ALU.max))
                done(V_.tensor_scalar(xn[:], sq[:], UP, None, ALU.mult))
                done(V_.tensor_copy(pair[:, :, 0, :], xn[:]))
                V_.tensor_tensor(pair[:, :, 1, :], xn[:], pair[:, :, 0, :], ALU.subtract).then_inc(st_out, 1)
                dve.wait_ge(st_out, 1)
                dve.wait_ge(u_t, 1)
                done(V_.tensor_copy(uT[:].rearrange("p h d -> p (h d)"), PS[0][0:P, 0:256]))
                for h, to in enumerate((scol, tcol)):
                    done(V_.tensor_tensor(xn[:], sq[:], uT[:, h:h + 1, :].to_broadcast([P, T, D]), ALU.mult))
                    done(V_.tensor_reduce(to[:], xn[:], X, ALU.add))
                dve.sem_inc(rows_free, 2)
                with dve.Fori(0, NBATCH // 2) as i:
                    for h in range(2):
                        dve.wait_ge(rows_sem[h], 32 * i + 32)
                        dve.wait_ge(rows_free, 2 * i + h + 1)
                        for q in range(BATCH):
                            t = (2 * i + h) * BATCH + q
                            r = h * BATCH + q
                            V_.scalar_tensor_tensor(junk[:, 2 * r, :], krow[:, r, :], keyc[:, bass.ds(t, 1)], wrow[:, r, :],
                                                    ALU.is_equal, ALU.mult, accum_out=wsum[:, bass.ds(t, 1)])
                            last = V_.scalar_tensor_tensor(junk[:, 2 * r + 1, :], krow[:, r, :], keyc[:, bass.ds(t, 1)], lower[:],
                                                           ALU.is_equal, ALU.mult, accum_out=rank[:, bass.ds(t, 1)])
                        last.then_inc(rows_free, 1)
                dve.wait_ge(rows_free, NBATCH + 2)
                nt = NBATCH * BATCH
                done(V_.tensor_scalar(wc[:, 0:nt], keyc[:, 0:nt], dump[:], -1.0, ALU.subtract, ALU.mult))
                done(V_.scalar_tensor_tensor(wc[:, 0:nt], rank[:, 0:nt], 0.0, wc[:, 0:nt], ALU.is_gt, ALU.mult))
                V_.tensor_tensor(scat[:, :, 0, :], wc[:, 0:nt].rearrange("p (b q) -> p b q", q=BATCH),
                                 keyc[:, 0:nt].rearrange("p (b q) -> p b q", q=BATCH), ALU.add).then_inc(scat_r, 1)
                V_.tensor_copy(scat[:, :, 1, :].bitcast(f32), wsum[:, 0:nt].rearrange("p (b q) -> p b q", q=BATCH)).then_inc(scat_r, 1)


def counts(nc, sem, PS, srcf, dstf, iota, visits, tcol, scol, ident, WT, CT, colD, rowD):
    with ExitStack() as c:
        def sb(name, shape, dt=f32):
            return c.enter_context(nc.sbuf_tensor(name, shape, dt))

        ohs = sb("ohs", [128, SLOTS, N + 1], f16)
        ohd = sb("ohd", [128, SLOTS, 128], f16)
        cd = sb("cd", [128, 2, N], f16)
        nz = sb("nz", [P, N], f16)
        acc = sb("acc", [P, N])
        deg = sb("deg", [128, T])
        zero = sb("zero", [128, ZW])
        col = sb("col", [P, 4, T])
        root = sb("root", [P, 3, T])
        top = sb("top", [P, 3, T])
        srows = sb("srows", [T, 2, P])
        oh_made, oh_used, act_out, dve_out, nz_made, acc_made, stored, zeros, zero_set, ones_set = (
            sem(s) for s in ("oh_made", "oh_used", "act_out", "dve_out", "nz_made", "acc_made", "stored", "zeros", "zero_set", "ones_set"))
        acc_t, acc_r, deg_r, root_r2, col_r, rows_r, rows_t, rows_c, col_out, chain2 = (
            sem(s) for s in ("acc_t", "acc_r", "deg_r", "root_r2", "col_r", "rows_r", "rows_t", "rows_c", "col_out", "chain2"))
        W = [CH] * NC + [N - NC * CH]
        AB, DB = (0, 2, 4, 6), (1, 3, 5)

        def bucket(eng, d):
            v0 = eng.value_load(visits[0:1, bass.ds(d, 1)], min_val=0, max_val=ET * T)
            v1 = eng.value_load(visits[0:1, bass.ds(d + 32, 1)], min_val=3, max_val=ET * T + 3 * T)
            return v0, v1

        with nc.Block() as block:
            @block.gpsimd
            def _(pool):
                nc.gpsimd.memset(ohs[:, :, N:N + 1], 1.0).then_inc(ones_set, 1)
                nc.gpsimd.memset(zero[:], 0.0).then_inc(zero_set, 1)

            @block.sync
            def _(sp):
                sp.sem_inc(stored, 32)
                sp.wait_ge(zero_set, 1)
                for z in range(ZF):
                    sp.dma_start(WT[z * LANE * ZW:(z + 1) * LANE * ZW, :].rearrange("(p w) o -> p (w o)", p=LANE), zero[:]).then_inc(zeros, 16)
                with sp.Fori(0, T) as d:
                    sp.wait_ge(act_out, 4 * d + 8)
                    sp.wait_ge(dve_out, 3 * d + 6)
                    sp.wait_ge(stored, 16 * d + 32)
                    sp.dma_start(CT[bass.ds(d, 1)].rearrange("o p n -> (o p) n"),
                                 cd[:, bass.ds(d % 2, 1), :].rearrange("p o n -> p (o n)")).then_inc(stored, 16)
                sp.wait_ge(stored, 16 * T + 32)
                sp.wait_ge(zeros, 16 * ZF)

            @block.vector
            def _(dve):
                V_ = nc.vector
                V_.memset(acc[:], 1e30).then_inc(acc_made, 1)
                dve.wait_ge(ones_set, 1)
                dve.sem_inc(dve_out, 3)
                dve.sem_inc(nz_made, 2)

                def visit(d, v, off):
                    t = nc.s_assert_within(v + off - int(FAR), 0, EG * LANE - 1, skip_runtime_bounds_check_because=
                                           "the table of visits keeps to the edge tiles")
                    dve.wait_ge(oh_used, v + 1)
                    slot = bass.ds(v % SLOTS, 1)
                    V_.tensor_scalar(ohs[:, slot, 0:N].rearrange("p o n -> p (o n)"), iota[:, 0:N], srcf[:, bass.ds(t, 1)], None, ALU.is_equal)
                    V_.tensor_scalar(ohd[:, slot, :].rearrange("p o n -> p (o n)"), iota[:, bass.ds(d * P, 128)], dstf[:, bass.ds(t, 1)],
                                     None, ALU.is_equal).then_inc(oh_made, 1)

                def take(d):
                    v1 = dve.value_load(visits[0:1, bass.ds(d + 32, 1)], min_val=3, max_val=ET * T + 3 * T)
                    half = bass.ds(d % 2, 1)
                    dve.wait_ge(oh_used, v1 + SLOTS)
                    dve.wait_ge(stored, 16 * d + 16)
                    for b in DB:
                        V_.tensor_copy(cd[:, half, b * CH:b * CH + W[b]].rearrange("p o n -> p (o n)"), PS[b][:, 0:W[b]]).then_inc(dve_out, 1)
                    dve.wait_ge(act_out, 4 * d + 8)
                    dve.wait_ge(dve_out, 3 * d + 6)
                    dve.wait_ge(acc_made, d + 1)
                    V_.tensor_scalar(nz[:], cd[0:P, half, :].rearrange("p o n -> p (o n)"), 0.0, BIG, ALU.is_equal, ALU.mult).then_inc(nz_made, 1)
                    dve.wait_ge(nz_made, d + 3)
                    V_.scalar_tensor_tensor(acc[:], nz[:], tcol[:, bass.ds(d, 1)], acc[:], ALU.subtract, ALU.min).then_inc(acc_made, 1)

                def visits_of(d, prior):
                    v0, v1 = bucket(dve, d)
                    off = dve.value_load(visits[0:1, bass.ds(d + 64, 1)], min_val=0, max_val=ET + int(FAR))
                    for i in range(3):
                        visit(d, v0 + i, off)
                    if prior is not None:
                        take(prior)
                    with dve.Fori(v0 + 3, v1) as v:
                        visit(d, v, off)

                visits_of(0, None)
                with dve.Fori(1, T) as d:
                    visits_of(d, d - 1)
                take(T - 1)
                for b in range(NC + 1):
                    dve.wait_ge(acc_t, b + 1)
                    k = W[b] // P
                    V_.tensor_reduce(top[:, 0, b * NQ:b * NQ + k], PS[b][0:P, 0:W[b]].rearrange("p (k q) -> p k q", k=k), X, ALU.min).then_inc(acc_r, 1)
                n = [0]

                def done(ins):
                    n[0] += 1
                    ins.then_inc(chain2, 1)
                    dve.wait_ge(chain2, n[0])
                dve.wait_ge(acc_r, NC + 1)
                done(V_.tensor_tensor(top[:, 1, :], scol[:], top[:, 0, :], ALU.subtract))
                done(V_.scalar_tensor_tensor(top[:, 2, :], top[:, 1, :], ALPHA, top[:, 1, :], ALU.mult, ALU.max))
                V_.tensor_tensor(top[:, 0, :], scol[:], top[:, 2, :], ALU.subtract)
                done(V_.scalar_tensor_tensor(top[:, 1, :], scol[:], ALPHA, top[:, 2, :], ALU.mult, ALU.subtract))
                V_.tensor_copy(col[:, 0, :], tcol[:]).then_inc(rows_r, 1)
                V_.tensor_scalar(col[:, 1, :], tcol[:], ALPHA, None, ALU.mult)
                done(V_.tensor_scalar(root[:, 0, :], deg[0:P, :], 1.0, None, ALU.add))
                V_.tensor_copy(root[:, 1, :], root[:, 0, :]).then_inc(deg_r, 1)
                dve.wait_ge(root_r2, 1)
                done(V_.reciprocal(root[:, 2, :], root[:, 1, :]))
                newton(V_, done, root[:, 2, :], root[:, 0, :], root[:, 1, :])
                V_.tensor_scalar(col[:, 3, :], root[:, 2, :], UP, None, ALU.mult)
                V_.tensor_copy(col[:, 2, :], root[:, 2, :]).then_inc(col_r, 1)
                dve.wait_ge(rows_t, 1)
                V_.tensor_copy(srows[:], PS[7][0:T, 0:256].rearrange("p (h c) -> p h c", h=2)[:, :, 0:P]).then_inc(rows_c, 1)

            @block.scalar
            def _(act):
                act.sem_inc(act_out, 4)
                with act.Fori(0, T) as d:
                    v1 = act.value_load(visits[0:1, bass.ds(d + 32, 1)], min_val=3, max_val=ET * T + 3 * T)
                    half = bass.ds(d % 2, 1)
                    act.wait_ge(oh_used, v1 + SLOTS)
                    act.wait_ge(stored, 16 * d + 16)
                    act.wait_ge(nz_made, d + 1)
                    for b in AB:
                        if b == NC:
                            nc.scalar.copy(deg[:, bass.ds(d, 1)], PS[b][:, W[b]:W[b] + 1])
                        nc.scalar.copy(cd[:, half, b * CH:b * CH + W[b]].rearrange("p o n -> p (o n)"), PS[b][:, 0:W[b]]).then_inc(act_out, 1)
                act.wait_ge(deg_r, 1)
                nc.scalar.activation(root[:, 1, :], root[:, 1, :], ACT.Sqrt).then_inc(root_r2, 1)
                act.wait_ge(col_r, 1)
                act.dma_start(colD, col[:].rearrange("p a t -> p (a t)")).then_inc(col_out, 16)
                act.wait_ge(rows_c, 1)
                act.dma_start(rowD.rearrange("h (k p) -> k h p", p=P), srows[:]).then_inc(col_out, 16)
                act.wait_ge(col_out, 32)

            @block.tensor
            def _(pe):
                pe.sem_inc(oh_used, SLOTS)

                def visit(v, start, stop, d=None):
                    pe.wait_ge(oh_made, v + 1)
                    slot = bass.ds(v % SLOTS, 1)
                    lhs = ohd[:, slot, :].rearrange("p o n -> p (o n)")
                    for b in range(NC + 1):
                        if start:
                            if b in AB:
                                pe.wait_ge(act_out, 4 * d + AB.index(b) + 1)
                            else:
                                pe.wait_ge(dve_out, 3 * d + DB.index(b) + 1)
                        w = W[b] + (b == NC)
                        last = nc.tensor.matmul(PS[b][:, 0:w], lhs, ohs[:, slot, b * CH:b * CH + w].rearrange("p o n -> p (o n)"),
                                                start=start, stop=stop)
                    last.then_inc(oh_used, 1)

                with pe.Fori(0, T) as d:
                    v0, v1 = bucket(pe, d)
                    visit(v0, True, False, d)
                    with pe.Fori(v0 + 1, v1 - 1) as v:
                        visit(v, False, False)
                    visit(v1 - 1, False, True)
                pe.wait_ge(acc_made, T + 1)
                pe.wait_ge(act_out, 4 * T + 4)
                for b in range(NC + 1):
                    for k in range(W[b] // P):
                        last = nc.tensor.transpose(PS[b][0:P, k * P:(k + 1) * P], acc[:, b * CH + k * P:b * CH + (k + 1) * P], ident[0:P, 0:P])
                    last.then_inc(acc_t, 1)
                pe.wait_ge(rows_r, 1)
                for h in range(2):
                    last = nc.tensor.transpose(PS[7][0:T, h * 128:h * 128 + P], top[:, h, :], ident[0:P, 0:P])
                last.then_inc(rows_t, 1)


class Done:

    def __init__(self, eng, sem):
        self.eng, self.sem, self.n = eng, sem, 0

    def __call__(self, ins, start=None):
        self.n += 1
        ins.then_inc(self.sem, 1)
        self.eng.wait_ge(self.sem, self.n if start is None else start + self.n)


def scatter(nc, pool, sems, scat, scatD, WT, first, end):
    got, added, landed = sems
    with pool.Fori(first, end) as b:
        pool.dma_start(scat[:], scatD[bass.ds(b, 1)].rearrange("o p c -> (o p) c")).then_inc(got, 16)
        pool.wait_ge(got, 16 * b + 16)
        pool.sem_inc(landed, 1)
        for q in range(BATCH):
            nc.gpsimd.indirect_dma_start(out=WT, out_offset=bass.IndirectOffsetOnAxis(ap=scat[:, q:q + 1], axis=0),
                                         in_=scat[:, BATCH + q:BATCH + q + 1].bitcast(f32), in_offset=None,
                                         compute_op=ALU.add).then_inc(added, 16)
            pool.wait_ge(added, 16 * (BATCH * b + q + 1))
            pool.sem_inc(landed, 1)


def layers(nc, sem, PS, x, aW, cW, cB, bih, bhh, l0b, l1b, b1, b2, out, CT, WT, scatD, VD, whhD, l0D, l1D, w12D,
           rowD, xhD, xh1D, x1D, x2D, colD, hnD, hTD, xhTD):
    with ExitStack() as c:
        def sb(name, shape, dt=f32):
            return c.enter_context(nc.sbuf_tensor(name, shape, dt))

        A = sb("A", [P, T, T, P], f16)
        ident = sb("identf", [128, 128])
        identh = sb("identh", [128, 128], f16)
        col = sb("cols", [P, 4, T])
        scat = sb("scatp", [128, 2 * BATCH], i32)
        scat_sems = [sem("scat_" + n) for n in ("got", "added", "landed")]
        attention(nc, sem, PS, x, aW, CT, rowD, xhD, xh1D, x1D, colD, A, ident, identh, col)
        convolutions(nc, sem, PS, cW, cB, scat, scat_sems, scatD, WT, xh1D, x1D, x2D, hnD, hTD, xhTD, A, ident, identh, col)
        gru(nc, sem, PS, bih, bhh, scat, scat_sems, scatD, WT, VD, whhD, hnD, hTD, A, ident)
    tail(nc, sem, PS, l0b, l1b, b1, b2, out, WT, l0D, l1D, w12D, x2D, hTD, xhTD)


def norm(V_, done, mid, y, xc, sq, st, relu_to):
    q = y.shape[1]
    bc = lambda a: a[:, :, None].to_broadcast([P, q, D])
    done(V_.tensor_reduce(st[:, 0, :], y, X, ALU.add))
    done(V_.tensor_scalar(st[:, 1, :], st[:, 0, :], 1.0 / D, None, ALU.mult))
    done(V_.tensor_tensor(xc, y, bc(st[:, 1, :]), ALU.subtract))
    done(V_.tensor_tensor(sq, xc, xc, ALU.mult))
    done(V_.tensor_reduce(st[:, 0, :], sq, X, ALU.add))
    mid(V_.tensor_scalar(st[:, 2, :], st[:, 0, :], 1.0 / D, EPS, ALU.mult, ALU.add))
    done(V_.reciprocal(st[:, 0, :], st[:, 3, :]))
    newton(V_, done, st[:, 0, :], st[:, 2, :], st[:, 3, :])
    if relu_to is None:
        done(V_.tensor_tensor(xc, xc, bc(st[:, 0, :]), ALU.mult))
    else:
        done(V_.tensor_tensor(xc, xc, bc(st[:, 0, :]), ALU.mult))
        done(V_.tensor_scalar(relu_to, xc, 0.0, None, ALU.max))


def attention(nc, sem, PS, x, aW, CT, rowD, xhD, xh1D, x1D, colD, A, ident, identh, col):
    with ExitStack() as c:
        def sb(name, shape, dt=f32):
            return c.enter_context(nc.sbuf_tensor(name, shape, dt))

        UN = 5
        xh = sb("xh", [P, T, 2, D], f16)
        sr = sb("sr", [P, 2, CH])
        ct = sb("ct", [128, 2, UN, CH], f16)
        z = sb("z", [P, UN, CH])
        ph = sb("ph", [P, 3, 2, CH], f16)
        inv = sb("inv", [128, CH])
        hT = sb("hT", [128, CH])
        xin = sb("xin", [P, NQ, D])
        ya = sb("ya", [P, NQ, D])
        yb = sb("yb", [P, NQ, D])
        st = sb("sta", [P, 4, NQ])
        W = sb("aWs", [128, D])
        ones = sb("ones", [P, 128], f16)
        names = ("made", "loaded", "sr_in", "sr_free", "ct_in", "a_r", "z_r", "e_r", "p_r", "ph_r", "pl_r", "cell_r", "tr_r",
                 "ev_r", "sum_r", "hT_r", "out_r", "exp_r", "var_r", "root_r", "x_in", "x_out", "y_r", "chain", "sum_free")
        (made, loaded, sr_in, sr_free, ct_in, a_r, z_r, e_r, p_r, ph_r, pl_r, cell_r, tr_r,
         ev_r, sum_r, hT_r, out_r, exp_r, var_r, root_r, x_in, x_out, y_r, chain, sum_free) = (sem("a0_" + n) for n in names)
        xt = x.rearrange("(k p) d -> p k d", p=P)

        def chunks(eng, body):
            with eng.Fori(0, NC) as ch:
                body(ch, CH)
            body(NC, P)

        def cells(eng, ch, stages, lag):
            def step(g, i, first, upto=None):
                for n, stage in enumerate(stages):
                    if not (first and i < n) and (upto is None or upto <= n):
                        k = i - n
                        stage(ch * T + g * UN + k, g * UN + k, k % UN, g if k >= 0 else g - 1)
            for i in range(UN):
                step(0, i, True)
            with eng.Fori(1, T // UN) as g:
                for i in range(UN):
                    step(g, i, False)
            for n in range(1, lag + 1):
                for m in range(n, lag + 1):
                    k = UN - 1 + n - m
                    stages[m](ch * T + T - UN + k, T - UN + k, k, T // UN - 1)

        with nc.Block() as block:
            @block.sync
            def _(sp):
                sp.dma_start(xh[:], xhD).then_inc(loaded, 16)
                sp.dma_start(col[:], colD.rearrange("p (a t) -> p a t", a=4)).then_inc(loaded, 16)
                sp.dma_start(W[:], aW).then_inc(loaded, 16)

                def body(ch, w):
                    k = w // P
                    sp.wait_ge(sr_free, 2 * ch + 2)
                    sp.dma_start(sr[:, :, 0:w], rowD[:, bass.ds(ch * CH, w)].rearrange("(o h) n -> o h n", o=1).to_broadcast([P, 2, w])).then_inc(sr_in, 16)
                    def group(g):
                        n = ch * (T // UN) + g
                        sp.wait_ge(ct_in, 16 * n + 16)
                        sp.wait_ge(cell_r, (n + 1) * UN)
                        sp.wait_ge(p_r, (n + 1) * UN)
                        sp.dma_start(ct[:, bass.ds(n % 2, 1), :, 0:w].rearrange("p o g n -> p (o g) n"),
                                     CT[bass.ds(g * UN, UN), :, bass.ds(ch * CH, w)].rearrange("g p n -> p g n")).then_inc(ct_in, 16)
                    group(0)
                    sp.wait_ge(x_in, 16 * ch + 16)
                    sp.wait_ge(x_out, 32 * ch + 32)
                    sp.dma_start(xin[:, 0:k, :], xt[:, bass.ds(ch * NQ, k), :]).then_inc(x_in, 16)
                    with sp.Fori(1, T // UN) as g:
                        group(g)
                    sp.wait_ge(y_r, 2 * ch + 1)
                    sp.dma_start(x1D[:, bass.ds(ch * NQ, k), :], ya[:, 0:k, :]).then_inc(x_out, 16)
                    sp.wait_ge(y_r, 2 * ch + 2)
                    sp.dma_start(xh1D[:, bass.ds(ch * NQ, k), :], yb[:, 0:k, :]).then_inc(x_out, 16)
                sp.sem_inc(ct_in, 16)
                sp.sem_inc(x_in, 16)
                sp.sem_inc(x_out, 32)
                chunks(sp, body)
                sp.wait_ge(x_out, 32 * (NC + 1) + 32)

            @block.gpsimd
            def _(pool):
                nc.gpsimd.memset(ones[:], 1.0).then_inc(made, 1)
                nc.gpsimd.memset(ident[:], 0.0).then_inc(made, 1)
                nc.gpsimd.memset(identh[:], 0.0).then_inc(made, 1)
                pool.wait_ge(made, 3)
                for m in (ident, identh):
                    nc.gpsimd.affine_select(out=m[:], in_=m[:], compare_op=ALU.not_equal, fill=1.0,
                                            base=0, pattern=[[-1, 128]], channel_multiplier=1).then_inc(made, 1)
                pool.sem_inc(pl_r, UN)

                def body(ch, w):
                    def low(m, j, i, g):
                        pool.wait_ge(ph_r, m + 1)
                        nc.gpsimd.tensor_tensor(ph[:, i % 3, 1, 0:w], z[:, i, 0:w], ph[:, i % 3, 0, 0:w], ALU.subtract).then_inc(pl_r, 1)
                    cells(pool, ch, [low], 0)
                chunks(pool, body)

            @block.scalar
            def _(act):
                act.wait_ge(loaded, 48)

                def body(ch, w):
                    k = w // P
                    act.wait_ge(sr_in, 16 * ch + 16)

                    def lift(m, j, i, g):
                        act.wait_ge(pl_r, m + 1)
                        nc.scalar.activation(z[:, i, 0:w], sr[:, 1, 0:w], ACT.Identity, bias=col[:, 1, bass.ds(j, 1)]).then_inc(a_r, 1)

                    def expo(m, j, i, g):
                        act.wait_ge(z_r, m + 1)
                        nc.scalar.activation(z[:, i, 0:w], z[:, i, 0:w], ACT.Exp).then_inc(e_r, 1)

                    def high(m, j, i, g):
                        act.wait_ge(p_r, m + 1 + 2 * UN)
                        act.wait_ge(cell_r, m - 1 + 2 * UN)
                        nc.scalar.copy(ph[:, i % 3, 0, 0:w], z[:, i, 0:w]).then_inc(ph_r, 1)
                    cells(act, ch, [lift, expo, high], 2)
                    act.sem_inc(sr_free, 1)
                    act.wait_ge(out_r, ch + 1)
                    nc.scalar.activation(yb[:, 0:k, :].rearrange("p k d -> p (k d)"), PS[5][0:P, 0:k * D], ACT.Exp).then_inc(exp_r, 1)
                    act.wait_ge(var_r, ch + 1)
                    nc.scalar.activation(st[:, 3, 0:k], st[:, 2, 0:k], ACT.Sqrt).then_inc(root_r, 1)
                chunks(act, body)

            @block.tensor
            def _(pe):
                pe.wait_ge(made, 5)
                pe.wait_ge(loaded, 48)
                pe.sem_inc(cell_r, 2 * UN)

                def body(ch, w):
                    k = w // P
                    pe.wait_ge(sum_free, ch + 1)

                    def cell(m, j, i, g, start=False, stop=False):
                        hi, lo = ph[:, i % 3, 0, 0:w], ph[:, i % 3, 1, 0:w]
                        xhi = xh[:, bass.ds(j, 1), 0, :].rearrange("p o d -> p (o d)")
                        xlo = xh[:, bass.ds(j, 1), 1, :].rearrange("p o d -> p (o d)")
                        half = (ch * (T // UN) + g) % 2
                        pe.wait_ge(ev_r, m + 1)
                        pe.wait_ge(ct_in, 16 * (ch * (T // UN) + g) + 32)
                        for q in range(k):
                            src = ct[0:P, bass.ds(half, 1), i, q * P:(q + 1) * P].rearrange("p o n -> p (o n)")
                            last = nc.tensor.matmul(PS[2 + i % 3][0:P, q * P:(q + 1) * P], src, identh[0:P, 0:P], start=True, stop=True)
                        last.then_inc(tr_r, 1)
                        pe.wait_ge(ph_r, m + 1)
                        nc.tensor.matmul(PS[0][:, 0:w], xhi, hi, start=start, stop=False)
                        nc.tensor.matmul(PS[0][:, 0:w], xlo, hi, start=False, stop=False)
                        nc.tensor.matmul(PS[1][:, 0:w], ones[:], hi, start=start, stop=False)
                        pe.wait_ge(pl_r, m + 1 + UN)
                        nc.tensor.matmul(PS[0][:, 0:w], xhi, lo, start=False, stop=stop)
                        last = nc.tensor.matmul(PS[1][:, 0:w], ones[:], lo, start=False, stop=stop)
                        last.then_inc(cell_r, 1)
                    for i in range(UN):
                        cell(ch * T + i, i, i, 0, start=(i == 0))
                    with pe.Fori(1, T // UN - 1) as g:
                        for i in range(UN):
                            cell(ch * T + g * UN + i, g * UN + i, i, g)
                    for i in range(UN):
                        g = T // UN - 1
                        cell(ch * T + g * UN + i, g * UN + i, i, g, stop=(i == UN - 1))
                    pe.wait_ge(hT_r, ch + 1)
                    for q in range(k):
                        last = nc.tensor.matmul(PS[5][0:P, q * D:(q + 1) * D], hT[:, q * P:(q + 1) * P], W[:], start=True, stop=True)
                    last.then_inc(out_r, 1)
                chunks(pe, body)

            @block.vector
            def _(dve):
                V_ = nc.vector
                dve.wait_ge(loaded, 48)
                dve.sem_inc(sr_free, 2)
                dve.sem_inc(ev_r, 2)
                dve.sem_inc(p_r, 2 * UN)
                dve.sem_inc(sum_free, 1)

                def body(ch, w):
                    k = w // P
                    dve.wait_ge(sr_in, 16 * ch + 16)

                    def logit(m, j, i, g):
                        dve.wait_ge(a_r, m + 1)
                        V_.scalar_tensor_tensor(z[:, i, 0:w], sr[:, 0, 0:w], col[:, 0, bass.ds(j, 1)], z[:, i, 0:w], ALU.add, ALU.max).then_inc(z_r, 1)

                    def weigh(m, j, i, g):
                        dve.wait_ge(e_r, m + 1)
                        n = ch * (T // UN) + g
                        dve.wait_ge(ct_in, 16 * n + 32)
                        V_.scalar_tensor_tensor(z[:, i, 0:w], z[:, i, 0:w], 1.0, ct[0:P, bass.ds(n % 2, 1), i, 0:w].rearrange("p o n -> p (o n)"),
                                                ALU.min, ALU.mult).then_inc(p_r, 1)

                    def keep(m, j, i, g):
                        dve.wait_ge(tr_r, m + 1)
                        V_.tensor_copy(A[:, bass.ds(j, 1), bass.ds(ch * NQ, k), :].rearrange("p o k n -> p (o k n)"),
                                       PS[2 + i % 3][0:P, 0:w]).then_inc(ev_r, 1)
                    cells(dve, ch, [logit, weigh, keep], 2)
                    dve.sem_inc(sr_free, 1)
                    dve.wait_ge(cell_r, ch * T + T + 2 * UN)
                    K_ = 17
                    n0 = done.n

                    def dn(ins):
                        done.n += 1
                        ins.then_inc(chain, 1)
                        dve.wait_ge(chain, ch * K_ + done.n - n0)
                    dn(V_.tensor_scalar(inv[:, 0:w], PS[1][:, 0:w], 1e-8, None, ALU.max))
                    dn(V_.reciprocal(inv[:, 0:w], inv[:, 0:w]))
                    V_.scalar_tensor_tensor(hT[:, 0:w], PS[0][:, 0:w], 1.0 / UP, inv[:, 0:w], ALU.mult, ALU.mult).then_inc(hT_r, 1)
                    dve.wait_ge(hT_r, ch + 1)
                    dve.sem_inc(sum_free, 1)
                    o = PS[5][0:P, 0:k * D].rearrange("p (k d) -> p k d", d=D)
                    y, t = ya[:, 0:k, :], yb[:, 0:k, :]
                    dve.wait_ge(exp_r, ch + 1)
                    dn(V_.tensor_scalar(t, t, 1.0, -1.0, ALU.min, ALU.add))
                    dn(V_.scalar_tensor_tensor(t, o, 0.0, t, ALU.max, ALU.add))
                    dve.wait_ge(x_in, 16 * ch + 32)
                    dn(V_.tensor_tensor(y, t, xin[:, 0:k, :], ALU.add))
                    dve.sem_inc(y_r, 1)

                    def mid(ins):
                        ins.then_inc(var_r, 1)
                        dve.wait_ge(root_r, ch + 1)
                    norm(V_, dn, mid, y, t, xin[:, 0:k, :], st[:, :, 0:k], t)
                    dve.sem_inc(y_r, 1)
                    dve.wait_ge(x_out, 32 * ch + 64)
                    assert done.n - n0 == K_, done.n - n0
                done = Done(dve, chain)
                chunks(dve, body)


def convolutions(nc, sem, PS, cW, cB, scat, scat_sems, scatD, WT, xh1D, x1D, x2D, hnD, hTD, xhTD, A, ident, identh, col):
    with ExitStack() as c:
        def sb(name, shape, dt=f32):
            return c.enter_context(nc.sbuf_tensor(name, shape, dt))

        xr = sb("xr", [P, T, D])
        G = sb("G1", [P, 2, T, 2, D], f16)
        F = G[:].rearrange("p a t h d -> p (a t h d)").bitcast(f32).rearrange("p (a t d) -> p a t d", a=2, t=T)
        pair = G[:, 0]
        aT = sb("aT1", [128, CH])
        W = sb("cWs", [128, CL, D])
        bias = sb("cBs", [P, CL, D])
        ya = sb("y1a", [P, NQ, D])
        yb = sb("y1b", [P, NQ, D])
        yc = sb("y1c", [P, NQ, D])
        st = sb("st1", [P, 4, NQ])
        stw = sb("st1w", [P, 4, T])
        hs = sb("hs1", [128, 2, CH])
        zt = sb("zt1", [128, 1, P])
        names = ("loaded", "g_r", "agg_r", "aT_r", "o_r", "var_r", "root_r", "chain", "y_free", "x1_in", "x2_r",
                 "x2_out", "pair_r", "pair_out", "tr_r", "hs_r", "hs_out0", "hs_out1", "zset", "z_out", "var2", "root2", "chain2")
        (loaded, g_r, agg_r, aT_r, o_r, var_r, root_r, chain, y_free, x1_in, x2_r,
         x2_out, pair_r, pair_out, tr_r, hs_r, hs_out0, hs_out1, zset, z_out, var2, root2, chain2) = (sem("c_" + n) for n in names)
        hs_out = (hs_out0, hs_out1)
        SC = NC + 1

        def steps(eng, body):
            with eng.Fori(0, CL) as l:
                with eng.Fori(0, NC) as ch:
                    body(l, ch, CH, l * SC + ch)
                body(l, NC, P, l * SC + NC)

        with nc.Block() as block:
            @block.gpsimd
            def _(pool):
                nc.gpsimd.memset(zt[:], 0.0).then_inc(zset, 1)
                scatter(nc, pool, scat_sems, scat, scatD, WT, 0, SPLIT)

            @block.sync
            def _(sp):
                sp.dma_start(xr[:], xh1D).then_inc(loaded, 16)
                sp.dma_start(W[:], cW.rearrange("l p d -> p l d")).then_inc(loaded, 16)
                sp.dma_start(bias[:], cB.rearrange("(o l) d -> o l d", o=1).to_broadcast([P, CL, D])).then_inc(loaded, 16)
                sp.wait_ge(zset, 1)
                sp.dma_start(hTD[:, 1, :].rearrange("p (t n) -> p t n", n=P), zt[:].to_broadcast([128, T, P])).then_inc(z_out, 16)
                sp.wait_ge(o_r, CL * SC + 1)
                sp.wait_ge(g_r, (CL + 1) * SC)
                sp.dma_start(F[:, 0], x1D).then_inc(x1_in, 16)
                sp.wait_ge(x2_r, 1)
                sp.dma_start(x2D, F[:, 0]).then_inc(x2_out, 16)
                sp.wait_ge(pair_r, 1)
                sp.dma_start(hnD[:, :, :, 0:D], pair).then_inc(pair_out, 16)
                for ch in range(SC):
                    w = min(CH, N - ch * CH)
                    sp.wait_ge(hs_r, ch + 1)
                    for to in (hTD[:, 0, ch * CH:ch * CH + w], xhTD[:, ch * CH:ch * CH + w]):
                        sp.dma_start(to, hs[:, ch % 2, 0:w]).then_inc(hs_out[ch % 2], 16)
                for s_, n in ((x2_out, 16), (pair_out, 16), (hs_out0, 32 * (SC - SC // 2)), (hs_out1, 32 * (SC // 2)), (z_out, 16)):
                    sp.wait_ge(s_, n)

            @block.tensor
            def _(pe):
                pe.wait_ge(loaded, 48)
                pe.sem_inc(o_r, 1)

                def step(l, ch, w, s):
                    k = w // P
                    half = bass.ds(l % 2, 1)
                    pe.wait_ge(g_r, l * SC + SC)
                    for j in range(T):
                        cols = A[:, bass.ds(ch * NQ, k), j, :]
                        for part in range(2):
                            nc.tensor.matmul(PS[0][:, 0:w], G[:, half, j, part, :].rearrange("p o d -> p (o d)"), cols,
                                             start=(j == 0 and part == 0), stop=False)
                    for q in range(k):
                        for part in range(2):
                            last = nc.tensor.matmul(PS[0][:, q * P:(q + 1) * P],
                                                    G[:, half, bass.ds(ch * NQ + q, 1), part, :].rearrange("p o a d -> p (o a d)"),
                                                    identh[0:P, 0:P], start=False, stop=(q == k - 1 and part == 1))
                    last.then_inc(agg_r, 1)
                    pe.wait_ge(aT_r, s + 1)
                    pe.wait_ge(y_free, s + 1)
                    for q in range(k):
                        last = nc.tensor.matmul(PS[1][0:P, q * D:(q + 1) * D], aT[:, q * P:(q + 1) * P],
                                                W[:, bass.ds(l, 1), :].rearrange("p o d -> p (o d)"), start=True, stop=True)
                    last.then_inc(o_r, 1)
                steps(pe, step)
                pe.wait_ge(pair_r, 1)
                for ch in range(SC):
                    if ch >= 2:
                        pe.wait_ge(hs_r, ch - 1)
                    for q in range(min(NQ, T - ch * NQ)):
                        last = nc.tensor.transpose(PS[2 + ch % 2][:, q * P:(q + 1) * P], F[:, 1, ch * NQ + q, :], ident[0:P, 0:P])
                    last.then_inc(tr_r, 1)

            @block.scalar
            def _(act):
                def step(l, ch, w, s):
                    k = w // P
                    act.wait_ge(agg_r, s + 1)
                    act.wait_ge(o_r, s + 1)
                    nc.scalar.activation(aT[:, 0:w], PS[0][:, 0:w], ACT.Copy, scale=1.0 / UP).then_inc(aT_r, 1)
                    act.wait_ge(var_r, s + 1)
                    nc.scalar.activation(st[:, 3, 0:k], st[:, 2, 0:k], ACT.Sqrt).then_inc(root_r, 1)
                steps(act, step)
                act.wait_ge(var2, 1)
                nc.scalar.activation(stw[:, 3, :], stw[:, 2, :], ACT.Sqrt).then_inc(root2, 1)
                for ch in range(SC):
                    w = min(CH, N - ch * CH)
                    act.wait_ge(tr_r, ch + 1)
                    if ch >= 2:
                        act.wait_ge(hs_out[ch % 2], 32 * (ch // 2))
                    nc.scalar.copy(hs[:, ch % 2, 0:w], PS[2 + ch % 2][:, 0:w]).then_inc(hs_r, 1)

            @block.vector
            def _(dve):
                V_ = nc.vector
                dve.wait_ge(loaded, 48)
                dve.sem_inc(y_free, 1)
                dn2 = Done(dve, chain2)
                wide = lambda a: a[:, :, None].to_broadcast([P, T, D])
                dn2(V_.tensor_tensor(F[:, 1], xr[:], wide(col[:, 3, :]), ALU.mult))
                dn2(V_.tensor_copy(G[:, 0, :, 0, :], F[:, 1]))
                dn2(V_.tensor_tensor(G[:, 0, :, 1, :], F[:, 1], G[:, 0, :, 0, :], ALU.subtract))
                dve.sem_inc(g_r, SC)
                done = Done(dve, chain)
                K_ = 17

                def step(l, ch, w, s):
                    k = w // P
                    n0 = done.n

                    def dn(ins):
                        done.n += 1
                        ins.then_inc(chain, 1)
                        dve.wait_ge(chain, s * K_ + done.n - n0)
                    tiles = bass.ds(ch * NQ, k)
                    bc = lambda a: a[:, :, None].to_broadcast([P, k, D])
                    y, xc, sq = ya[:, 0:k, :], yb[:, 0:k, :], yc[:, 0:k, :]
                    dve.wait_ge(o_r, s + 2)
                    dn(V_.tensor_tensor(y, PS[1][0:P, 0:k * D].rearrange("p (k d) -> p k d", d=D), bc(col[:, 2, tiles]), ALU.mult))
                    dve.sem_inc(y_free, 1)
                    dn(V_.tensor_tensor(y, y, bias[:, bass.ds(l, 1), :].to_broadcast([P, k, D]), ALU.add))
                    dn(V_.tensor_scalar(y, y, 0.0, None, ALU.max))

                    def mid(ins):
                        ins.then_inc(var_r, 1)
                        dve.wait_ge(root_r, s + 1)
                    norm(V_, dn, mid, y, xc, sq, st[:, :, 0:k], None)
                    dn(V_.tensor_tensor(xr[:, tiles, :], xr[:, tiles, :], xc, ALU.add))
                    dn(V_.tensor_tensor(y, xr[:, tiles, :], bc(col[:, 3, tiles]), ALU.mult))
                    nxt = bass.ds((l + 1) % 2, 1)
                    dn(V_.tensor_copy(G[:, nxt, tiles, 0, :].rearrange("p o k d -> p (o k) d"), y))
                    V_.tensor_tensor(G[:, nxt, tiles, 1, :].rearrange("p o k d -> p (o k) d"), y,
                                     G[:, nxt, tiles, 0, :].rearrange("p o k d -> p (o k) d"), ALU.subtract).then_inc(g_r, 1)
                    dve.wait_ge(g_r, s + 1 + SC)
                    assert done.n - n0 == K_, done.n - n0
                steps(dve, step)
                dve.wait_ge(x1_in, 16)
                dn2(V_.tensor_tensor(F[:, 0], F[:, 0], xr[:], ALU.add))
                dve.sem_inc(x2_r, 1)

                def mid(ins):
                    ins.then_inc(var2, 1)
                    dve.wait_ge(root2, 1)
                norm(V_, dn2, mid, F[:, 0], F[:, 1], xr[:], stw, F[:, 1])
                dn2(V_.tensor_scalar(xr[:], F[:, 1], UP, None, ALU.mult))
                dve.wait_ge(x2_out, 16)
                dn2(V_.tensor_copy(pair[:, :, 0, :], xr[:]))
                V_.tensor_tensor(pair[:, :, 1, :], xr[:], pair[:, :, 0, :], ALU.subtract).then_inc(pair_r, 1)


def gru(nc, sem, PS, bih, bhh, scat, scat_sems, scatD, WT, VD, whhD, hnD, hTD, A, ident):
    with ExitStack() as c:
        def sb(name, shape, dt=f32):
            return c.enter_context(nc.sbuf_tensor(name, shape, dt))

        G = sb("G2", [P, T, 2, S2], f16)
        V = sb("V2", [128, 2, GATES])
        U = sb("U2", [128, 2, GATES])
        aT = sb("aT2", [128, 2, CH])
        H = sb("H2", [128, 2, CH])
        HN = sb("HN2", [128, 2, CH])
        R = sb("R2", [128, CH])
        stg = sb("stg2", [P, NQ, 2, 128], f16)
        bi = sb("bi2", [128, 6])
        bh = sb("bh2", [128, 6])
        bs = sb("bs2", [128, 4])
        names = ("loaded", "G_in", "V_in", "H_in", "agg_r", "aT_r", "r_g", "h_g", "i_g", "z_g", "r_r", "z_r", "n_r", "u1", "u2",
                 "d_r", "dz_r", "hn_r", "hn_out", "tr_r", "hi_r", "lo_r", "st_out", "bs_r", "tick")
        (loaded, G_in, V_in, H_in, agg_r, aT_r, r_g, h_g, i_g, z_g, r_r, z_r, n_r, u1, u2,
         d_r, dz_r, hn_r, hn_out, tr_r, hi_r, lo_r, st_out, bs_r, tick) = (sem("g_" + n) for n in names)
        SC = NC + 1

        def steps(eng, step, late, end):
            def layer(l, halves):
                step(l, 0, CH, l * SC, halves, lambda: None)
                with eng.Fori(1, NC) as ch:
                    step(l, ch, CH, l * SC + ch, halves, lambda: late(ch - 1, CH, l * SC + ch - 1))
                step(l, NC, P, l * SC + NC, halves, lambda: late(NC - 1, CH, l * SC + NC - 1))
                late(NC, P, l * SC + NC)
                end(l)
            layer(0, 1)
            with eng.Fori(1, GL) as l:
                layer(l, 2)

        with nc.Block() as block:
            @block.gpsimd
            def _(pool):
                scatter(nc, pool, scat_sems, scat, scatD, WT, SPLIT, NBATCH)

            @block.sync
            def _(sp):
                sp.dma_start(G[:, :, :, 0:D], hnD[:, :, :, 0:D]).then_inc(G_in, 16)
                sp.dma_start(V[:], VD[0].rearrange("p (a g) -> p a g", a=2)).then_inc(V_in, 16)
                sp.dma_start(U[:], whhD.rearrange("p (a g) -> p a g", a=2)).then_inc(loaded, 16)
                sp.dma_start(bi[:], bih.rearrange("(c p) -> p c", p=128), allow_slow_non_contiguous=True).then_inc(loaded, 16)
                sp.dma_start(bh[:], bhh.rearrange("(c p) -> p c", p=128), allow_slow_non_contiguous=True).then_inc(loaded, 16)

                def store(e, ch, k, hf):
                    sp.wait_ge(lo_r, e + 3)
                    sp.dma_start(hnD[:, bass.ds(ch * NQ, k), :, hf * 128:(hf + 1) * 128], stg[:, 0:k]).then_inc(st_out, 16)

                def step(l, ch, w, s, halves, late):
                    sp.wait_ge(hn_r, 2 * s + 1)
                    sp.sem_inc(tick, 1)
                    sp.wait_ge(z_g, 2 * s + 2)
                    sp.wait_ge(hn_out, 32 * s + 32)
                    sp.dma_start(H[:, :, 0:w], hTD[:, :, bass.ds(ch * CH, w)]).then_inc(H_in, 16)
                    late()
                    for hf in range(2):
                        sp.wait_ge(hn_r, 2 * s + hf + 2)
                        sp.dma_start(hTD[:, hf, bass.ds(ch * CH, w)], HN[:, hf, 0:w]).then_inc(hn_out, 16)
                    store(2 * s, ch, w // P, 0)

                def late(ch, w, s):
                    store(2 * s + 1, ch, w // P, 1)

                def end(l):
                    sp.wait_ge(st_out, 32 * SC * l + 32 * SC + 16)
                    sp.dma_start(G[:], hnD).then_inc(G_in, 16)
                    nxt = (l + 1) % GL
                    sp.wait_ge(z_g, 2 * SC * l + 2 * SC + 2)
                    sp.dma_start(V[:].rearrange("p a g -> p (a g)"), VD[bass.ds(nxt, 1)].rearrange("o p g -> (o p) g")).then_inc(V_in, 16)
                sp.sem_inc(st_out, 16)
                sp.sem_inc(hn_out, 32)
                steps(sp, step, late, end)
                sp.wait_ge(G_in, 16 * GL + 16)
                sp.wait_ge(V_in, 16 * GL + 16)
                sp.wait_ge(hn_out, 32 * SC * GL + 32)

            @block.tensor
            def _(pe):
                pe.sem_inc(z_g, 2)
                pe.wait_ge(loaded, 48)

                def turn(e, hf, k):
                    pe.wait_ge(hn_r, e + 2)
                    pe.wait_ge(lo_r, e + 1)
                    for q in range(k):
                        last = nc.tensor.transpose(PS[6 + hf][0:P, q * 128:(q + 1) * 128], HN[:, hf, q * P:(q + 1) * P], ident[:])
                    last.then_inc(tr_r, 1)

                def step(l, ch, w, s, halves, late):
                    k = w // P
                    pe.wait_ge(G_in, 16 * l + 16)
                    for half in range(halves):
                        for j in range(T):
                            for part in range(2):
                                last = nc.tensor.matmul(PS[half][:, 0:w], G[:, j, part, half * 128:(half + 1) * 128],
                                                        A[:, bass.ds(ch * NQ, k), j, :],
                                                        start=(j == 0 and part == 0), stop=(j == T - 1 and part == 1))
                    last.then_inc(agg_r, 1)
                    late()
                    pe.wait_ge(aT_r, s + 1)
                    pe.wait_ge(H_in, 16 * s + 16)
                    pe.wait_ge(V_in, 16 * l + 16)
                    for hf in range(2):
                        m = 2 * s + hf

                        def gate(bank, free, ready, g, terms):
                            pe.wait_ge(free, m + 1)
                            terms = [(wt, a, kt) for wt, a in terms for kt in range(halves)]
                            for n, (wt, a, kt) in enumerate(terms):
                                last = nc.tensor.matmul(PS[bank][:, 0:w], wt[:, kt, g:g + 128], a[:, kt, 0:w],
                                                        start=(n == 0), stop=(n == len(terms) - 1))
                            last.then_inc(ready, 1)
                        gate(2, r_r, r_g, hf * 128, ((V, aT), (U, H)))
                        gate(3, u1, h_g, 2 * S2 + hf * 128, ((U, H),))
                        gate(4, u2, i_g, 2 * S2 + hf * 128, ((V, aT),))
                        gate(5, dz_r, z_g, S2 + hf * 128, ((V, aT), (U, H)))
                    turn(2 * s, 0, k)

                def late(ch, w, s):
                    turn(2 * s + 1, 1, w // P)
                steps(pe, step, late, lambda l: None)

            @block.scalar
            def _(act):
                act.wait_ge(bs_r, 1)
                act.sem_inc(r_r, 1)

                def high(e, hf, k):
                    act.wait_ge(tr_r, e + 1)
                    act.wait_ge(st_out, 16 * e + 16)
                    nc.scalar.activation(stg[:, 0:k, 0, :], PS[6 + hf][0:P, 0:k * 128].rearrange("p (k d) -> p k d", k=k),
                                         ACT.Copy, scale=UP).then_inc(hi_r, 1)

                def step(l, ch, w, s, halves, late):
                    act.wait_ge(agg_r, s + 1)
                    act.wait_ge(z_g, 2 * s + 2)
                    for half in range(halves):
                        last = nc.scalar.activation(aT[:, half, 0:w], PS[half][:, 0:w], ACT.Copy, scale=1.0 / UP)
                    last.then_inc(aT_r, 1)
                    late()
                    for hf in range(2):
                        m = 2 * s + hf
                        act.wait_ge(r_g, m + 1)
                        act.wait_ge(hn_r, m + 1)
                        nc.scalar.activation(R[:, 0:w], PS[2][:, 0:w], ACT.Sigmoid, bias=bs[:, hf:hf + 1]).then_inc(r_r, 1)
                        act.wait_ge(z_g, m + 3)
                        nc.scalar.activation(PS[5][:, 0:w], PS[5][:, 0:w], ACT.Sigmoid, bias=bs[:, 2 + hf:3 + hf]).then_inc(z_r, 1)
                        act.wait_ge(u2, m + 2)
                        nc.scalar.activation(R[:, 0:w], R[:, 0:w], ACT.Tanh, bias=bi[:, 4 + hf:5 + hf]).then_inc(n_r, 1)
                    high(2 * s, 0, w // P)

                def late(ch, w, s):
                    high(2 * s + 1, 1, w // P)
                steps(act, step, late, lambda l: None)

            @block.vector
            def _(dve):
                V_ = nc.vector
                dve.wait_ge(loaded, 48)
                V_.tensor_tensor(bs[:], bi[:, 0:4], bh[:, 0:4], ALU.add).then_inc(bs_r, 1)
                for s_, n in ((u1, 1), (u2, 1), (dz_r, 1), (hn_r, 1), (lo_r, 2)):
                    dve.sem_inc(s_, n)

                def low(e, hf, k):
                    dve.wait_ge(hi_r, e + 1)
                    V_.scalar_tensor_tensor(stg[:, 0:k, 1, :], PS[6 + hf][0:P, 0:k * 128].rearrange("p (k d) -> p k d", k=k), UP,
                                            stg[:, 0:k, 0, :], ALU.mult, ALU.subtract).then_inc(lo_r, 1)

                def step(l, ch, w, s, halves, late):
                    late()
                    dve.wait_ge(hn_out, 32 * s + 32)
                    dve.wait_ge(H_in, 16 * s + 16)
                    for hf in range(2):
                        m = 2 * s + hf
                        dve.wait_ge(tr_r, m - 1 + (hf == 0)) if not isinstance(m, int) or m > 1 else None
                        dve.wait_ge(r_r, m + 2)
                        dve.wait_ge(h_g, m + 1)
                        r, n = R[:, 0:w], HN[:, hf, 0:w]
                        V_.scalar_tensor_tensor(r, PS[3][:, 0:w], bh[:, 4 + hf:5 + hf], r, ALU.add, ALU.mult).then_inc(u1, 1)
                        dve.wait_ge(u1, m + 2)
                        dve.wait_ge(i_g, m + 1)
                        V_.tensor_tensor(r, r, PS[4][:, 0:w], ALU.add).then_inc(u2, 1)
                        dve.wait_ge(n_r, m + 1)
                        V_.tensor_tensor(n, H[:, hf, 0:w], r, ALU.subtract).then_inc(d_r, 1)
                        dve.wait_ge(d_r, m + 1)
                        dve.wait_ge(z_r, m + 1)
                        V_.tensor_tensor(n, n, PS[5][:, 0:w], ALU.mult).then_inc(dz_r, 1)
                        dve.wait_ge(dz_r, m + 2)
                        V_.tensor_tensor(n, n, r, ALU.add).then_inc(hn_r, 1)
                    low(2 * s, 0, w // P)

                def late(ch, w, s):
                    low(2 * s + 1, 1, w // P)
                steps(dve, step, late, lambda l: None)


def tail(nc, sem, PS, l0b, l1b, b1, b2, out, WT, l0D, l1D, w12D, x2D, hTD, xhTD):
    with ExitStack() as c:
        def sb(name, shape, dt=f32):
            return c.enter_context(nc.sbuf_tensor(name, shape, dt))

        RING = 5
        wt = sb("wt", [128, RING, N])
        hT = sb("hT3", [128, 2, CH])
        xT = sb("xT3", [128, CH])
        x3 = sb("x3", [P, T, D])
        xc = sb("xc3", [P, T, D])
        sq = sb("sq3", [P, T, D])
        st = sb("st3", [P, 4, T])
        x3T = sb("x3T", [128, N])
        y0 = sb("y0", [128, 2, CH])
        y1 = sb("y1", [128, CH])
        a = sb("a3", [128, 2, CH])
        b = sb("b3", [128, 2, CH])
        o = sb("o3", [P, 2, NQ, D])
        L0, L1, W = sb("L0", [128, 3, 256]), sb("L1", [128, 2, 128]), sb("W3", [128, 2, D])
        bl0, bl1 = sb("bl0", [128, 2]), sb("bl1", [128, 1])
        bb = sb("bb", [P, 2, D])
        ident = sb("ident3", [128, 128])
        names = ("made", "loaded", "h_in", "m0", "a0", "m1", "a1", "tr", "x_r", "var_r", "root_r", "chain", "xh_r", "t2", "t2c",
                 "agg", "a_r", "b_r", "o_g", "o_r", "out0", "out1", "bias_r", "w_used", "o1", "o2")
        (made, loaded, h_in, m0, a0, m1, a1, tr, x_r, var_r, root_r, chain, xh_r, t2, t2c,
         agg, a_r, b_r, o_g, o_r, out0, out1, bias_r, w_used, o1, o2) = (sem("t_" + n) for n in names)
        w_in = [sem(f"t_w{i}") for i in range(RING)]
        outs = (out0, out1)
        SC = NC + 1
        wid = lambda ch: min(CH, N - ch * CH)
        ot = out.rearrange("(k p) d -> p k d", p=P)

        with nc.Block() as block:
            @block.gpsimd
            def _(pool):
                nc.gpsimd.memset(ident[:], 0.0).then_inc(made, 1)
                pool.wait_ge(made, 1)
                nc.gpsimd.affine_select(out=ident[:], in_=ident[:], compare_op=ALU.not_equal, fill=1.0,
                                        base=0, pattern=[[-1, 128]], channel_multiplier=1).then_inc(made, 1)

            @block.sync
            def _(sp):
                for to, frm in ((L0, l0D), (L1, l1D), (W, w12D)):
                    sp.dma_start(to[:].rearrange("p a b -> p (a b)"), frm).then_inc(loaded, 16)
                sp.dma_start(bl0[:], l0b.rearrange("(c p) -> p c", p=128), allow_slow_non_contiguous=True).then_inc(loaded, 16)
                sp.dma_start(bl1[:], l1b.rearrange("(c p) -> p c", p=128), allow_slow_non_contiguous=True).then_inc(loaded, 16)
                for n, v in enumerate((b1, b2)):
                    sp.dma_start(bb[:, n, :], v.rearrange("(o d) -> o d", o=1).to_broadcast([P, D])).then_inc(loaded, 16)
                sp.dma_start(x3[:], x2D).then_inc(loaded, 16)
                for ch in range(SC):
                    w = wid(ch)
                    if ch:
                        sp.wait_ge(m0, ch)
                    sp.dma_start(hT[:, :, 0:w], hTD[:, :, ch * CH:ch * CH + w]).then_inc(h_in, 16)
                    sp.dma_start(xT[:, 0:w], xhTD[:, ch * CH:ch * CH + w]).then_inc(h_in, 16)
                for ch in range(SC):
                    sp.wait_ge(o_r, ch + 1)
                    k = wid(ch) // P
                    sp.dma_start(ot[:, ch * NQ:ch * NQ + k, :], o[:, ch % 2, 0:k, :]).then_inc(outs[ch % 2], 16)
                sp.wait_ge(out0, 16 * (SC - SC // 2))
                sp.wait_ge(out1, 16 * (SC // 2))

            @block.scalar
            def _(act):
                rows = WT.rearrange("n o -> (n o)")

                def load(g, i):
                    act.dma_start(wt[:, i, :], rows[bass.ds((g * RING + i) * P * N, 128 * N)].rearrange("(p n) -> p n", n=N)).then_inc(w_in[i], 16)
                for i in range(RING):
                    load(0, i)
                act.wait_ge(loaded, 16 * 8)
                for ch in range(SC):
                    w = wid(ch)
                    act.wait_ge(m0, ch + 1)
                    if ch:
                        act.wait_ge(m1, ch)
                    for h in range(2):
                        last = nc.scalar.activation(y0[:, h, 0:w], PS[h][:, 0:w], ACT.Relu, bias=bl0[:, h:h + 1])
                    last.then_inc(a0, 1)
                    act.wait_ge(m1, ch + 1)
                    if ch:
                        act.wait_ge(tr, ch)
                    nc.scalar.activation(y1[:, 0:w], PS[2][:, 0:w], ACT.Relu, bias=bl1[:, 0:1]).then_inc(a1, 1)
                act.wait_ge(var_r, 1)
                nc.scalar.activation(st[:, 3, :], st[:, 2, :], ACT.Sqrt).then_inc(root_r, 1)
                for ch in range(SC):
                    w = wid(ch)
                    act.wait_ge(t2, ch + 1)
                    nc.scalar.copy(x3T[:, ch * CH:ch * CH + w], PS[6 + ch % 2][:, 0:w]).then_inc(t2c, 1)
                with act.Fori(1, T // RING) as g:
                    for i in range(RING):
                        act.wait_ge(w_used, g * RING + i - (RING - 1))
                        load(g, i)

            @block.tensor
            def _(pe):
                pe.wait_ge(made, 2)
                pe.wait_ge(loaded, 16 * 8)
                for ch in range(SC):
                    w = wid(ch)
                    pe.wait_ge(h_in, 32 * ch + 32)
                    if ch:
                        pe.wait_ge(a0, ch)
                    for h in range(2):
                        for kt, v in enumerate((hT[:, 0, 0:w], hT[:, 1, 0:w], xT[:, 0:w])):
                            last = nc.tensor.matmul(PS[h][:, 0:w], L0[:, kt, h * 128:(h + 1) * 128], v, start=(kt == 0), stop=(kt == 2))
                    last.then_inc(m0, 1)
                    pe.wait_ge(a0, ch + 1)
                    if ch:
                        pe.wait_ge(a1, ch)
                    for kt in range(2):
                        last = nc.tensor.matmul(PS[2][:, 0:w], L1[:, kt, :], y0[:, kt, 0:w], start=(kt == 0), stop=(kt == 1))
                    last.then_inc(m1, 1)
                    pe.wait_ge(a1, ch + 1)
                    if ch:
                        pe.wait_ge(x_r, ch)
                    for q in range(w // P):
                        last = nc.tensor.transpose(PS[3][0:P, q * 128:(q + 1) * 128], y1[:, q * P:(q + 1) * P], ident[:])
                    last.then_inc(tr, 1)
                pe.wait_ge(xh_r, 1)
                for ch in range(SC):
                    w = wid(ch)
                    if ch >= 2:
                        pe.wait_ge(t2c, ch - 1)
                    for q in range(w // P):
                        last = nc.tensor.transpose(PS[6 + ch % 2][:, q * P:(q + 1) * P], xc[:, ch * NQ + q, :], ident[0:P, 0:P])
                    last.then_inc(t2, 1)
                pe.wait_ge(t2c, SC)

                def tile(g, i, start=False, stop=False):
                    pe.wait_ge(w_in[i], 16 * g + 16)
                    for ch in range(SC):
                        w = wid(ch)
                        last = nc.tensor.matmul(PS[ch][:, 0:w], xcs(g, i), wt[0:P, i, ch * CH:ch * CH + w], start=start, stop=stop)
                    last.then_inc(w_used, 1)
                xcs = lambda g, i: xc[:, g * RING + i, :]
                for g in range(T // RING):
                    for i in range(RING):
                        tile(g, i, start=(g == 0 and i == 0), stop=(g == T // RING - 1 and i == RING - 1))
                for ch in range(SC):
                    k = wid(ch) // P
                    pe.wait_ge(a_r, ch + 1)
                    pe.wait_ge(b_r, ch + 1)
                    for q in range(k):
                        for n, v in enumerate((a, b)):
                            last = nc.tensor.matmul(PS[ch][0:P, q * D:(q + 1) * D], v[:, ch % 2, q * P:(q + 1) * P], W[:, n, :], start=(n == 0), stop=(n == 1))
                    last.then_inc(o_g, 1)

            @block.vector
            def _(dve):
                V_ = nc.vector
                dn = Done(dve, chain)
                dve.wait_ge(loaded, 16 * 8)
                dn(V_.tensor_tensor(bb[:, 0, :], bb[:, 0, :], bb[:, 1, :], ALU.add))
                for ch in range(SC):
                    k = wid(ch) // P
                    dve.wait_ge(tr, ch + 1)
                    v = x3[:, ch * NQ:ch * NQ + k, :]
                    V_.tensor_tensor(v, v, PS[3][0:P, 0:k * D].rearrange("p (k d) -> p k d", d=D), ALU.add).then_inc(x_r, 1)
                dve.wait_ge(x_r, SC)

                def mid(ins):
                    ins.then_inc(var_r, 1)
                    dve.wait_ge(root_r, 1)
                norm(V_, dn, mid, x3[:], xc[:], sq[:], st, xc[:])
                dve.sem_inc(xh_r, 1)
                dve.wait_ge(w_used, T)
                dve.wait_ge(t2c, SC)

                def finish(ch):
                    k = wid(ch) // P
                    dve.wait_ge(o_g, ch + 1)
                    if ch >= 2:
                        dve.wait_ge(outs[ch % 2], 16 * (ch // 2))
                    v = o[:, ch % 2, 0:k, :]
                    V_.tensor_tensor(v, PS[ch][0:P, 0:k * D].rearrange("p (k d) -> p k d", d=D), bb[:, 0:1, :].to_broadcast([P, k, D]), ALU.add).then_inc(o1, 1)
                    dve.wait_ge(o1, ch + 1)
                    V_.scalar_tensor_tensor(v, v, ALPHA, v, ALU.mult, ALU.max).then_inc(o2, 1)
                    dve.wait_ge(o2, ch + 1)
                    V_.tensor_tensor(v, v, x3[:, ch * NQ:ch * NQ + k, :], ALU.add).then_inc(o_r, 1)
                for ch in range(SC):
                    w = wid(ch)
                    if ch >= 2:
                        dve.wait_ge(o_g, ch - 1)
                    t = x3T[:, ch * CH:ch * CH + w]
                    V_.tensor_tensor(a[:, ch % 2, 0:w], PS[ch][:, 0:w], t, ALU.add).then_inc(a_r, 1)
                    V_.tensor_tensor(b[:, ch % 2, 0:w], PS[ch][:, 0:w], t, ALU.mult).then_inc(b_r, 1)
                    if ch:
                        finish(ch - 1)
                finish(SC - 1)


_INS = ['x', 'src', 'dst', 'edge_weight', 'L0_gnn_W', 'L0_gnn_a', 'L1_gnn_W', 'L1_gnn_b', 'L2_gnn_W',
        'L2_gnn_w_ih', 'L2_gnn_w_hh', 'L2_gnn_b_ih', 'L2_gnn_b_hh', 'L2_gnn_l0_w', 'L2_gnn_l0_b',
        'L2_gnn_l1_w', 'L2_gnn_l1_b', 'L3_gnn_W1', 'L3_gnn_b1', 'L3_gnn_W2', 'L3_gnn_b2']


def kernel(**inputs):
    import numpy as _np
    import concourse.bacc as _bacc
    from concourse import mybir as _mybir
    from concourse.bass_utils import run_bass_kernel_spmd as _run

    nc = _bacc.Bacc("TRN2", target_bir_lowering=False, num_devices=1)
    arrays, args = {}, []
    for name in _INS:
        a = _np.ascontiguousarray(inputs[name])
        arrays[f"in_{name}_dram"] = a
        args.append(nc.dram_tensor(f"in_{name}_dram", a.shape, _mybir.dt.from_np(a.dtype), kind="ExternalInput").ap())
    args.append(nc.dram_tensor("out_0_dram", (N, D), f32, kind="ExternalOutput").ap())
    gnn_kernel(nc, *args)
    r = _run(nc, [arrays], core_ids=[0])
    return r.results[0]["out_0_dram"]
```

```python
import concourse.bass as bass
from concourse import mybir
from concourse.alu_op_type import AluOpType as ALU
from contextlib import ExitStack

N, D, E = 3125, 128, 50000
P = 125
T = N // P
CH = 500
NQ = CH // P
NC = N // CH
SC = NC + 1
LANE = 128
ET = -(-E // LANE)
EG = 4
WIN = 512 // T
NW = -(-N // WIN)
WC = WIN * T
SB = -(-NW * 4 // LANE)
ROUND = 1.5 * 2.0 ** 23
S2 = 256
GL, CL = 5, 3
GATES = 3 * S2
UP = 256.0
EPS = 1e-5
ALPHA = 0.2
BIG = 60000.0
SPAN = 4
STEP = 4
PAD_SRC, PAD_DST = N + 1, -2
BATCH = 5
NBATCH = 2 * -(-ET // (2 * BATCH))
MERGE = (NW - 1) // STEP
assert (NW - 1) % STEP == 0 and NBATCH == 2 * MERGE + 2 and NBATCH * BATCH <= EG * LANE
ZF = MERGE
ZN = 490
ZW = 4 * ZN
TABLE = ZF * LANE * ZW
DUMP = N * N + 8192
FAR = 1000.0
RAISE = 100000.0
SPLIT = 16
assert TABLE >= DUMP + LANE and TABLE >= (N + 3) * N and PAD_SRC * N < DUMP

f32, f16, bf16, i32 = mybir.dt.float32, mybir.dt.float16, mybir.dt.bfloat16, mybir.dt.int32
ACT = mybir.ActivationFunctionType
X = mybir.AxisListType.X


def gnn_kernel(nc, x, src, dst, ew, aW, aA, cW, cB, gW, wih, whh, bih, bhh, l0w, l0b, l1w, l1b,
               w1, b1, w2, b2, out):
    ctx = ExitStack()

    def dram(name, shape, dt=f32):
        return nc.dram_tensor(name, shape, dt).ap()

    WT = dram("WT", (TABLE, 1))
    keyD = dram("keyD", (EG * LANE, LANE))
    csD = dram("csD", (EG * LANE, 2 * LANE))
    scatD = dram("scatD", (NBATCH, LANE, 2 * BATCH), i32)
    VD = dram("VD", (GL, LANE, 2 * GATES))
    whhD = dram("whhD", (LANE, 2 * GATES))
    l0D = dram("l0D", (LANE, 3 * 256))
    l1D = dram("l1D", (LANE, 2 * LANE))
    w12D = dram("w12D", (LANE, 2 * LANE))
    rowD = dram("rowD", (2, N))
    xhD = dram("xhD", (P, T, 2, D), f16)
    xh1D = dram("xh1D", (P, T, D))
    hnD = dram("hnD", (P, T, 2, S2), f16)
    hTD = dram("hTD", (128, 2, N))
    xhTD = dram("xhTD", (128, N))
    x1D = dram("x1D", (P, T, D))
    x2D = dram("x2D", (P, T, D))
    colD = dram("colD", (P, 4 * T))

    with ctx:
        def sem(name):
            return ctx.enter_context(nc.semaphore(name))

        banks = ctx.enter_context(nc.psum_tensor("banks", [128, 8, 512], f32))
        PS = [banks[:, i, :] for i in range(8)]
        big = ctx.enter_context(nc.sbuf_tensor("big", [128, T * N // 2 + 1], f32))
        A = big[:].bitcast(f16)[0:P, 0:T * N].rearrange("p (t n) -> p t n", n=N)
        with ExitStack() as c:
            def sb(name, shape, dt=f32):
                return c.enter_context(nc.sbuf_tensor(name, shape, dt))

            ecol = sb("ecol", [128, 4, EG * LANE])
            edges = dict(
                ecol=ecol,
                comb=ecol[:, 0],
                sib=ecol[:, 1],
                keyc=ecol[:, 2],
                wc=ecol[:, 3],
                wp=sb("wp", [128, EG * LANE, 4], bf16),
                rank=sb("rank", [128, 1], i32),
                wcol=sb("wcol", [128, 2, SB * LANE]),
                visits=sb("visits", [1, 4, 160], i32),
                tcol=sb("tcol", [P, T]),
                scol=sb("scol", [P, T]),
                ident=sb("ident", [128, 128]))
            prepare(nc, sem, PS, big, edges, x, src, dst, ew, aW, aA, gW, wih, whh, l0w, l1w, w1, w2,
                    keyD, csD, VD, whhD, l0D, l1D, w12D, xhD)
            counts(nc, sem, PS, banks, A, edges, keyD, scatD, WT, colD, rowD)
        layers(nc, sem, PS, big, A, x, aW, cW, cB, bih, bhh, l0b, l1b, b1, b2, out, WT, scatD, VD, whhD, l0D, l1D, w12D,
               rowD, xhD, xh1D, x1D, x2D, colD, hnD, hTD, xhTD)


def pieces(big):
    used = [0]

    def sb(name, shape, dt=f32):
        size, at = 1, used[0]
        for n in shape[1:]:
            size *= n
        used[0] += -(-size // (2 if dt == f16 else 1))
        assert used[0] <= T * N // 2, name
        v = big[0:shape[0], at:used[0]]
        if dt != f32:
            v = v.bitcast(dt)
        dims = " ".join(f"d{i}" for i in range(1, len(shape)))
        kw = {f"d{i}": shape[i] for i in range(2, len(shape))}
        return v[:, 0:size].rearrange(f"p ({dims}) -> p {dims}", **kw) if len(shape) > 2 else v[:, 0:size]
    return sb


def newton(V_, done, y, v, tmp):
    done(V_.tensor_tensor(tmp, y, y, ALU.mult))
    done(V_.tensor_tensor(tmp, tmp, v, ALU.mult))
    done(V_.tensor_scalar(tmp, tmp, -0.5, 1.5, ALU.mult, ALU.add))
    done(V_.tensor_tensor(y, y, tmp, ALU.mult))


def prepare(nc, sem, PS, big, edges, x, src, dst, ew, aW, aA, gW, wih, whh, l0w, l1w, w1, w2,
            keyD, csD, VD, whhD, l0D, l1D, w12D, xhD):
    with ExitStack() as c:
        sb = pieces(big)
        ecol, wcol, wp, rank, visits, tcol, scol, ident = (
            edges[n] for n in ("ecol", "wcol", "wp", "rank", "visits", "tcol", "scol", "ident"))
        ei = sb("ei", [128, 2, EG, LANE], i32)
        ef = sb("ef", [128, 2, EG, LANE])
        we = sb("we", [128, EG, LANE])
        key = sb("key", [128, EG, LANE])
        near = sb("near", [128, EG, LANE])
        dmin = sb("dmin", [128, EG])
        dmax = sb("dmax", [128, EG])
        tile_no = sb("tile_no", [128, EG])
        base = sb("base", [128, NW])
        over = sb("over", [128, EG, 3, NW])
        cand = sb("cand", [128, 2, NW])
        red = sb("red", [128, 2, NW])
        vis = sb("vis", [1, 6, NW])
        nil = sb("nil", [1, NW])
        wno = sb("wno", [1, NW])
        top = sb("top", [1, 1])
        part = sb("part", [128, EG, LANE])
        cs = sb("cs", [128, EG, 2, LANE])
        near4 = sb("near4", [128, 32])
        hit = sb("hit", [128, 32])
        place = sb("place", [128, 1])
        woff = sb("woff", [128, SB])
        start = sb("start", [128, SB * 32])
        picked = sb("picked", [128, SB, 32])
        tile = sb("tile", [128, SB])
        tilei = sb("tilei", [128, SB], i32)
        gath = sb("gath", [128, SB, 2, LANE])
        xn = sb("xn", [P, T, D])
        sq = sb("sq", [P, T, D])
        pair = sb("pair", [P, T, 2, D], f16)
        st = sb("st", [P, 4, T])
        eps = sb("eps", [128, 1])
        uT = sb("uT", [P, 2, D])
        acol = sb("acol", [128, 2])
        abc = sb("abc", [128, 2, P])
        wihN, whhN = sb("wihN", [128, 6, S2]), sb("whhN", [128, 6, S2])
        l0N, l1N = sb("l0N", [128, 2, 384]), sb("l1N", [128, 1, S2])
        w12N, aWN = sb("w12N", [128, 2, D]), sb("aWN", [128, 1, D])
        gWN = sb("gWN", [128, 2 * GL, S2])
        wihT, whhT = sb("wihT", [128, 2, GATES]), sb("whhT", [128, 2, GATES])
        l0T, l1T = sb("l0T", [128, 3, 256]), sb("l1T", [128, 2, 128])
        w12T, aWT = sb("w12T", [128, 1, 256]), sb("aWT", [128, 1, 128])
        gWT = sb("gWT", [128, 2, GL * S2])
        V = sb("V", [128, 2, 2 * GATES])

        loaded, eloaded, padded, made, chain = (sem(s) for s in ("loaded", "eloaded", "padded", "made", "chain"))
        edge_t, edge_c, w_t, w_c, v_t, v_c, v_st = (
            sem(s) for s in ("edge_t", "edge_c", "w_t", "w_c", "v_t", "v_c", "v_st"))
        x_in, u_t, root_r, red_r, outs, cs_out, gathered, gath_t, gath_c = (
            sem(s) for s in ("x_in", "u_t", "root_r", "red_r", "outs", "cs_out", "gathered", "gath_t", "gath_c"))
        dve_did = sem("dve_did")
        ABC, EDGES, CS, CAND, ROWS, LESS, VAR, PAIR = range(1, 9)

        def runs(nat, rows, cols, tr, per=4):
            r = []
            for b in range(cols):
                for a in range(0, rows, per):
                    r.append((nat, tr, b, a, min(per, rows - a)))
            return r
        jobs = (runs(aWN, 1, 1, aWT) + runs(wihN, 6, 2, wihT, 3) + runs(gWN, 2 * GL, 2, gWT)
                + runs(whhN, 6, 2, whhT, 3) + runs(l0N, 2, 3, l0T) + runs(l1N, 1, 2, l1T) + runs(w12N, 2, 1, w12T))
        full = (E // (LANE * LANE))
        rest = E - full * LANE * LANE
        rt, rl = rest // LANE, rest % LANE
        edge_dmas = 3 * 3 if rl else 3 * 2
        HALF = 2 * GATES // 4

        with nc.Block() as block:
            @block.gpsimd
            def _(pool):
                nc.gpsimd.memset(ei[:, 0], PAD_SRC).then_inc(padded, 1)
                nc.gpsimd.memset(ei[:, 1], PAD_DST).then_inc(padded, 1)
                nc.gpsimd.memset(we[:], 0.0).then_inc(padded, 1)
                nc.gpsimd.memset(eps[:], EPS).then_inc(made, 1)
                nc.gpsimd.iota(base[:], [[WIN, NW]], base=0, channel_multiplier=0,
                               allow_small_or_imprecise_dtypes=True).then_inc(made, 1)
                nc.gpsimd.iota(tile_no[:], [[LANE, EG]], base=0, channel_multiplier=1,
                               allow_small_or_imprecise_dtypes=True).then_inc(made, 1)
                nc.gpsimd.iota(near4[:], [[-4, 32]], base=0, channel_multiplier=1,
                               allow_small_or_imprecise_dtypes=True).then_inc(made, 1)
                nc.gpsimd.iota(woff[:], [[32 * WC, SB]], base=0, channel_multiplier=WC // 4,
                               allow_small_or_imprecise_dtypes=True).then_inc(made, 1)
                nc.gpsimd.iota(rank[:], [[0, 1]], base=(127 + 100) << 23, channel_multiplier=-(1 << 23)).then_inc(made, 1)
                nc.gpsimd.iota(wno[:], [[1, NW]], base=1, channel_multiplier=0,
                               allow_small_or_imprecise_dtypes=True).then_inc(made, 1)
                nc.gpsimd.memset(ident[:], 0.0).then_inc(made, 1)
                pool.wait_ge(made, 8)
                nc.gpsimd.affine_select(out=ident[:], in_=ident[:], compare_op=ALU.not_equal, fill=1.0,
                                        base=0, pattern=[[-1, 128]], channel_multiplier=1).then_inc(made, 1)
                pool.wait_ge(dve_did, CAND)
                nc.gpsimd.partition_all_reduce(red[:].rearrange("p a w -> p (a w)"), cand[:].rearrange("p a w -> p (a w)"), 128,
                                               bass.bass_isa.ReduceOp.max).then_inc(red_r, 1)
                pool.wait_ge(dve_did, ROWS)
                pool.wait_ge(cs_out, 16)
                for b in range(SB):
                    nc.gpsimd.indirect_dma_start(out=gath[:, b].rearrange("p a e -> p (a e)"), out_offset=None, in_=csD,
                                                 in_offset=bass.IndirectOffsetOnAxis(ap=tilei[:, b:b + 1], axis=0)).then_inc(gathered, 16)
                pool.wait_ge(gathered, 16 * SB)

            @block.sync
            def _(sp):
                sp.wait_ge(padded, 3)
                for n, (arr, to) in enumerate(((src, ei[:, 0]), (dst, ei[:, 1]), (ew, we))):
                    m = full * LANE * LANE
                    sp.dma_start(to[:, 0:full, :], arr[0:m].rearrange("(g t e) -> t g e", t=LANE, e=LANE)).then_inc(eloaded, 16)
                    sp.dma_start(to[0:rt, full, :], arr[m:m + rt * LANE].rearrange("(t e) -> t e", e=LANE)).then_inc(eloaded, 16)
                    if rl:
                        m += rt * LANE
                        sp.dma_start(to[rt:rt + 1, full, 0:rl], arr[m:E].rearrange("(t e) -> t e", t=1)).then_inc(eloaded, 16)
                sp.wait_ge(dve_did, EDGES)
                sp.dma_start(keyD.rearrange("(g t) e -> t g e", g=EG), key[:]).then_inc(outs, 16)
                sp.wait_ge(dve_did, CS)
                sp.dma_start(csD.rearrange("(g t) e -> t g e", g=EG), cs[:].rearrange("t g a e -> t g (a e)")).then_inc(cs_out, 16)
                sp.wait_ge(dve_did, PAIR)
                sp.dma_start(xhD, pair[:]).then_inc(outs, 16)
                sp.wait_ge(w_c, len(jobs))
                for d_, s_ in ((whhD, whhT), (l0D, l0T), (l1D, l1T), (w12D, w12T)):
                    sp.dma_start(d_, s_[:].rearrange("p a b -> p (a b)")).then_inc(outs, 16)
                sp.wait_ge(outs, 16 * 6)

            @block.tensor
            def _(pe):
                pe.wait_ge(made, 9)
                n = [0]

                def bank():
                    i = n[0]
                    if i >= 6:
                        pe.wait_ge(w_c, i - 5)
                    n[0] += 1
                    return PS[i % 6]
                pe.wait_ge(loaded, 16 * 9)
                for nat, tr, b, a, m in jobs:
                    ps = bank()
                    for q in range(m):
                        last = nc.tensor.transpose(ps[:, q * 128:(q + 1) * 128], nat[:, a + q, b * 128:(b + 1) * 128], ident[:])
                    last.then_inc(w_t, 1)
                pe.wait_ge(dve_did, ABC)
                pe.wait_ge(w_c, len(jobs))
                for h in range(2):
                    last = nc.tensor.matmul(PS[0][0:P, h * 128:(h + 1) * 128], abc[:, h, :], aWT[:, 0, :], start=True, stop=True)
                last.then_inc(u_t, 1)
                pe.wait_ge(dve_did, EDGES)
                pe.wait_ge(dve_did, CS)
                for g in range(EG):
                    if g:
                        pe.wait_ge(edge_c, g)
                    for q, a in enumerate((cs[:, g, 0], cs[:, g, 1], key[:, g], we[:, g])):
                        last = nc.tensor.transpose(PS[6][:, q * 128:(q + 1) * 128], a, ident[:])
                    last.then_inc(edge_t, 1)
                pe.wait_ge(u_t, 1)
                for l in range(GL):
                    for kt in range(2):
                        for h in range(2):
                            i = (l * 2 + kt) * 2 + h
                            if i >= 4:
                                pe.wait_ge(v_c, i - 3)
                            for mt in range(2):
                                last = nc.tensor.matmul(PS[1 + i % 4][:, 0:HALF],
                                                        gWT[:, mt, l * S2 + kt * 128:l * S2 + (kt + 1) * 128],
                                                        wihT[:, mt, h * HALF:(h + 1) * HALF], start=(mt == 0), stop=(mt == 1))
                            last.then_inc(v_t, 1)
                pe.wait_ge(dve_did, LESS)
                for b in range(SB):
                    if b >= 2:
                        pe.wait_ge(gath_c, b - 1)
                    else:
                        pe.wait_ge(edge_c, EG)
                    for q in range(2):
                        last = nc.tensor.transpose(PS[6 + b % 2][:, q * 128:(q + 1) * 128], gath[:, b, q], ident[:])
                    last.then_inc(gath_t, 1)

            @block.scalar
            def _(act):
                act.dma_start(aWN[:, 0, :], aW).then_inc(loaded, 16)
                act.dma_start(wihN[:], wih.rearrange("(a p) m -> p a m", p=128)).then_inc(loaded, 16)
                act.dma_start(gWN[:], gW.rearrange("l (a p) m -> p (l a) m", p=128)).then_inc(loaded, 16)
                act.dma_start(whhN[:], whh.rearrange("(a p) m -> p a m", p=128)).then_inc(loaded, 16)
                act.dma_start(l0N[:], l0w.rearrange("(a p) m -> p a m", p=128)).then_inc(loaded, 16)
                act.dma_start(l1N[:, 0, :], l1w).then_inc(loaded, 16)
                act.dma_start(w12N[:, 0, :], w1).then_inc(loaded, 16)
                act.dma_start(w12N[:, 1, :], w2).then_inc(loaded, 16)
                act.dma_start(acol[:], aA.rearrange("(h p) o -> p (h o)", p=128), allow_slow_non_contiguous=True).then_inc(loaded, 16)
                act.dma_start(xn[:], x.rearrange("(k p) d -> p k d", p=P)).then_inc(x_in, 16)
                for i, (nat, tr, b, a, m) in enumerate(jobs):
                    act.wait_ge(w_t, i + 1)
                    nc.scalar.copy(tr[:, b, a * 128:(a + m) * 128], PS[i % 6][:, 0:m * 128]).then_inc(w_c, 1)
                act.wait_ge(dve_did, VAR)
                act.wait_ge(made, 1)
                nc.scalar.activation(st[:, 1, :], st[:, 0, :], ACT.Sqrt, bias=eps[0:P, :], scale=1.0 / D).then_inc(root_r, 1)
                for i in range(4 * GL):
                    l, j = i // 4, i % 4
                    act.wait_ge(v_t, i + 1)
                    if l >= 2 and j == 0:
                        act.wait_ge(v_st, 16 * (l - 1))
                    nc.scalar.copy(V[:, l % 2, (j // 2) * GATES + (j % 2) * HALF:(j // 2) * GATES + (j % 2 + 1) * HALF],
                                   PS[1 + i % 4][:, 0:HALF]).then_inc(v_c, 1)
                    if j == 3:
                        act.wait_ge(v_c, i + 1)
                        if l:
                            act.wait_ge(v_st, 16 * l)
                        act.dma_start(VD[l], V[:, l % 2, :]).then_inc(v_st, 16)
                act.wait_ge(v_st, 16 * GL)

            @block.vector
            def _(dve):
                n = [0]

                def done(ins):
                    n[0] += 1
                    ins.then_inc(chain, 1)
                    dve.wait_ge(chain, n[0])
                V_ = nc.vector
                dve.wait_ge(loaded, 16 * 9)
                last = V_.tensor_copy(abc[:], acol[:, :, None].to_broadcast([128, 2, P]))
                last.then_inc(dve_did, 1)
                dve.wait_ge(eloaded, 16 * edge_dmas)
                done(V_.tensor_copy(ef[:], ei[:]))
                V_.scalar_tensor_tensor(key[:], ef[:, 0], float(N), ef[:, 1], ALU.mult, ALU.add).then_inc(dve_did, 1)
                dve.wait_ge(dve_did, EDGES)
                done(V_.tensor_scalar(part[:], ef[:, 0], -float(P // 2), 1.0 / P, ALU.add, ALU.mult))
                done(V_.tensor_scalar(part[:], part[:], ROUND, None, ALU.add))
                done(V_.tensor_scalar(part[:], part[:], -ROUND, None, ALU.add))
                V_.scalar_tensor_tensor(cs[:, :, 0, :], ef[:, 1], float(T), part[:], ALU.mult, ALU.add)
                V_.scalar_tensor_tensor(cs[:, :, 1, :], part[:], -float(P), ef[:, 0], ALU.mult, ALU.add).then_inc(dve_did, 1)
                done(V_.tensor_scalar(near[:], ef[:, 1], 0.0, 1e5, ALU.is_lt, ALU.mult))
                done(V_.tensor_tensor(near[:], near[:], ef[:, 1], ALU.add))
                V_.tensor_reduce(dmin[:], near[:], X, ALU.min)
                done(V_.tensor_reduce(dmax[:], ef[:, 1], X, ALU.max))
                done(V_.tensor_scalar(dmin[:], dmin[:], -float(WIN - 1), None, ALU.add))
                dve.wait_ge(made, 9)
                for g in range(EG):
                    done(V_.tensor_scalar(over[:, g, 1, :], base[:], dmax[:, g:g + 1], None, ALU.is_le))
                    done(V_.scalar_tensor_tensor(over[:, g, 0, :], base[:], dmin[:, g:g + 1], over[:, g, 1, :], ALU.is_ge, ALU.mult))
                    done(V_.tensor_scalar(over[:, g, 1, :], over[:, g, 0, :], tile_no[:, g:g + 1], None, ALU.mult))
                    V_.tensor_tensor(over[:, g, 2, :], over[:, g, 1, :], over[:, g, 0, :], ALU.add)
                    done(V_.scalar_tensor_tensor(over[:, g, 1, :], over[:, g, 0, :], -FAR, over[:, g, 1, :], ALU.mult, ALU.add))
                for g in range(1, EG):
                    a = (cand[:, 0, :], cand[:, 1, :]) if g > 1 else (over[:, 0, 1, :], over[:, 0, 2, :])
                    V_.tensor_tensor(cand[:, 0, :], a[0], over[:, g, 1, :], ALU.min)
                    done(V_.tensor_tensor(cand[:, 1, :], a[1], over[:, g, 2, :], ALU.max))
                V_.tensor_scalar(cand[:, 0, :], cand[:, 0, :], -1.0, None, ALU.mult).then_inc(dve_did, 1)
                dve.wait_ge(red_r, 1)
                V_.memset(nil[:], 0.0)
                done(V_.memset(start[:], 0.0))
                done(V_.tensor_scalar(start[:, 0:NW], red[:, 0, :], -1.0, FAR, ALU.mult, ALU.add))
                done(V_.tensor_scalar(start[:, 0:NW], start[:, 0:NW], float(ET - 1), None, ALU.min))
                done(V_.tensor_scalar(hit[:], near4[:], 0.0, None, ALU.is_ge))
                done(V_.scalar_tensor_tensor(hit[:], near4[:], 3.0, hit[:], ALU.is_le, ALU.mult))
                done(V_.tensor_tensor(near4[:], near4[:], hit[:], ALU.mult))
                done(V_.tensor_reduce(place[:], near4[:], X, ALU.add))
                done(V_.tensor_tensor(picked[:], start[:].rearrange("p (b j) -> p b j", j=32),
                                      hit[:, None, :].to_broadcast([128, SB, 32]), ALU.mult))
                done(V_.tensor_reduce(tile[:], picked[:], X, ALU.add))
                done(V_.tensor_scalar(tile[:], tile[:], place[:], None, ALU.add))
                V_.tensor_copy(tilei[:], tile[:]).then_inc(dve_did, 1)
                done(V_.tensor_scalar(place[:], place[:], -float(WC // 4), None, ALU.mult))
                done(V_.tensor_scalar(woff[:], woff[:], place[:], None, ALU.add))
                done(V_.tensor_scalar(vis[:, 0, :], start[0:1, 0:NW], float(SPAN), None, ALU.add))
                done(V_.tensor_tensor(vis[:, 1, :], red[0:1, 1, :], vis[:, 0, :], ALU.subtract))
                done(V_.scalar_tensor_tensor(vis[:, 2, :], vis[:, 1, :], 0.0, wno[:], ALU.is_gt, ALU.mult))
                done(V_.tensor_reduce(top[:], vis[:, 2, 0:NW - 1], X, ALU.max))
                done(V_.tensor_scalar(top[:], top[:], 1.0, None, ALU.max))
                done(V_.tensor_scalar(vis[:, 2, :], wno[:], top[:], None, ALU.is_le))
                done(V_.memset(vis[:, 2, NW - 1:NW], 1.0))
                done(V_.scalar_tensor_tensor(vis[:, 2, :], vis[:, 1, :], 1.0, vis[:, 2, :], ALU.max, ALU.mult))
                done(V_.tensor_tensor_scan(vis[:, 3, :], vis[:, 2, :], nil[:], 0.0, ALU.add, ALU.add))
                done(V_.tensor_tensor(vis[:, 4, :], vis[:, 3, :], vis[:, 2, :], ALU.subtract))
                done(V_.scalar_tensor_tensor(vis[:, 5, :], vis[:, 0, :], RAISE, vis[:, 4, :], ALU.add, ALU.subtract))
                V_.tensor_copy(visits[:, 0, 0:NW], vis[:, 4, :])
                V_.tensor_copy(visits[:, 1, 0:NW], vis[:, 3, :])
                V_.tensor_copy(visits[:, 3, 0:1], top[:])
                done(V_.tensor_copy(visits[:, 2, 0:NW], vis[:, 5, :]))
                for g in range(EG):
                    dve.wait_ge(edge_t, g + 1)
                    V_.tensor_copy(ecol[:, :, g * LANE:(g + 1) * LANE], PS[6][:].rearrange("p (a t) -> p a t", a=4)).then_inc(edge_c, 1)
                dve.wait_ge(edge_c, EG)
                w = ecol[:, 3]
                V_.tensor_copy(wp[:, :, 3], rank[:].bitcast(f32).to_broadcast([128, EG * LANE]))
                left = [a[:].rearrange("p g e -> p (g e)") for a in (near, part)]
                for q in range(3):
                    done(V_.tensor_copy(wp[:, :, q], w))
                    if q < 2:
                        done(V_.tensor_tensor(left[q], w, wp[:, :, q], ALU.subtract))
                        w = left[q]
                dve.wait_ge(gathered, 16 * SB)
                V_.tensor_tensor(gath[:, :, 0, :], gath[:, :, 0, :], woff[:, :, None].to_broadcast([128, SB, LANE]), ALU.subtract).then_inc(dve_did, 1)
                dve.wait_ge(x_in, 16)
                bc = lambda a: a[:, :, None].to_broadcast([P, T, D])
                done(V_.tensor_reduce(st[:, 2, :], xn[:], X, ALU.add))
                done(V_.tensor_scalar(st[:, 3, :], st[:, 2, :], 1.0 / D, None, ALU.mult))
                done(V_.tensor_tensor(xn[:], xn[:], bc(st[:, 3, :]), ALU.subtract))
                done(V_.tensor_tensor(sq[:], xn[:], xn[:], ALU.mult))
                V_.tensor_reduce(st[:, 0, :], sq[:], X, ALU.add).then_inc(dve_did, 1)
                dve.wait_ge(root_r, 1)
                done(V_.reciprocal(st[:, 2, :], st[:, 1, :]))
                done(V_.tensor_scalar(st[:, 0, :], st[:, 0, :], 1.0 / D, EPS, ALU.mult, ALU.add))
                newton(V_, done, st[:, 2, :], st[:, 0, :], st[:, 1, :])
                done(V_.tensor_tensor(xn[:], xn[:], bc(st[:, 2, :]), ALU.mult))
                done(V_.tensor_scalar(sq[:], xn[:], 0.0, None, ALU.max))
                done(V_.tensor_scalar(xn[:], sq[:], UP, None, ALU.mult))
                done(V_.tensor_copy(pair[:, :, 0, :], xn[:]))
                V_.tensor_tensor(pair[:, :, 1, :], xn[:], pair[:, :, 0, :], ALU.subtract).then_inc(dve_did, 1)
                dve.wait_ge(dve_did, PAIR)
                dve.wait_ge(u_t, 1)
                done(V_.tensor_copy(uT[:].rearrange("p h d -> p (h d)"), PS[0][0:P, 0:256]))
                for h, to in enumerate((scol, tcol)):
                    done(V_.tensor_tensor(xn[:], sq[:], uT[:, h:h + 1, :].to_broadcast([P, T, D]), ALU.mult))
                    done(V_.tensor_reduce(to[:], xn[:], X, ALU.add))
                for b in range(SB):
                    dve.wait_ge(gath_t, b + 1)
                    V_.tensor_copy(wcol[:, :, b * LANE:(b + 1) * LANE],
                                   PS[6 + b % 2][:, 0:256].rearrange("p (a r) -> p a r", a=2)).then_inc(gath_c, 1)


def counts(nc, sem, PS, banks, A, edges, keyD, scatD, WT, colD, rowD):
    with ExitStack() as c:
        def sb(name, shape, dt=f32):
            return c.enter_context(nc.sbuf_tensor(name, shape, dt))

        comb, sib, keyc, wc, wp, rank, wcol, visits, tcol, scol, ident = (
            edges[n] for n in ("comb", "sib", "keyc", "wc", "wp", "rank", "wcol", "visits", "tcol", "scol", "ident"))
        pairs = sb("pairs", [128, WC], f16)
        nodes = sb("nodes", [128, P], f16)
        first = sb("first", [128, NW])
        OHP = SPAN * WC
        wide = sb("wide", [128, OHP + 2 * BATCH * LANE])
        ohp = wide[:, 0:OHP].bitcast(f16).rearrange("p (h s n) -> p h s n", h=2, s=SPAN)
        krow = wide[:, OHP:].rearrange("p (h q e) -> p h q e", h=2, q=BATCH)
        acc = wide[0:P, 0:N]
        ohs = sb("ohs", [128, 2, SPAN, P], f16)
        gap = sb("gap", [128, BATCH, LANE])
        eq = sb("eq", [128, 2, BATCH, LANE], bf16)
        kcol = sb("kcol", [128, 2, BATCH])
        onef = sb("onef", [128, 1])
        oneh = sb("oneh", [P, 1], f16)
        dump = sb("dump", [128, 1])
        identh = sb("identh0", [128, 128], f16)
        far = sb("far", [128, 1])
        nzb = sb("nz", [128, SC, CH], f16)
        nz = nzb[0:P]
        zero = nzb[:].rearrange("p b n -> p (b n)").bitcast(f32)[:, 0:ZN].rearrange("p (o z) -> p o z", o=1)
        col = sb("col", [P, 4, T])
        root = sb("root", [P, 3, T])
        top = sb("top", [P, 3, T])
        srows = sb("srows", [T, 2, P])
        thr = sb("thr", [128, 1])
        scat = wcol[:].rearrange("p a r -> p (a r)").bitcast(i32)[:, 0:NBATCH * 2 * BATCH].rearrange("p (b k q) -> p b k q", k=2, q=BATCH)
        names = ("set", "oh_made", "win_r", "win_out", "x_made", "x_prod", "x_added", "k0", "k1", "gap_r", "eq_r",
                 "eq_used", "tp_r", "nz_r", "acc_r", "acc_x", "root_r", "outs", "chain",
                 "kcol_r", "zeros", "tick", "dve_did", "pe_did")
        (set_, oh_made, win_r, win_out, x_made, x_prod, x_added, k0, k1, gap_r, eq_r,
         eq_used, tp_r, nz_r, acc_r, acc_x, root_r,
         outs, chain, kcol_r, zeros, tick, dve_did, pe_did) = (sem("w_" + n) for n in names)
        k_in = (k0, k1)
        SCAT, TOPS, DEGREES, COLS, ROWS = 2, 3, 4, 5, 6
        DEG_T, ROWS_T = 1, SC + 2
        W = [CH] * NC + [N - NC * CH]
        NSET = 9
        sums = banks[:, 4:8, :].rearrange("p b (t k) -> p (b t) k", k=4)
        assert NBATCH * BATCH <= 512
        LAST = N - (NW - 1) * WIN

        def windows(eng, window, merge=None, ahead=0):
            for b in range(ahead):
                merge(0, b)
            with eng.Fori(0, MERGE) as i:
                for j in range(STEP):
                    window(i * STEP + j, WIN, j)
                    if merge and j % 2:
                        b = j // 2 + ahead
                        merge(i + b // 2, b % 2)
            window(NW - 1, LAST, 0)
            if merge:
                for h in range(ahead, 2):
                    merge(MERGE, h)

        def rest(eng, window):
            end = eng.value_load(visits[0:1, 3, 0:1], min_val=1, max_val=NW - 1)
            with eng.Fori(0, end) as w:
                window(w, WIN)
            window(NW - 1, LAST)

        def span(eng, w):
            at = bass.ds(w, 1)
            return (eng.value_load(visits[0:1, 0, at], min_val=0, max_val=(ET + 3) * NW),
                    eng.value_load(visits[0:1, 1, at], min_val=1, max_val=(ET + 3) * NW))

        with nc.Block() as block:
            @block.gpsimd
            def _(pool):
                g = nc.gpsimd
                g.iota(pairs[:], [[1, WC]], base=0, channel_multiplier=0, allow_small_or_imprecise_dtypes=True).then_inc(set_, 1)
                g.iota(nodes[:], [[1, P]], base=0, channel_multiplier=0, allow_small_or_imprecise_dtypes=True).then_inc(set_, 1)
                g.iota(first[:], [[-WC, NW]], base=0, channel_multiplier=0, allow_small_or_imprecise_dtypes=True).then_inc(set_, 1)
                g.iota(dump[:], [[0, 1]], base=DUMP, channel_multiplier=1, allow_small_or_imprecise_dtypes=True).then_inc(set_, 1)
                g.memset(onef[:], 1.0).then_inc(set_, 1)
                g.memset(oneh[:], 1.0).then_inc(set_, 1)
                g.memset(zero, 0.0).then_inc(set_, 1)
                g.memset(far[:], BIG).then_inc(set_, 1)
                g.memset(identh[:], 0.0).then_inc(set_, 1)
                pool.wait_ge(set_, NSET)
                g.affine_select(out=identh[:], in_=identh[:], compare_op=ALU.not_equal, fill=1.0,
                                base=0, pattern=[[-1, 128]], channel_multiplier=1).then_inc(set_, 1)
                pool.wait_ge(set_, NSET + 1)

            @block.sync
            def _(sp):
                sp.wait_ge(set_, NSET)
                def keys(b, h):
                    sp.wait_ge(gap_r, b + 1)
                    rows = keyD[bass.ds(b * BATCH, BATCH), :].rearrange("(o t) e -> o (t e)", o=1)
                    sp.dma_start(krow[:, h].rearrange("p t e -> p (t e)"), rows.to_broadcast([128, BATCH * LANE])).then_inc(k_in[h], 16)
                with sp.Fori(0, MERGE) as i:
                    for h in range(2):
                        keys(2 * i + h, h)
                    sp.dma_start(WT[bass.ds(i * (LANE * ZW), LANE * ZW), :].rearrange("(p a w) o -> p a (w o)", p=LANE, w=ZN),
                                 zero.to_broadcast([128, ZW // ZN, ZN])).then_inc(zeros, 16)
                for h in range(2):
                    keys(2 * MERGE + h, h)
                sp.wait_ge(dve_did, SCAT)
                sp.dma_start(scatD.rearrange("b p c -> p b c"), scat.rearrange("p b k q -> p b (k q)")).then_inc(outs, 16)
                sp.wait_ge(dve_did, COLS)
                sp.dma_start(colD, col[:].rearrange("p a t -> p (a t)")).then_inc(outs, 16)
                sp.wait_ge(dve_did, ROWS)
                sp.dma_start(rowD.rearrange("h (k p) -> k h p", p=P), srows[:]).then_inc(outs, 16)
                sp.wait_ge(outs, 48)
                sp.wait_ge(zeros, 16 * ZF)

            @block.vector
            def _(dve):
                V_ = nc.vector
                dve.wait_ge(set_, NSET + 1)

                def window(w, n, j):
                    dve.wait_ge(win_r, w + 1)
                    V_.tensor_tensor(ohs[:, j % 2], nodes[:, None, :].to_broadcast([128, SPAN, P]),
                                     wcol[:, 1, bass.ds(w * SPAN, SPAN)][:, :, None].to_broadcast([128, SPAN, P]), ALU.is_equal)
                    for k in range(SPAN):
                        last = V_.tensor_scalar(ohp[:, j % 2, k], pairs[:], wcol[:, 0, bass.ds(w * SPAN + k, 1)], None, ALU.is_equal)
                    last.then_inc(oh_made, 1)
                windows(dve, window)

                dve.wait_ge(win_out, NW + 4)
                dve.wait_ge(win_r, NW + 2)

                def more(w, n):
                    v0, v1 = span(dve, w)
                    off = dve.value_load(visits[0:1, 2, bass.ds(w, 1)], min_val=0, max_val=ET + SPAN + int(RAISE))
                    with dve.Fori(v0, v1) as v:
                        t = nc.s_assert_within(v + off - int(RAISE), 0, EG * LANE - 1, skip_runtime_bounds_check_because=
                                               "the table of visits keeps to the edge tiles")
                        V_.tensor_scalar(ohs[:, 0, 0], nodes[:], sib[:, bass.ds(t, 1)], None, ALU.is_equal)
                        V_.tensor_scalar(ohp[:, 0, 0], pairs[:], first[:, bass.ds(w, 1)], comb[:, bass.ds(t, 1)],
                                         ALU.subtract, ALU.is_equal).then_inc(x_made, 1)
                        dve.wait_ge(x_prod, v + 1)
                        dve.sem_inc(tick, 1)
                        part = A[:, :, bass.ds(w * WIN, n)]
                        V_.tensor_tensor(part, part, PS[0][0:P, 0:n * T].rearrange("p (n a) -> p a n", a=T), ALU.add).then_inc(x_added, 1)
                        dve.wait_ge(x_added, v + 1)
                rest(dve, more)
                n = [0]

                def done(ins):
                    n[0] += 1
                    ins.then_inc(chain, 1)
                    dve.wait_ge(chain, n[0])
                nt = NBATCH * BATCH
                dve.wait_ge(eq_used, NBATCH + 2)
                bq = lambda a: a.rearrange("p (b q) -> p b q", q=BATCH)
                V_.tensor_reduce(scat[:, :, 1, :].bitcast(f32), sums[:, 0:nt, 0:3].rearrange("p (b q) k -> p b q k", q=BATCH),
                                 X, ALU.add).then_inc(dve_did, 1)
                done(V_.tensor_scalar(thr[:], rank[:].bitcast(f32), 2.5, None, ALU.mult))
                done(V_.tensor_scalar(wc[:, 0:nt], keyc[:, 0:nt], dump[:], -1.0, ALU.subtract, ALU.mult))
                done(V_.scalar_tensor_tensor(wc[:, 0:nt], sums[:, 0:nt, 3], thr[:], wc[:, 0:nt], ALU.is_gt, ALU.mult))
                V_.tensor_tensor(scat[:, :, 0, :], bq(wc[:, 0:nt]), bq(keyc[:, 0:nt]), ALU.add).then_inc(dve_did, 1)
                dve.wait_ge(dve_did, SCAT)
                V_.memset(acc, 1e30).then_inc(acc_r, SC)
                with dve.Fori(0, T) as j:
                    for b in range(SC):
                        part = acc[:, b * CH:b * CH + W[b]]
                        dve.wait_ge(nz_r, SC * j + b + 1 + SC)
                        dve.wait_ge(acc_r, SC * j + b + 1)
                        V_.scalar_tensor_tensor(part, nz[:, b, 0:W[b]], tcol[:, bass.ds(j, 1)], part, ALU.subtract, ALU.min).then_inc(acc_r, 1)
                for b in range(SC):
                    dve.wait_ge(pe_did, 1 + b + 1)
                    k = W[b] // P
                    V_.tensor_reduce(top[:, 0, b * NQ:b * NQ + k], PS[b][0:P, 0:W[b]].rearrange("p (k q) -> p k q", k=k), X, ALU.min).then_inc(acc_x, 1)
                dve.wait_ge(acc_x, SC)
                done(V_.tensor_tensor(top[:, 1, :], scol[:], top[:, 0, :], ALU.subtract))
                done(V_.scalar_tensor_tensor(top[:, 2, :], top[:, 1, :], ALPHA, top[:, 1, :], ALU.mult, ALU.max))
                V_.tensor_tensor(top[:, 0, :], scol[:], top[:, 2, :], ALU.subtract)
                done(V_.scalar_tensor_tensor(top[:, 1, :], scol[:], ALPHA, top[:, 2, :], ALU.mult, ALU.subtract))
                V_.tensor_copy(col[:, 0, :], tcol[:]).then_inc(dve_did, 1)
                V_.tensor_scalar(col[:, 1, :], tcol[:], ALPHA, None, ALU.mult)
                dve.wait_ge(pe_did, DEG_T)
                done(V_.tensor_scalar(root[:, 0, :], PS[7][0:P, 0:T], 1.0, None, ALU.add))
                V_.tensor_copy(root[:, 1, :], root[:, 0, :]).then_inc(dve_did, 1)
                dve.wait_ge(root_r, 1)
                done(V_.reciprocal(root[:, 2, :], root[:, 1, :]))
                newton(V_, done, root[:, 2, :], root[:, 0, :], root[:, 1, :])
                V_.tensor_scalar(col[:, 3, :], root[:, 2, :], UP, None, ALU.mult)
                V_.tensor_copy(col[:, 2, :], root[:, 2, :]).then_inc(dve_did, 1)
                dve.wait_ge(pe_did, ROWS_T)
                V_.tensor_copy(srows[:], PS[0][0:T, 0:256].rearrange("p (h c) -> p h c", h=2)[:, :, 0:P]).then_inc(dve_did, 1)

            @block.scalar
            def _(act):
                act.wait_ge(set_, NSET + 1)
                act.sem_inc(win_out, 4)
                act.sem_inc(nz_r, SC)
                act.sem_inc(gap_r, 2)

                def window(w, n, j):
                    act.wait_ge(win_r, w + 3)
                    nc.scalar.copy(A[:, :, bass.ds(w * WIN, n)], PS[j][0:P, 0:n * T].rearrange("p (n a) -> p a n", a=T)).then_inc(win_out, 1)

                def merge(i, h):
                    b = 2 * i + h
                    nc.scalar.copy(kcol[:, h, :], keyc[:, bass.ds(b * BATCH, BATCH)]).then_inc(kcol_r, 1)
                    act.wait_ge(k_in[h], 16 * i + 16)
                    act.wait_ge(kcol_r, b + 1)
                    act.sem_inc(tick, 1)
                    for q in range(BATCH):
                        last = nc.scalar.activation(gap[:, q], krow[:, h, q], ACT.Square, bias=kcol[:, h, q:q + 1], scale=-1.0)
                    last.then_inc(gap_r, 1)
                    act.wait_ge(gap_r, b + 3)
                    act.wait_ge(eq_used, b + 1)
                    nc.scalar.activation(eq[:, h], gap[:], ACT.Relu, bias=onef[:], scale=-2.0).then_inc(eq_r, 1)
                windows(act, window, merge, ahead=1)
                act.wait_ge(zeros, 16 * ZF)
                with act.Fori(0, T) as j:
                    for b in range(SC):
                        act.wait_ge(tp_r, SC * j + b + 1)
                        act.wait_ge(acc_r, SC * j + b + 1)
                        nc.scalar.activation(nz[:, b, 0:W[b]], PS[b][0:P, 0:W[b]], ACT.Relu, scale=-BIG, bias=far[0:P, :]).then_inc(nz_r, 1)
                act.wait_ge(dve_did, DEGREES)
                nc.scalar.activation(root[:, 1, :], root[:, 1, :], ACT.Sqrt).then_inc(root_r, 1)

            @block.tensor
            def _(pe):
                pe.sem_inc(win_r, 2)
                pe.sem_inc(eq_used, 2)
                pe.wait_ge(set_, NSET + 1)

                def window(w, n, j):
                    pe.wait_ge(win_out, w + 1)
                    pe.wait_ge(oh_made, w + 1)
                    for k in range(SPAN):
                        last = nc.tensor.matmul(PS[j][0:P, 0:WC], ohs[:, j % 2, k], ohp[:, j % 2, k], start=(k == 0), stop=(k == SPAN - 1))
                    last.then_inc(win_r, 1)

                def merge(i, h):
                    b = 2 * i + h
                    pe.wait_ge(eq_r, b + 1)
                    for q in range(BATCH):
                        t = bass.ds(b * BATCH + q, 1)
                        last = nc.tensor.matmul(sums[:, t, :].rearrange("p o k -> p (o k)"), eq[:, h, q], wp[:, t, :].rearrange("p o k -> p (o k)"),
                                                start=True, stop=True)
                    last.then_inc(eq_used, 1)
                windows(pe, window, merge)

                def more(w, n):
                    v0, v1 = span(pe, w)
                    with pe.Fori(v0, v1) as v:
                        pe.wait_ge(x_made, v + 1)
                        nc.tensor.matmul(PS[0][0:P, 0:WC], ohs[:, 0, 0], ohp[:, 0, 0], start=True, stop=True).then_inc(x_prod, 1)
                rest(pe, more)
                pe.wait_ge(dve_did, SCAT)
                with pe.Fori(0, T) as j:
                    for b in range(SC):
                        pe.wait_ge(nz_r, SC * j + b + 1)
                        for q in range(W[b] // P):
                            a = b * NQ + q
                            tile = A[:, a, bass.ds(j * P, P)]
                            nc.tensor.matmul(PS[7][0:P, bass.ds(j, 1)], tile, oneh[:], start=(a == 0), stop=(a == T - 1))
                            last = nc.tensor.matmul(PS[b][0:P, q * P:(q + 1) * P], tile, identh[0:P, 0:P], start=True, stop=True)
                        last.then_inc(tp_r, 1)
                pe.sem_inc(pe_did, 1)
                pe.wait_ge(acc_r, SC * T + SC)
                for b in range(SC):
                    for k in range(W[b] // P):
                        last = nc.tensor.transpose(PS[b][0:P, k * P:(k + 1) * P], acc[:, b * CH + k * P:b * CH + (k + 1) * P], ident[0:P, 0:P])
                    last.then_inc(pe_did, 1)
                pe.wait_ge(dve_did, TOPS)
                for h in range(2):
                    last = nc.tensor.transpose(PS[0][0:T, h * 128:h * 128 + P], top[:, h, :], ident[0:P, 0:P])
                last.then_inc(pe_did, 1)


class Done:

    def __init__(self, eng, sem):
        self.eng, self.sem, self.n = eng, sem, 0

    def __call__(self, ins, start=None):
        self.n += 1
        ins.then_inc(self.sem, 1)
        self.eng.wait_ge(self.sem, self.n if start is None else start + self.n)


def scatter(nc, pool, sems, scat, scatD, WT, first, end):
    got, added, landed = sems
    with pool.Fori(first, end) as b:
        pool.dma_start(scat[:], scatD[bass.ds(b, 1)].rearrange("o p c -> (o p) c")).then_inc(got, 16)
        pool.wait_ge(got, 16 * b + 16)
        pool.sem_inc(landed, 1)
        for q in range(BATCH):
            nc.gpsimd.indirect_dma_start(out=WT, out_offset=bass.IndirectOffsetOnAxis(ap=scat[:, q:q + 1], axis=0),
                                         in_=scat[:, BATCH + q:BATCH + q + 1].bitcast(f32), in_offset=None,
                                         compute_op=ALU.add).then_inc(added, 16)
            pool.wait_ge(added, 16 * (BATCH * b + q + 1))
            pool.sem_inc(landed, 1)


def layers(nc, sem, PS, big, A, x, aW, cW, cB, bih, bhh, l0b, l1b, b1, b2, out, WT, scatD, VD, whhD, l0D, l1D, w12D,
           rowD, xhD, xh1D, x1D, x2D, colD, hnD, hTD, xhTD):
    with ExitStack() as c:
        def sb(name, shape, dt=f32):
            return c.enter_context(nc.sbuf_tensor(name, shape, dt))

        ident = sb("identf", [128, 128])
        identh = sb("identh", [128, 128], f16)
        col = sb("cols", [P, 4, T])
        scat = sb("scatp", [128, 2 * BATCH], i32)
        scat_sems = [sem("scat_" + n) for n in ("got", "added", "landed")]
        attention(nc, sem, PS, x, aW, rowD, xhD, xh1D, x1D, colD, A, ident, identh, col)
        convolutions(nc, sem, PS, cW, cB, scat, scat_sems, scatD, WT, xh1D, x1D, x2D, hnD, hTD, xhTD, A, ident, identh, col)
        gru(nc, sem, PS, bih, bhh, scat, scat_sems, scatD, WT, VD, whhD, hnD, hTD, A, ident)
    tail(nc, sem, PS, big, l0b, l1b, b1, b2, out, WT, l0D, l1D, w12D, x2D, hTD, xhTD)


def norm(V_, done, mid, y, xc, sq, st, relu_to):
    q = y.shape[1]
    bc = lambda a: a[:, :, None].to_broadcast([P, q, D])
    done(V_.tensor_reduce(st[:, 0, :], y, X, ALU.add))
    done(V_.tensor_scalar(st[:, 1, :], st[:, 0, :], 1.0 / D, None, ALU.mult))
    done(V_.tensor_tensor(xc, y, bc(st[:, 1, :]), ALU.subtract))
    done(V_.tensor_tensor(sq, xc, xc, ALU.mult))
    done(V_.tensor_reduce(st[:, 0, :], sq, X, ALU.add))
    mid(V_.tensor_scalar(st[:, 2, :], st[:, 0, :], 1.0 / D, EPS, ALU.mult, ALU.add))
    done(V_.reciprocal(st[:, 0, :], st[:, 3, :]))
    newton(V_, done, st[:, 0, :], st[:, 2, :], st[:, 3, :])
    if relu_to is None:
        done(V_.tensor_tensor(xc, xc, bc(st[:, 0, :]), ALU.mult))
    else:
        done(V_.tensor_tensor(xc, xc, bc(st[:, 0, :]), ALU.mult))
        done(V_.tensor_scalar(relu_to, xc, 0.0, None, ALU.max))


def attention(nc, sem, PS, x, aW, rowD, xhD, xh1D, x1D, colD, A, ident, identh, col):
    with ExitStack() as c:
        def sb(name, shape, dt=f32):
            return c.enter_context(nc.sbuf_tensor(name, shape, dt))

        UN = 5
        xh = sb("xh", [P, T, 2, D], f16)
        sr = sb("sr", [P, 2, CH])
        z = sb("z", [P, UN, CH])
        ph = sb("ph", [P, 3, 2, CH], f16)
        inv = sb("inv", [128, CH])
        hT = sb("hT", [128, CH])
        xin = sb("xin", [P, NQ, D])
        ya = sb("ya", [P, NQ, D])
        yb = sb("yb", [P, NQ, D])
        st = sb("sta", [P, 4, NQ])
        W = sb("aWs", [128, D])
        ones = sb("ones", [P, 128], f16)
        names = ("made", "loaded", "sr_in", "sr_free", "a_r", "z_r", "e_r", "p_r", "ph_r", "pl_r", "cell_r", "tr_r",
                 "sum_r", "hT_r", "out_r", "exp_r", "var_r", "root_r", "x_in", "x_out", "y_r", "chain", "sum_free")
        (made, loaded, sr_in, sr_free, a_r, z_r, e_r, p_r, ph_r, pl_r, cell_r, tr_r,
         sum_r, hT_r, out_r, exp_r, var_r, root_r, x_in, x_out, y_r, chain, sum_free) = (sem("a0_" + n) for n in names)
        xt = x.rearrange("(k p) d -> p k d", p=P)

        def chunks(eng, body):
            with eng.Fori(0, NC) as ch:
                body(ch, CH)
            body(NC, P)

        def cells(eng, ch, stages, lag):
            def step(g, i, first, upto=None):
                for n, stage in enumerate(stages):
                    if not (first and i < n) and (upto is None or upto <= n):
                        k = i - n
                        stage(ch * T + g * UN + k, g * UN + k, k % UN, g if k >= 0 else g - 1)
            for i in range(UN):
                step(0, i, True)
            with eng.Fori(1, T // UN) as g:
                for i in range(UN):
                    step(g, i, False)
            for n in range(1, lag + 1):
                for m in range(n, lag + 1):
                    k = UN - 1 + n - m
                    stages[m](ch * T + T - UN + k, T - UN + k, k, T // UN - 1)

        with nc.Block() as block:
            @block.sync
            def _(sp):
                sp.dma_start(xh[:], xhD).then_inc(loaded, 16)
                sp.dma_start(col[:], colD.rearrange("p (a t) -> p a t", a=4)).then_inc(loaded, 16)
                sp.dma_start(W[:], aW).then_inc(loaded, 16)

                def body(ch, w):
                    k = w // P
                    sp.wait_ge(sr_free, 2 * ch + 2)
                    sp.dma_start(sr[:, :, 0:w], rowD[:, bass.ds(ch * CH, w)].rearrange("(o h) n -> o h n", o=1).to_broadcast([P, 2, w])).then_inc(sr_in, 16)
                    sp.wait_ge(x_in, 16 * ch + 16)
                    sp.wait_ge(x_out, 32 * ch + 32)
                    sp.dma_start(xin[:, 0:k, :], xt[:, bass.ds(ch * NQ, k), :]).then_inc(x_in, 16)
                    sp.wait_ge(y_r, 2 * ch + 1)
                    sp.dma_start(x1D[:, bass.ds(ch * NQ, k), :], ya[:, 0:k, :]).then_inc(x_out, 16)
                    sp.wait_ge(y_r, 2 * ch + 2)
                    sp.dma_start(xh1D[:, bass.ds(ch * NQ, k), :], yb[:, 0:k, :]).then_inc(x_out, 16)
                sp.sem_inc(x_in, 16)
                sp.sem_inc(x_out, 32)
                chunks(sp, body)
                sp.wait_ge(x_out, 32 * (NC + 1) + 32)

            @block.gpsimd
            def _(pool):
                nc.gpsimd.memset(ones[:], 1.0).then_inc(made, 1)
                nc.gpsimd.memset(ident[:], 0.0).then_inc(made, 1)
                nc.gpsimd.memset(identh[:], 0.0).then_inc(made, 1)
                pool.wait_ge(made, 3)
                for m in (ident, identh):
                    nc.gpsimd.affine_select(out=m[:], in_=m[:], compare_op=ALU.not_equal, fill=1.0,
                                            base=0, pattern=[[-1, 128]], channel_multiplier=1).then_inc(made, 1)
                pool.sem_inc(pl_r, UN)

                def body(ch, w):
                    def low(m, j, i, g):
                        pool.wait_ge(ph_r, m + 1)
                        nc.gpsimd.tensor_tensor(ph[:, i % 3, 1, 0:w], z[:, i, 0:w], ph[:, i % 3, 0, 0:w], ALU.subtract).then_inc(pl_r, 1)
                    cells(pool, ch, [low], 0)
                chunks(pool, body)

            @block.scalar
            def _(act):
                act.wait_ge(loaded, 48)

                def body(ch, w):
                    k = w // P
                    act.wait_ge(sr_in, 16 * ch + 16)

                    def lift(m, j, i, g):
                        act.wait_ge(pl_r, m + 1)
                        nc.scalar.activation(z[:, i, 0:w], sr[:, 1, 0:w], ACT.Identity, bias=col[:, 1, bass.ds(j, 1)]).then_inc(a_r, 1)

                    def expo(m, j, i, g):
                        act.wait_ge(z_r, m + 1)
                        nc.scalar.activation(z[:, i, 0:w], z[:, i, 0:w], ACT.Exp).then_inc(e_r, 1)

                    def high(m, j, i, g):
                        act.wait_ge(p_r, m + 1 + 2 * UN)
                        act.wait_ge(cell_r, m - 1 + 2 * UN)
                        nc.scalar.copy(ph[:, i % 3, 0, 0:w], z[:, i, 0:w]).then_inc(ph_r, 1)
                    cells(act, ch, [lift, expo, high], 2)
                    act.sem_inc(sr_free, 1)
                    act.wait_ge(out_r, ch + 1)
                    nc.scalar.activation(yb[:, 0:k, :].rearrange("p k d -> p (k d)"), PS[5][0:P, 0:k * D], ACT.Exp).then_inc(exp_r, 1)
                    act.wait_ge(var_r, ch + 1)
                    nc.scalar.activation(st[:, 3, 0:k], st[:, 2, 0:k], ACT.Sqrt).then_inc(root_r, 1)
                chunks(act, body)

            @block.tensor
            def _(pe):
                pe.wait_ge(made, 5)
                pe.wait_ge(loaded, 48)
                pe.sem_inc(cell_r, 2 * UN)

                def body(ch, w):
                    k = w // P
                    pe.wait_ge(sum_free, ch + 1)

                    def turn(m, j, i, g):
                        pe.wait_ge(p_r, m - 1 + 2 * UN)
                        for q in range(k):
                            last = nc.tensor.matmul(PS[2 + i % 3][0:P, q * P:(q + 1) * P],
                                                    A[:, bass.ds(ch * NQ + q, 1), bass.ds(j * P, P)].rearrange("p o n -> p (o n)"),
                                                    identh[0:P, 0:P], start=True, stop=True)
                        last.then_inc(tr_r, 1)

                    def wait_turn(m, j, i, g):
                        pass

                    def cell(m, j, i, g):
                        start, stop = (isinstance(j, int) and j == n for n in (0, T - 1))
                        hi, lo = ph[:, i % 3, 0, 0:w], ph[:, i % 3, 1, 0:w]
                        xhi = xh[:, bass.ds(j, 1), 0, :].rearrange("p o d -> p (o d)")
                        xlo = xh[:, bass.ds(j, 1), 1, :].rearrange("p o d -> p (o d)")
                        pe.wait_ge(ph_r, m + 1)
                        nc.tensor.matmul(PS[0][:, 0:w], xhi, hi, start=start, stop=False)
                        nc.tensor.matmul(PS[0][:, 0:w], xlo, hi, start=False, stop=False)
                        nc.tensor.matmul(PS[1][:, 0:w], ones[:], hi, start=start, stop=False)
                        pe.wait_ge(pl_r, m + 1 + UN)
                        nc.tensor.matmul(PS[0][:, 0:w], xhi, lo, start=False, stop=stop)
                        nc.tensor.matmul(PS[1][:, 0:w], ones[:], lo, start=False, stop=stop).then_inc(cell_r, 1)
                    cells(pe, ch, [turn, wait_turn, cell], 2)
                    pe.wait_ge(hT_r, ch + 1)
                    for q in range(k):
                        last = nc.tensor.matmul(PS[5][0:P, q * D:(q + 1) * D], hT[:, q * P:(q + 1) * P], W[:], start=True, stop=True)
                    last.then_inc(out_r, 1)
                chunks(pe, body)

            @block.vector
            def _(dve):
                V_ = nc.vector
                dve.wait_ge(loaded, 48)
                dve.sem_inc(sr_free, 2)
                dve.sem_inc(p_r, 2 * UN)
                dve.sem_inc(sum_free, 1)

                def body(ch, w):
                    k = w // P
                    dve.wait_ge(sr_in, 16 * ch + 16)

                    def logit(m, j, i, g):
                        dve.wait_ge(a_r, m + 1)
                        V_.scalar_tensor_tensor(z[:, i, 0:w], sr[:, 0, 0:w], col[:, 0, bass.ds(j, 1)], z[:, i, 0:w], ALU.add, ALU.max).then_inc(z_r, 1)

                    def weigh(m, j, i, g):
                        dve.wait_ge(e_r, m + 1)
                        dve.wait_ge(tr_r, m + 1)
                        V_.scalar_tensor_tensor(z[:, i, 0:w], z[:, i, 0:w], 1.0, PS[2 + i % 3][0:P, 0:w], ALU.min, ALU.mult).then_inc(p_r, 1)
                    cells(dve, ch, [logit, weigh], 1)
                    dve.sem_inc(sr_free, 1)
                    dve.wait_ge(cell_r, ch * T + T + 2 * UN)
                    K_ = 17
                    n0 = done.n

                    def dn(ins):
                        done.n += 1
                        ins.then_inc(chain, 1)
                        dve.wait_ge(chain, ch * K_ + done.n - n0)
                    dn(V_.tensor_scalar(inv[:, 0:w], PS[1][:, 0:w], 1e-8, None, ALU.max))
                    dn(V_.reciprocal(inv[:, 0:w], inv[:, 0:w]))
                    V_.scalar_tensor_tensor(hT[:, 0:w], PS[0][:, 0:w], 1.0 / UP, inv[:, 0:w], ALU.mult, ALU.mult).then_inc(hT_r, 1)
                    dve.wait_ge(hT_r, ch + 1)
                    dve.sem_inc(sum_free, 1)
                    o = PS[5][0:P, 0:k * D].rearrange("p (k d) -> p k d", d=D)
                    y, t = ya[:, 0:k, :], yb[:, 0:k, :]
                    dve.wait_ge(exp_r, ch + 1)
                    dn(V_.tensor_scalar(t, t, 1.0, -1.0, ALU.min, ALU.add))
                    dn(V_.scalar_tensor_tensor(t, o, 0.0, t, ALU.max, ALU.add))
                    dve.wait_ge(x_in, 16 * ch + 32)
                    dn(V_.tensor_tensor(y, t, xin[:, 0:k, :], ALU.add))
                    dve.sem_inc(y_r, 1)

                    def mid(ins):
                        ins.then_inc(var_r, 1)
                        dve.wait_ge(root_r, ch + 1)
                    norm(V_, dn, mid, y, t, xin[:, 0:k, :], st[:, :, 0:k], t)
                    dve.sem_inc(y_r, 1)
                    dve.wait_ge(x_out, 32 * ch + 64)
                    assert done.n - n0 == K_, done.n - n0
                done = Done(dve, chain)
                chunks(dve, body)


def convolutions(nc, sem, PS, cW, cB, scat, scat_sems, scatD, WT, xh1D, x1D, x2D, hnD, hTD, xhTD, A, ident, identh, col):
    with ExitStack() as c:
        def sb(name, shape, dt=f32):
            return c.enter_context(nc.sbuf_tensor(name, shape, dt))

        xr = sb("xr", [P, T, D])
        G = sb("G1", [P, 2, T, 2, D], f16)
        F = G[:].rearrange("p a t h d -> p (a t h d)").bitcast(f32).rearrange("p (a t d) -> p a t d", a=2, t=T)
        pair = G[:, 0]
        aT = sb("aT1", [128, CH])
        W = sb("cWs", [128, CL, D])
        bias = sb("cBs", [P, CL, D])
        ya = sb("y1a", [P, NQ, D])
        yb = sb("y1b", [P, NQ, D])
        yc = sb("y1c", [P, NQ, D])
        st = sb("st1", [P, 4, NQ])
        stw = sb("st1w", [P, 4, T])
        hs = sb("hs1", [128, 2, CH])
        zt = sb("zt1", [128, 1, P])
        names = ("loaded", "g_r", "agg_r", "aT_r", "o_r", "var_r", "root_r", "chain", "y_free", "x1_in", "x2_r",
                 "x2_out", "pair_r", "pair_out", "tr_r", "hs_r", "hs_out0", "hs_out1", "zset", "z_out", "var2", "root2", "chain2")
        (loaded, g_r, agg_r, aT_r, o_r, var_r, root_r, chain, y_free, x1_in, x2_r,
         x2_out, pair_r, pair_out, tr_r, hs_r, hs_out0, hs_out1, zset, z_out, var2, root2, chain2) = (sem("c_" + n) for n in names)
        hs_out = (hs_out0, hs_out1)

        def steps(eng, body):
            with eng.Fori(0, CL) as l:
                with eng.Fori(0, NC) as ch:
                    body(l, ch, CH, l * SC + ch)
                body(l, NC, P, l * SC + NC)

        with nc.Block() as block:
            @block.gpsimd
            def _(pool):
                nc.gpsimd.memset(zt[:], 0.0).then_inc(zset, 1)
                scatter(nc, pool, scat_sems, scat, scatD, WT, 0, SPLIT)

            @block.sync
            def _(sp):
                sp.dma_start(xr[:], xh1D).then_inc(loaded, 16)
                sp.dma_start(W[:], cW.rearrange("l p d -> p l d")).then_inc(loaded, 16)
                sp.dma_start(bias[:], cB.rearrange("(o l) d -> o l d", o=1).to_broadcast([P, CL, D])).then_inc(loaded, 16)
                sp.wait_ge(zset, 1)
                sp.dma_start(hTD[:, 1, :].rearrange("p (t n) -> p t n", n=P), zt[:].to_broadcast([128, T, P])).then_inc(z_out, 16)
                sp.wait_ge(o_r, CL * SC + 1)
                sp.wait_ge(g_r, (CL + 1) * SC)
                sp.dma_start(F[:, 0], x1D).then_inc(x1_in, 16)
                sp.wait_ge(x2_r, 1)
                sp.dma_start(x2D, F[:, 0]).then_inc(x2_out, 16)
                sp.wait_ge(pair_r, 1)
                sp.dma_start(hnD[:, :, :, 0:D], pair).then_inc(pair_out, 16)
                for ch in range(SC):
                    w = min(CH, N - ch * CH)
                    sp.wait_ge(hs_r, ch + 1)
                    for to in (hTD[:, 0, ch * CH:ch * CH + w], xhTD[:, ch * CH:ch * CH + w]):
                        sp.dma_start(to, hs[:, ch % 2, 0:w]).then_inc(hs_out[ch % 2], 16)
                for s_, n in ((x2_out, 16), (pair_out, 16), (hs_out0, 32 * (SC - SC // 2)), (hs_out1, 32 * (SC // 2)), (z_out, 16)):
                    sp.wait_ge(s_, n)

            @block.tensor
            def _(pe):
                pe.wait_ge(loaded, 48)
                pe.sem_inc(o_r, 1)

                def step(l, ch, w, s):
                    k = w // P
                    half = bass.ds(l % 2, 1)
                    pe.wait_ge(g_r, l * SC + SC)
                    for j in range(T):
                        cols = A[:, j, bass.ds(ch * CH, w)]
                        for part in range(2):
                            nc.tensor.matmul(PS[0][:, 0:w], G[:, half, j, part, :].rearrange("p o d -> p (o d)"), cols,
                                             start=(j == 0 and part == 0), stop=False)
                    for q in range(k):
                        for part in range(2):
                            last = nc.tensor.matmul(PS[0][:, q * P:(q + 1) * P],
                                                    G[:, half, bass.ds(ch * NQ + q, 1), part, :].rearrange("p o a d -> p (o a d)"),
                                                    identh[0:P, 0:P], start=False, stop=(q == k - 1 and part == 1))
                    last.then_inc(agg_r, 1)
                    pe.wait_ge(aT_r, s + 1)
                    pe.wait_ge(y_free, s + 1)
                    for q in range(k):
                        last = nc.tensor.matmul(PS[1][0:P, q * D:(q + 1) * D], aT[:, q * P:(q + 1) * P],
                                                W[:, bass.ds(l, 1), :].rearrange("p o d -> p (o d)"), start=True, stop=True)
                    last.then_inc(o_r, 1)
                steps(pe, step)
                pe.wait_ge(pair_r, 1)
                for ch in range(SC):
                    if ch >= 2:
                        pe.wait_ge(hs_r, ch - 1)
                    for q in range(min(NQ, T - ch * NQ)):
                        last = nc.tensor.transpose(PS[2 + ch % 2][:, q * P:(q + 1) * P], F[:, 1, ch * NQ + q, :], ident[0:P, 0:P])
                    last.then_inc(tr_r, 1)

            @block.scalar
            def _(act):
                def step(l, ch, w, s):
                    k = w // P
                    act.wait_ge(agg_r, s + 1)
                    act.wait_ge(o_r, s + 1)
                    nc.scalar.activation(aT[:, 0:w], PS[0][:, 0:w], ACT.Copy, scale=1.0 / UP).then_inc(aT_r, 1)
                    act.wait_ge(var_r, s + 1)
                    nc.scalar.activation(st[:, 3, 0:k], st[:, 2, 0:k], ACT.Sqrt).then_inc(root_r, 1)
                steps(act, step)
                act.wait_ge(var2, 1)
                nc.scalar.activation(stw[:, 3, :], stw[:, 2, :], ACT.Sqrt).then_inc(root2, 1)
                for ch in range(SC):
                    w = min(CH, N - ch * CH)
                    act.wait_ge(tr_r, ch + 1)
                    if ch >= 2:
                        act.wait_ge(hs_out[ch % 2], 32 * (ch // 2))
                    nc.scalar.copy(hs[:, ch % 2, 0:w], PS[2 + ch % 2][:, 0:w]).then_inc(hs_r, 1)

            @block.vector
            def _(dve):
                V_ = nc.vector
                dve.wait_ge(loaded, 48)
                dve.sem_inc(y_free, 1)
                dn2 = Done(dve, chain2)
                wide = lambda a: a[:, :, None].to_broadcast([P, T, D])
                dn2(V_.tensor_tensor(F[:, 1], xr[:], wide(col[:, 3, :]), ALU.mult))
                dn2(V_.tensor_copy(G[:, 0, :, 0, :], F[:, 1]))
                dn2(V_.tensor_tensor(G[:, 0, :, 1, :], F[:, 1], G[:, 0, :, 0, :], ALU.subtract))
                dve.sem_inc(g_r, SC)
                done = Done(dve, chain)
                K_ = 17

                def step(l, ch, w, s):
                    k = w // P
                    n0 = done.n

                    def dn(ins):
                        done.n += 1
                        ins.then_inc(chain, 1)
                        dve.wait_ge(chain, s * K_ + done.n - n0)
                    tiles = bass.ds(ch * NQ, k)
                    bc = lambda a: a[:, :, None].to_broadcast([P, k, D])
                    y, xc, sq = ya[:, 0:k, :], yb[:, 0:k, :], yc[:, 0:k, :]
                    dve.wait_ge(o_r, s + 2)
                    dn(V_.tensor_tensor(y, PS[1][0:P, 0:k * D].rearrange("p (k d) -> p k d", d=D), bc(col[:, 2, tiles]), ALU.mult))
                    dve.sem_inc(y_free, 1)
                    dn(V_.tensor_tensor(y, y, bias[:, bass.ds(l, 1), :].to_broadcast([P, k, D]), ALU.add))
                    dn(V_.tensor_scalar(y, y, 0.0, None, ALU.max))

                    def mid(ins):
                        ins.then_inc(var_r, 1)
                        dve.wait_ge(root_r, s + 1)
                    norm(V_, dn, mid, y, xc, sq, st[:, :, 0:k], None)
                    dn(V_.tensor_tensor(xr[:, tiles, :], xr[:, tiles, :], xc, ALU.add))
                    dn(V_.tensor_tensor(y, xr[:, tiles, :], bc(col[:, 3, tiles]), ALU.mult))
                    nxt = bass.ds((l + 1) % 2, 1)
                    dn(V_.tensor_copy(G[:, nxt, tiles, 0, :].rearrange("p o k d -> p (o k) d"), y))
                    V_.tensor_tensor(G[:, nxt, tiles, 1, :].rearrange("p o k d -> p (o k) d"), y,
                                     G[:, nxt, tiles, 0, :].rearrange("p o k d -> p (o k) d"), ALU.subtract).then_inc(g_r, 1)
                    dve.wait_ge(g_r, s + 1 + SC)
                    assert done.n - n0 == K_, done.n - n0
                steps(dve, step)
                dve.wait_ge(x1_in, 16)
                dn2(V_.tensor_tensor(F[:, 0], F[:, 0], xr[:], ALU.add))
                dve.sem_inc(x2_r, 1)

                def mid(ins):
                    ins.then_inc(var2, 1)
                    dve.wait_ge(root2, 1)
                norm(V_, dn2, mid, F[:, 0], F[:, 1], xr[:], stw, F[:, 1])
                dn2(V_.tensor_scalar(xr[:], F[:, 1], UP, None, ALU.mult))
                dve.wait_ge(x2_out, 16)
                dn2(V_.tensor_copy(pair[:, :, 0, :], xr[:]))
                V_.tensor_tensor(pair[:, :, 1, :], xr[:], pair[:, :, 0, :], ALU.subtract).then_inc(pair_r, 1)


def gru(nc, sem, PS, bih, bhh, scat, scat_sems, scatD, WT, VD, whhD, hnD, hTD, A, ident):
    with ExitStack() as c:
        def sb(name, shape, dt=f32):
            return c.enter_context(nc.sbuf_tensor(name, shape, dt))

        G = sb("G2", [P, T, 2, S2], f16)
        V = sb("V2", [128, 2, GATES])
        U = sb("U2", [128, 2, GATES])
        aT = sb("aT2", [128, 2, CH])
        H = sb("H2", [128, 2, CH])
        HN = sb("HN2", [128, 2, CH])
        R = sb("R2", [128, CH])
        stg = sb("stg2", [P, NQ, 2, 128], f16)
        bi = sb("bi2", [128, 6])
        bh = sb("bh2", [128, 6])
        bs = sb("bs2", [128, 4])
        names = ("loaded", "G_in", "V_in", "H_in", "agg_r", "aT_r", "r_g", "h_g", "i_g", "z_g", "r_r", "z_r", "n_r", "u1", "u2",
                 "d_r", "dz_r", "hn_r", "hn_out", "tr_r", "hi_r", "lo_r", "st_out", "bs_r", "tick")
        (loaded, G_in, V_in, H_in, agg_r, aT_r, r_g, h_g, i_g, z_g, r_r, z_r, n_r, u1, u2,
         d_r, dz_r, hn_r, hn_out, tr_r, hi_r, lo_r, st_out, bs_r, tick) = (sem("g_" + n) for n in names)

        def steps(eng, step, late, end):
            def layer(l, halves):
                step(l, 0, CH, l * SC, halves, lambda: None)
                with eng.Fori(1, NC) as ch:
                    step(l, ch, CH, l * SC + ch, halves, lambda: late(ch - 1, CH, l * SC + ch - 1))
                step(l, NC, P, l * SC + NC, halves, lambda: late(NC - 1, CH, l * SC + NC - 1))
                late(NC, P, l * SC + NC)
                end(l)
            layer(0, 1)
            with eng.Fori(1, GL) as l:
                layer(l, 2)

        with nc.Block() as block:
            @block.gpsimd
            def _(pool):
                scatter(nc, pool, scat_sems, scat, scatD, WT, SPLIT, NBATCH)

            @block.sync
            def _(sp):
                sp.dma_start(G[:, :, :, 0:D], hnD[:, :, :, 0:D]).then_inc(G_in, 16)
                sp.dma_start(V[:], VD[0].rearrange("p (a g) -> p a g", a=2)).then_inc(V_in, 16)
                sp.dma_start(U[:], whhD.rearrange("p (a g) -> p a g", a=2)).then_inc(loaded, 16)
                sp.dma_start(bi[:], bih.rearrange("(c p) -> p c", p=128), allow_slow_non_contiguous=True).then_inc(loaded, 16)
                sp.dma_start(bh[:], bhh.rearrange("(c p) -> p c", p=128), allow_slow_non_contiguous=True).then_inc(loaded, 16)

                def store(e, ch, k, hf):
                    sp.wait_ge(lo_r, e + 3)
                    sp.dma_start(hnD[:, bass.ds(ch * NQ, k), :, hf * 128:(hf + 1) * 128], stg[:, 0:k]).then_inc(st_out, 16)

                def step(l, ch, w, s, halves, late):
                    sp.wait_ge(hn_r, 2 * s + 1)
                    sp.sem_inc(tick, 1)
                    sp.wait_ge(z_g, 2 * s + 2)
                    sp.wait_ge(hn_out, 32 * s + 32)
                    sp.dma_start(H[:, :, 0:w], hTD[:, :, bass.ds(ch * CH, w)]).then_inc(H_in, 16)
                    late()
                    for hf in range(2):
                        sp.wait_ge(hn_r, 2 * s + hf + 2)
                        sp.dma_start(hTD[:, hf, bass.ds(ch * CH, w)], HN[:, hf, 0:w]).then_inc(hn_out, 16)
                    store(2 * s, ch, w // P, 0)

                def late(ch, w, s):
                    store(2 * s + 1, ch, w // P, 1)

                def end(l):
                    sp.wait_ge(st_out, 32 * SC * l + 32 * SC + 16)
                    sp.dma_start(G[:], hnD).then_inc(G_in, 16)
                    nxt = (l + 1) % GL
                    sp.wait_ge(z_g, 2 * SC * l + 2 * SC + 2)
                    sp.dma_start(V[:].rearrange("p a g -> p (a g)"), VD[bass.ds(nxt, 1)].rearrange("o p g -> (o p) g")).then_inc(V_in, 16)
                sp.sem_inc(st_out, 16)
                sp.sem_inc(hn_out, 32)
                steps(sp, step, late, end)
                sp.wait_ge(G_in, 16 * GL + 16)
                sp.wait_ge(V_in, 16 * GL + 16)
                sp.wait_ge(hn_out, 32 * SC * GL + 32)

            @block.tensor
            def _(pe):
                pe.sem_inc(z_g, 2)
                pe.wait_ge(loaded, 48)

                def turn(e, hf, k):
                    pe.wait_ge(hn_r, e + 2)
                    pe.wait_ge(lo_r, e + 1)
                    for q in range(k):
                        last = nc.tensor.transpose(PS[6 + hf][0:P, q * 128:(q + 1) * 128], HN[:, hf, q * P:(q + 1) * P], ident[:])
                    last.then_inc(tr_r, 1)

                def step(l, ch, w, s, halves, late):
                    k = w // P
                    pe.wait_ge(G_in, 16 * l + 16)
                    for half in range(halves):
                        for j in range(T):
                            for part in range(2):
                                last = nc.tensor.matmul(PS[half][:, 0:w], G[:, j, part, half * 128:(half + 1) * 128],
                                                        A[:, j, bass.ds(ch * CH, w)],
                                                        start=(j == 0 and part == 0), stop=(j == T - 1 and part == 1))
                    last.then_inc(agg_r, 1)
                    late()
                    pe.wait_ge(aT_r, s + 1)
                    pe.wait_ge(H_in, 16 * s + 16)
                    pe.wait_ge(V_in, 16 * l + 16)
                    for hf in range(2):
                        m = 2 * s + hf

                        def gate(bank, free, ready, g, terms):
                            pe.wait_ge(free, m + 1)
                            terms = [(wt, a, kt) for wt, a in terms for kt in range(halves)]
                            for n, (wt, a, kt) in enumerate(terms):
                                last = nc.tensor.matmul(PS[bank][:, 0:w], wt[:, kt, g:g + 128], a[:, kt, 0:w],
                                                        start=(n == 0), stop=(n == len(terms) - 1))
                            last.then_inc(ready, 1)
                        gate(2, r_r, r_g, hf * 128, ((V, aT), (U, H)))
                        gate(3, u1, h_g, 2 * S2 + hf * 128, ((U, H),))
                        gate(4, u2, i_g, 2 * S2 + hf * 128, ((V, aT),))
                        gate(5, dz_r, z_g, S2 + hf * 128, ((V, aT), (U, H)))
                    turn(2 * s, 0, k)

                def late(ch, w, s):
                    turn(2 * s + 1, 1, w // P)
                steps(pe, step, late, lambda l: None)

            @block.scalar
            def _(act):
                act.wait_ge(bs_r, 1)
                act.sem_inc(r_r, 1)

                def high(e, hf, k):
                    act.wait_ge(tr_r, e + 1)
                    act.wait_ge(st_out, 16 * e + 16)
                    nc.scalar.activation(stg[:, 0:k, 0, :], PS[6 + hf][0:P, 0:k * 128].rearrange("p (k d) -> p k d", k=k),
                                         ACT.Copy, scale=UP).then_inc(hi_r, 1)

                def step(l, ch, w, s, halves, late):
                    act.wait_ge(agg_r, s + 1)
                    act.wait_ge(z_g, 2 * s + 2)
                    for half in range(halves):
                        last = nc.scalar.activation(aT[:, half, 0:w], PS[half][:, 0:w], ACT.Copy, scale=1.0 / UP)
                    last.then_inc(aT_r, 1)
                    late()
                    for hf in range(2):
                        m = 2 * s + hf
                        act.wait_ge(r_g, m + 1)
                        act.wait_ge(hn_r, m + 1)
                        nc.scalar.activation(R[:, 0:w], PS[2][:, 0:w], ACT.Sigmoid, bias=bs[:, hf:hf + 1]).then_inc(r_r, 1)
                        act.wait_ge(z_g, m + 3)
                        nc.scalar.activation(PS[5][:, 0:w], PS[5][:, 0:w], ACT.Sigmoid, bias=bs[:, 2 + hf:3 + hf]).then_inc(z_r, 1)
                        act.wait_ge(u2, m + 2)
                        nc.scalar.activation(R[:, 0:w], R[:, 0:w], ACT.Tanh, bias=bi[:, 4 + hf:5 + hf]).then_inc(n_r, 1)
                    high(2 * s, 0, w // P)

                def late(ch, w, s):
                    high(2 * s + 1, 1, w // P)
                steps(act, step, late, lambda l: None)

            @block.vector
            def _(dve):
                V_ = nc.vector
                dve.wait_ge(loaded, 48)
                V_.tensor_tensor(bs[:], bi[:, 0:4], bh[:, 0:4], ALU.add).then_inc(bs_r, 1)
                for s_, n in ((u1, 1), (u2, 1), (dz_r, 1), (hn_r, 1), (lo_r, 2)):
                    dve.sem_inc(s_, n)

                def low(e, hf, k):
                    dve.wait_ge(hi_r, e + 1)
                    V_.scalar_tensor_tensor(stg[:, 0:k, 1, :], PS[6 + hf][0:P, 0:k * 128].rearrange("p (k d) -> p k d", k=k), UP,
                                            stg[:, 0:k, 0, :], ALU.mult, ALU.subtract).then_inc(lo_r, 1)

                def step(l, ch, w, s, halves, late):
                    late()
                    dve.wait_ge(hn_out, 32 * s + 32)
                    dve.wait_ge(H_in, 16 * s + 16)
                    for hf in range(2):
                        m = 2 * s + hf
                        dve.wait_ge(tr_r, m - 1 + (hf == 0)) if not isinstance(m, int) or m > 1 else None
                        dve.wait_ge(r_r, m + 2)
                        dve.wait_ge(h_g, m + 1)
                        r, n = R[:, 0:w], HN[:, hf, 0:w]
                        V_.scalar_tensor_tensor(r, PS[3][:, 0:w], bh[:, 4 + hf:5 + hf], r, ALU.add, ALU.mult).then_inc(u1, 1)
                        dve.wait_ge(u1, m + 2)
                        dve.wait_ge(i_g, m + 1)
                        V_.tensor_tensor(r, r, PS[4][:, 0:w], ALU.add).then_inc(u2, 1)
                        dve.wait_ge(n_r, m + 1)
                        V_.tensor_tensor(n, H[:, hf, 0:w], r, ALU.subtract).then_inc(d_r, 1)
                        dve.wait_ge(d_r, m + 1)
                        dve.wait_ge(z_r, m + 1)
                        V_.tensor_tensor(n, n, PS[5][:, 0:w], ALU.mult).then_inc(dz_r, 1)
                        dve.wait_ge(dz_r, m + 2)
                        V_.tensor_tensor(n, n, r, ALU.add).then_inc(hn_r, 1)
                    low(2 * s, 0, w // P)

                def late(ch, w, s):
                    low(2 * s + 1, 1, w // P)
                steps(dve, step, late, lambda l: None)


def tail(nc, sem, PS, big, l0b, l1b, b1, b2, out, WT, l0D, l1D, w12D, x2D, hTD, xhTD):
    with ExitStack() as c:
        sb = pieces(big)
        RING = 5
        wt = sb("wt", [128, RING, N])
        hT = sb("hT3", [128, 2, CH])
        xT = sb("xT3", [128, CH])
        x3 = sb("x3", [P, T, D])
        xc = sb("xc3", [P, T, D])
        sq = sb("sq3", [P, T, D])
        st = sb("st3", [P, 4, T])
        x3T = sb("x3T", [128, N])
        y0 = sb("y0", [128, 2, CH])
        y1 = sb("y1", [128, CH])
        a = sb("a3", [128, 2, CH])
        b = sb("b3", [128, 2, CH])
        o = sb("o3", [P, 2, NQ, D])
        L0, L1, W = sb("L0", [128, 3, 256]), sb("L1", [128, 2, 128]), sb("W3", [128, 2, D])
        bl0, bl1 = sb("bl0", [128, 2]), sb("bl1", [128, 1])
        bb = sb("bb", [P, 2, D])
        ident = sb("ident3", [128, 128])
        names = ("made", "loaded", "h_in", "m0", "a0", "m1", "a1", "tr", "x_r", "var_r", "root_r", "chain", "xh_r", "t2", "t2c",
                 "agg", "a_r", "b_r", "o_g", "o_r", "out0", "out1", "bias_r", "w_used", "o1", "o2")
        (made, loaded, h_in, m0, a0, m1, a1, tr, x_r, var_r, root_r, chain, xh_r, t2, t2c,
         agg, a_r, b_r, o_g, o_r, out0, out1, bias_r, w_used, o1, o2) = (sem("t_" + n) for n in names)
        w_in = [sem(f"t_w{i}") for i in range(RING)]
        outs = (out0, out1)
        wid = lambda ch: min(CH, N - ch * CH)
        ot = out.rearrange("(k p) d -> p k d", p=P)

        with nc.Block() as block:
            @block.gpsimd
            def _(pool):
                nc.gpsimd.memset(ident[:], 0.0).then_inc(made, 1)
                pool.wait_ge(made, 1)
                nc.gpsimd.affine_select(out=ident[:], in_=ident[:], compare_op=ALU.not_equal, fill=1.0,
                                        base=0, pattern=[[-1, 128]], channel_multiplier=1).then_inc(made, 1)

            @block.sync
            def _(sp):
                for to, frm in ((L0, l0D), (L1, l1D), (W, w12D)):
                    sp.dma_start(to[:].rearrange("p a b -> p (a b)"), frm).then_inc(loaded, 16)
                sp.dma_start(bl0[:], l0b.rearrange("(c p) -> p c", p=128), allow_slow_non_contiguous=True).then_inc(loaded, 16)
                sp.dma_start(bl1[:], l1b.rearrange("(c p) -> p c", p=128), allow_slow_non_contiguous=True).then_inc(loaded, 16)
                for n, v in enumerate((b1, b2)):
                    sp.dma_start(bb[:, n, :], v.rearrange("(o d) -> o d", o=1).to_broadcast([P, D])).then_inc(loaded, 16)
                sp.dma_start(x3[:], x2D).then_inc(loaded, 16)
                for ch in range(SC):
                    w = wid(ch)
                    if ch:
                        sp.wait_ge(m0, ch)
                    sp.dma_start(hT[:, :, 0:w], hTD[:, :, ch * CH:ch * CH + w]).then_inc(h_in, 16)
                    sp.dma_start(xT[:, 0:w], xhTD[:, ch * CH:ch * CH + w]).then_inc(h_in, 16)
                for ch in range(SC):
                    sp.wait_ge(o_r, ch + 1)
                    k = wid(ch) // P
                    sp.dma_start(ot[:, ch * NQ:ch * NQ + k, :], o[:, ch % 2, 0:k, :]).then_inc(outs[ch % 2], 16)
                sp.wait_ge(out0, 16 * (SC - SC // 2))
                sp.wait_ge(out1, 16 * (SC // 2))

            @block.scalar
            def _(act):
                rows = WT.rearrange("n o -> (n o)")

                def load(g, i):
                    act.dma_start(wt[:, i, :], rows[bass.ds((g * RING + i) * P * N, 128 * N)].rearrange("(p n) -> p n", n=N)).then_inc(w_in[i], 16)
                for i in range(RING):
                    load(0, i)
                act.wait_ge(loaded, 16 * 8)
                for ch in range(SC):
                    w = wid(ch)
                    act.wait_ge(m0, ch + 1)
                    if ch:
                        act.wait_ge(m1, ch)
                    for h in range(2):
                        last = nc.scalar.activation(y0[:, h, 0:w], PS[h][:, 0:w], ACT.Relu, bias=bl0[:, h:h + 1])
                    last.then_inc(a0, 1)
                    act.wait_ge(m1, ch + 1)
                    if ch:
                        act.wait_ge(tr, ch)
                    nc.scalar.activation(y1[:, 0:w], PS[2][:, 0:w], ACT.Relu, bias=bl1[:, 0:1]).then_inc(a1, 1)
                act.wait_ge(var_r, 1)
                nc.scalar.activation(st[:, 3, :], st[:, 2, :], ACT.Sqrt).then_inc(root_r, 1)
                for ch in range(SC):
                    w = wid(ch)
                    act.wait_ge(t2, ch + 1)
                    nc.scalar.copy(x3T[:, ch * CH:ch * CH + w], PS[6 + ch % 2][:, 0:w]).then_inc(t2c, 1)
                with act.Fori(1, T // RING) as g:
                    for i in range(RING):
                        act.wait_ge(w_used, g * RING + i - (RING - 1))
                        load(g, i)

            @block.tensor
            def _(pe):
                pe.wait_ge(made, 2)
                pe.wait_ge(loaded, 16 * 8)
                for ch in range(SC):
                    w = wid(ch)
                    pe.wait_ge(h_in, 32 * ch + 32)
                    if ch:
                        pe.wait_ge(a0, ch)
                    for h in range(2):
                        for kt, v in enumerate((hT[:, 0, 0:w], hT[:, 1, 0:w], xT[:, 0:w])):
                            last = nc.tensor.matmul(PS[h][:, 0:w], L0[:, kt, h * 128:(h + 1) * 128], v, start=(kt == 0), stop=(kt == 2))
                    last.then_inc(m0, 1)
                    pe.wait_ge(a0, ch + 1)
                    if ch:
                        pe.wait_ge(a1, ch)
                    for kt in range(2):
                        last = nc.tensor.matmul(PS[2][:, 0:w], L1[:, kt, :], y0[:, kt, 0:w], start=(kt == 0), stop=(kt == 1))
                    last.then_inc(m1, 1)
                    pe.wait_ge(a1, ch + 1)
                    if ch:
                        pe.wait_ge(x_r, ch)
                    for q in range(w // P):
                        last = nc.tensor.transpose(PS[3][0:P, q * 128:(q + 1) * 128], y1[:, q * P:(q + 1) * P], ident[:])
                    last.then_inc(tr, 1)
                pe.wait_ge(xh_r, 1)
                for ch in range(SC):
                    w = wid(ch)
                    if ch >= 2:
                        pe.wait_ge(t2c, ch - 1)
                    for q in range(w // P):
                        last = nc.tensor.transpose(PS[6 + ch % 2][:, q * P:(q + 1) * P], xc[:, ch * NQ + q, :], ident[0:P, 0:P])
                    last.then_inc(t2, 1)
                pe.wait_ge(t2c, SC)

                def tile(g, i, start=False, stop=False):
                    pe.wait_ge(w_in[i], 16 * g + 16)
                    for ch in range(SC):
                        w = wid(ch)
                        last = nc.tensor.matmul(PS[ch][:, 0:w], xcs(g, i), wt[0:P, i, ch * CH:ch * CH + w], start=start, stop=stop)
                    last.then_inc(w_used, 1)
                xcs = lambda g, i: xc[:, g * RING + i, :]
                for g in range(T // RING):
                    for i in range(RING):
                        tile(g, i, start=(g == 0 and i == 0), stop=(g == T // RING - 1 and i == RING - 1))
                for ch in range(SC):
                    k = wid(ch) // P
                    pe.wait_ge(a_r, ch + 1)
                    pe.wait_ge(b_r, ch + 1)
                    for q in range(k):
                        for n, v in enumerate((a, b)):
                            last = nc.tensor.matmul(PS[ch][0:P, q * D:(q + 1) * D], v[:, ch % 2, q * P:(q + 1) * P], W[:, n, :], start=(n == 0), stop=(n == 1))
                    last.then_inc(o_g, 1)

            @block.vector
            def _(dve):
                V_ = nc.vector
                dn = Done(dve, chain)
                dve.wait_ge(loaded, 16 * 8)
                dn(V_.tensor_tensor(bb[:, 0, :], bb[:, 0, :], bb[:, 1, :], ALU.add))
                for ch in range(SC):
                    k = wid(ch) // P
                    dve.wait_ge(tr, ch + 1)
                    v = x3[:, ch * NQ:ch * NQ + k, :]
                    V_.tensor_tensor(v, v, PS[3][0:P, 0:k * D].rearrange("p (k d) -> p k d", d=D), ALU.add).then_inc(x_r, 1)
                dve.wait_ge(x_r, SC)

                def mid(ins):
                    ins.then_inc(var_r, 1)
                    dve.wait_ge(root_r, 1)
                norm(V_, dn, mid, x3[:], xc[:], sq[:], st, xc[:])
                dve.sem_inc(xh_r, 1)
                dve.wait_ge(w_used, T)
                dve.wait_ge(t2c, SC)

                def finish(ch):
                    k = wid(ch) // P
                    dve.wait_ge(o_g, ch + 1)
                    if ch >= 2:
                        dve.wait_ge(outs[ch % 2], 16 * (ch // 2))
                    v = o[:, ch % 2, 0:k, :]
                    V_.tensor_tensor(v, PS[ch][0:P, 0:k * D].rearrange("p (k d) -> p k d", d=D), bb[:, 0:1, :].to_broadcast([P, k, D]), ALU.add).then_inc(o1, 1)
                    dve.wait_ge(o1, ch + 1)
                    V_.scalar_tensor_tensor(v, v, ALPHA, v, ALU.mult, ALU.max).then_inc(o2, 1)
                    dve.wait_ge(o2, ch + 1)
                    V_.tensor_tensor(v, v, x3[:, ch * NQ:ch * NQ + k, :], ALU.add).then_inc(o_r, 1)
                for ch in range(SC):
                    w = wid(ch)
                    if ch >= 2:
                        dve.wait_ge(o_g, ch - 1)
                    t = x3T[:, ch * CH:ch * CH + w]
                    V_.tensor_tensor(a[:, ch % 2, 0:w], PS[ch][:, 0:w], t, ALU.add).then_inc(a_r, 1)
                    V_.tensor_tensor(b[:, ch % 2, 0:w], PS[ch][:, 0:w], t, ALU.mult).then_inc(b_r, 1)
                    if ch:
                        finish(ch - 1)
                finish(SC - 1)


_INS = ['x', 'src', 'dst', 'edge_weight', 'L0_gnn_W', 'L0_gnn_a', 'L1_gnn_W', 'L1_gnn_b', 'L2_gnn_W',
        'L2_gnn_w_ih', 'L2_gnn_w_hh', 'L2_gnn_b_ih', 'L2_gnn_b_hh', 'L2_gnn_l0_w', 'L2_gnn_l0_b',
        'L2_gnn_l1_w', 'L2_gnn_l1_b', 'L3_gnn_W1', 'L3_gnn_b1', 'L3_gnn_W2', 'L3_gnn_b2']


def kernel(**inputs):
    import numpy as _np
    import concourse.bacc as _bacc
    from concourse import mybir as _mybir
    from concourse.bass_utils import run_bass_kernel_spmd as _run

    nc = _bacc.Bacc("TRN2", target_bir_lowering=False, num_devices=1)
    arrays, args = {}, []
    for name in _INS:
        a = _np.ascontiguousarray(inputs[name])
        arrays[f"in_{name}_dram"] = a
        args.append(nc.dram_tensor(f"in_{name}_dram", a.shape, _mybir.dt.from_np(a.dtype), kind="ExternalInput").ap())
    args.append(nc.dram_tensor("out_0_dram", (N, D), f32, kind="ExternalOutput").ap())
    gnn_kernel(nc, *args)
    r = _run(nc, [arrays], core_ids=[0])
    return r.results[0]["out_0_dram"]
```

```python
import concourse.bass as bass
from concourse import mybir
from concourse.alu_op_type import AluOpType as ALU
from contextlib import ExitStack

N, D, E = 3125, 128, 50000
P = 125
T = N // P
CH = 500
NQ = CH // P
NC = N // CH
SC = NC + 1
LANE = 128
ET = -(-E // LANE)
EG = 4
WIN = 512 // T
NW = -(-N // WIN)
WC = WIN * T
SB = -(-NW * 4 // LANE)
ROUND = 1.5 * 2.0 ** 23
S2 = 256
GL, CL = 5, 3
GATES = 3 * S2
UP = 256.0
EPS = 1e-5
ALPHA = 0.2
BIG = 60000.0
SPAN = 4
STEP = 4
PAD_SRC, PAD_DST = N + 1, -2
BATCH = 5
NBATCH = 2 * -(-ET // (2 * BATCH))
MERGE = (NW - 1) // STEP
assert (NW - 1) % STEP == 0 and NBATCH == 2 * MERGE + 2 and NBATCH * BATCH <= EG * LANE
ZF = MERGE
ZN = 490
ZW = 4 * ZN
TABLE = ZF * LANE * ZW
DUMP = N * N + 8192
FAR = 1000.0
RAISE = 100000.0
SPLIT = 16
assert TABLE >= DUMP + LANE and TABLE >= (N + 3) * N and PAD_SRC * N < DUMP

f32, f16, bf16, i32 = mybir.dt.float32, mybir.dt.float16, mybir.dt.bfloat16, mybir.dt.int32
ACT = mybir.ActivationFunctionType
X = mybir.AxisListType.X


def gnn_kernel(nc, x, src, dst, ew, aW, aA, cW, cB, gW, wih, whh, bih, bhh, l0w, l0b, l1w, l1b,
               w1, b1, w2, b2, out):
    ctx = ExitStack()

    def dram(name, shape, dt=f32):
        return nc.dram_tensor(name, shape, dt).ap()

    WT = dram("WT", (TABLE, 1))
    keyD = dram("keyD", (EG * LANE, LANE))
    csD = dram("csD", (EG * LANE, 2 * LANE))
    scatD = dram("scatD", (NBATCH, LANE, 2 * BATCH), i32)
    VD = dram("VD", (GL, LANE, 2 * GATES))
    whhD = dram("whhD", (LANE, 2 * GATES))
    l0D = dram("l0D", (LANE, 3 * 256))
    l1D = dram("l1D", (LANE, 2 * LANE))
    w12D = dram("w12D", (LANE, 2 * LANE))
    rowD = dram("rowD", (2, N))
    xhD = dram("xhD", (P, T, 2, D), f16)
    xh1D = dram("xh1D", (P, T, D))
    hnD = dram("hnD", (P, T, 2, S2), f16)
    hTD = dram("hTD", (128, 2, N))
    xhTD = dram("xhTD", (128, N))
    x1D = dram("x1D", (P, T, D))
    x2D = dram("x2D", (P, T, D))
    colD = dram("colD", (P, 4 * T))

    with ctx:
        def sem(name):
            return ctx.enter_context(nc.semaphore(name))

        banks = ctx.enter_context(nc.psum_tensor("banks", [128, 8, 512], f32))
        PS = [banks[:, i, :] for i in range(8)]
        big = ctx.enter_context(nc.sbuf_tensor("big", [128, T * N // 2 + 1], f32))
        A = big[:].bitcast(f16)[0:P, 0:T * N].rearrange("p (t n) -> p t n", n=N)
        with ExitStack() as c:
            def sb(name, shape, dt=f32):
                return c.enter_context(nc.sbuf_tensor(name, shape, dt))

            ecol = sb("ecol", [128, 4, EG * LANE])
            edges = dict(
                ecol=ecol,
                comb=ecol[:, 0],
                sib=ecol[:, 1],
                keyc=ecol[:, 2],
                wc=ecol[:, 3],
                wp=sb("wp", [128, EG * LANE, 4], bf16),
                rank=sb("rank", [128, 1], i32),
                wcol=sb("wcol", [128, 2, SB * LANE]),
                visits=sb("visits", [1, 4, 160], i32),
                tcol=sb("tcol", [P, T]),
                scol=sb("scol", [P, T]),
                ident=sb("ident", [128, 128]))
            prepare(nc, sem, PS, big, edges, x, src, dst, ew, aW, aA, gW, wih, whh, l0w, l1w, w1, w2,
                    keyD, csD, VD, whhD, l0D, l1D, w12D, xhD)
            counts(nc, sem, PS, banks, A, edges, keyD, scatD, WT, colD, rowD)
        layers(nc, sem, PS, big, A, x, aW, cW, cB, bih, bhh, l0b, l1b, b1, b2, out, WT, scatD, VD, whhD, l0D, l1D, w12D,
               rowD, xhD, xh1D, x1D, x2D, colD, hnD, hTD, xhTD)


def pieces(big):
    used = [0]

    def sb(name, shape, dt=f32):
        size, at = 1, used[0]
        for n in shape[1:]:
            size *= n
        used[0] += -(-size // (2 if dt == f16 else 1))
        assert used[0] <= T * N // 2, name
        v = big[0:shape[0], at:used[0]]
        if dt != f32:
            v = v.bitcast(dt)
        dims = " ".join(f"d{i}" for i in range(1, len(shape)))
        kw = {f"d{i}": shape[i] for i in range(2, len(shape))}
        return v[:, 0:size].rearrange(f"p ({dims}) -> p {dims}", **kw) if len(shape) > 2 else v[:, 0:size]
    return sb


def newton(V_, done, y, v, tmp):
    done(V_.tensor_tensor(tmp, y, y, ALU.mult))
    done(V_.tensor_tensor(tmp, tmp, v, ALU.mult))
    done(V_.tensor_scalar(tmp, tmp, -0.5, 1.5, ALU.mult, ALU.add))
    done(V_.tensor_tensor(y, y, tmp, ALU.mult))


def prepare(nc, sem, PS, big, edges, x, src, dst, ew, aW, aA, gW, wih, whh, l0w, l1w, w1, w2,
            keyD, csD, VD, whhD, l0D, l1D, w12D, xhD):
    with ExitStack() as c:
        sb = pieces(big)
        ecol, wcol, wp, rank, visits, tcol, scol, ident = (
            edges[n] for n in ("ecol", "wcol", "wp", "rank", "visits", "tcol", "scol", "ident"))
        ei = sb("ei", [128, 2, EG, LANE], i32)
        ef = sb("ef", [128, 2, EG, LANE])
        we = sb("we", [128, EG, LANE])
        key = sb("key", [128, EG, LANE])
        near = sb("near", [128, EG, LANE])
        dmin = sb("dmin", [128, EG])
        dmax = sb("dmax", [128, EG])
        tile_no = sb("tile_no", [128, EG])
        base = sb("base", [128, NW])
        over = sb("over", [128, EG, 3, NW])
        cand = sb("cand", [128, 2, NW])
        red = sb("red", [128, 2, NW])
        vis = sb("vis", [1, 6, NW])
        nil = sb("nil", [1, NW])
        wno = sb("wno", [1, NW])
        top = sb("top", [1, 1])
        part = sb("part", [128, EG, LANE])
        cs = sb("cs", [128, EG, 2, LANE])
        near4 = sb("near4", [128, 32])
        hit = sb("hit", [128, 32])
        place = sb("place", [128, 1])
        woff = sb("woff", [128, SB])
        start = sb("start", [128, SB * 32])
        picked = sb("picked", [128, SB, 32])
        tile = sb("tile", [128, SB])
        tilei = sb("tilei", [128, SB], i32)
        gath = sb("gath", [128, SB, 2, LANE])
        xn = sb("xn", [P, T, D])
        sq = sb("sq", [P, T, D])
        pair = sb("pair", [P, T, 2, D], f16)
        st = sb("st", [P, 4, T])
        eps = sb("eps", [128, 1])
        uT = sb("uT", [P, 2, D])
        acol = sb("acol", [128, 2])
        abc = sb("abc", [128, 2, P])
        wihN, whhN = sb("wihN", [128, 6, S2]), sb("whhN", [128, 6, S2])
        l0N, l1N = sb("l0N", [128, 2, 384]), sb("l1N", [128, 1, S2])
        w12N, aWN = sb("w12N", [128, 2, D]), sb("aWN", [128, 1, D])
        gWN = sb("gWN", [128, 2 * GL, S2])
        wihT, whhT = sb("wihT", [128, 2, GATES]), sb("whhT", [128, 2, GATES])
        l0T, l1T = sb("l0T", [128, 3, 256]), sb("l1T", [128, 2, 128])
        w12T, aWT = sb("w12T", [128, 1, 256]), sb("aWT", [128, 1, 128])
        gWT = sb("gWT", [128, 2, GL * S2])
        V = sb("V", [128, 2, 2 * GATES])

        loaded, eloaded, padded, made, chain = (sem(s) for s in ("loaded", "eloaded", "padded", "made", "chain"))
        edge_t, edge_c, w_t, w_c, v_t, v_c, v_st = (
            sem(s) for s in ("edge_t", "edge_c", "w_t", "w_c", "v_t", "v_c", "v_st"))
        x_in, u_t, root_r, red_r, outs, cs_out, gathered, gath_t, gath_c = (
            sem(s) for s in ("x_in", "u_t", "root_r", "red_r", "outs", "cs_out", "gathered", "gath_t", "gath_c"))
        dve_did = sem("dve_did")
        ABC, EDGES, CS, CAND, ROWS, LESS, VAR, PAIR = range(1, 9)

        def runs(nat, rows, cols, tr, per=4):
            r = []
            for b in range(cols):
                for a in range(0, rows, per):
                    r.append((nat, tr, b, a, min(per, rows - a)))
            return r
        jobs = (runs(aWN, 1, 1, aWT) + runs(wihN, 6, 2, wihT, 3) + runs(gWN, 2 * GL, 2, gWT)
                + runs(whhN, 6, 2, whhT, 3) + runs(l0N, 2, 3, l0T) + runs(l1N, 1, 2, l1T) + runs(w12N, 2, 1, w12T))
        full = (E // (LANE * LANE))
        rest = E - full * LANE * LANE
        rt, rl = rest // LANE, rest % LANE
        edge_dmas = 3 * 3 if rl else 3 * 2
        HALF = 2 * GATES // 4

        with nc.Block() as block:
            @block.gpsimd
            def _(pool):
                nc.gpsimd.memset(ei[:, 0], PAD_SRC).then_inc(padded, 1)
                nc.gpsimd.memset(ei[:, 1], PAD_DST).then_inc(padded, 1)
                nc.gpsimd.memset(we[:], 0.0).then_inc(padded, 1)
                nc.gpsimd.memset(eps[:], EPS).then_inc(made, 1)
                nc.gpsimd.iota(base[:], [[WIN, NW]], base=0, channel_multiplier=0,
                               allow_small_or_imprecise_dtypes=True).then_inc(made, 1)
                nc.gpsimd.iota(tile_no[:], [[LANE, EG]], base=0, channel_multiplier=1,
                               allow_small_or_imprecise_dtypes=True).then_inc(made, 1)
                nc.gpsimd.iota(near4[:], [[-4, 32]], base=0, channel_multiplier=1,
                               allow_small_or_imprecise_dtypes=True).then_inc(made, 1)
                nc.gpsimd.iota(woff[:], [[32 * WC, SB]], base=0, channel_multiplier=WC // 4,
                               allow_small_or_imprecise_dtypes=True).then_inc(made, 1)
                nc.gpsimd.iota(rank[:], [[0, 1]], base=(127 + 100) << 23, channel_multiplier=-(1 << 23)).then_inc(made, 1)
                nc.gpsimd.iota(wno[:], [[1, NW]], base=1, channel_multiplier=0,
                               allow_small_or_imprecise_dtypes=True).then_inc(made, 1)
                nc.gpsimd.memset(ident[:], 0.0).then_inc(made, 1)
                pool.wait_ge(made, 8)
                nc.gpsimd.affine_select(out=ident[:], in_=ident[:], compare_op=ALU.not_equal, fill=1.0,
                                        base=0, pattern=[[-1, 128]], channel_multiplier=1).then_inc(made, 1)
                pool.wait_ge(dve_did, CAND)
                nc.gpsimd.partition_all_reduce(red[:].rearrange("p a w -> p (a w)"), cand[:].rearrange("p a w -> p (a w)"), 128,
                                               bass.bass_isa.ReduceOp.max).then_inc(red_r, 1)
                pool.wait_ge(dve_did, ROWS)
                pool.wait_ge(cs_out, 16)
                for b in range(SB):
                    nc.gpsimd.indirect_dma_start(out=gath[:, b].rearrange("p a e -> p (a e)"), out_offset=None, in_=csD,
                                                 in_offset=bass.IndirectOffsetOnAxis(ap=tilei[:, b:b + 1], axis=0)).then_inc(gathered, 16)
                pool.wait_ge(gathered, 16 * SB)

            @block.sync
            def _(sp):
                sp.wait_ge(padded, 3)
                for n, (arr, to) in enumerate(((src, ei[:, 0]), (dst, ei[:, 1]), (ew, we))):
                    m = full * LANE * LANE
                    sp.dma_start(to[:, 0:full, :], arr[0:m].rearrange("(g t e) -> t g e", t=LANE, e=LANE)).then_inc(eloaded, 16)
                    sp.dma_start(to[0:rt, full, :], arr[m:m + rt * LANE].rearrange("(t e) -> t e", e=LANE)).then_inc(eloaded, 16)
                    if rl:
                        m += rt * LANE
                        sp.dma_start(to[rt:rt + 1, full, 0:rl], arr[m:E].rearrange("(t e) -> t e", t=1)).then_inc(eloaded, 16)
                sp.wait_ge(dve_did, EDGES)
                sp.dma_start(keyD.rearrange("(g t) e -> t g e", g=EG), key[:]).then_inc(outs, 16)
                sp.wait_ge(dve_did, CS)
                sp.dma_start(csD.rearrange("(g t) e -> t g e", g=EG), cs[:].rearrange("t g a e -> t g (a e)")).then_inc(cs_out, 16)
                sp.wait_ge(dve_did, PAIR)
                sp.dma_start(xhD, pair[:]).then_inc(outs, 16)
                sp.wait_ge(w_c, len(jobs))
                for d_, s_ in ((whhD, whhT), (l0D, l0T), (l1D, l1T), (w12D, w12T)):
                    sp.dma_start(d_, s_[:].rearrange("p a b -> p (a b)")).then_inc(outs, 16)
                sp.wait_ge(outs, 16 * 6)

            @block.tensor
            def _(pe):
                pe.wait_ge(made, 9)
                n = [0]

                def bank():
                    i = n[0]
                    if i >= 6:
                        pe.wait_ge(w_c, i - 5)
                    n[0] += 1
                    return PS[i % 6]
                pe.wait_ge(loaded, 16 * 9)
                for nat, tr, b, a, m in jobs:
                    ps = bank()
                    for q in range(m):
                        last = nc.tensor.transpose(ps[:, q * 128:(q + 1) * 128], nat[:, a + q, b * 128:(b + 1) * 128], ident[:])
                    last.then_inc(w_t, 1)
                pe.wait_ge(dve_did, ABC)
                pe.wait_ge(w_c, len(jobs))
                for h in range(2):
                    last = nc.tensor.matmul(PS[0][0:P, h * 128:(h + 1) * 128], abc[:, h, :], aWT[:, 0, :], start=True, stop=True)
                last.then_inc(u_t, 1)
                pe.wait_ge(dve_did, EDGES)
                pe.wait_ge(dve_did, CS)
                for g in range(EG):
                    if g:
                        pe.wait_ge(edge_c, g)
                    for q, a in enumerate((cs[:, g, 0], cs[:, g, 1], key[:, g], we[:, g])):
                        last = nc.tensor.transpose(PS[6][:, q * 128:(q + 1) * 128], a, ident[:])
                    last.then_inc(edge_t, 1)
                pe.wait_ge(u_t, 1)
                for l in range(GL):
                    for kt in range(2):
                        for h in range(2):
                            i = (l * 2 + kt) * 2 + h
                            if i >= 4:
                                pe.wait_ge(v_c, i - 3)
                            for mt in range(2):
                                last = nc.tensor.matmul(PS[1 + i % 4][:, 0:HALF],
                                                        gWT[:, mt, l * S2 + kt * 128:l * S2 + (kt + 1) * 128],
                                                        wihT[:, mt, h * HALF:(h + 1) * HALF], start=(mt == 0), stop=(mt == 1))
                            last.then_inc(v_t, 1)
                pe.wait_ge(dve_did, LESS)
                for b in range(SB):
                    if b >= 2:
                        pe.wait_ge(gath_c, b - 1)
                    else:
                        pe.wait_ge(edge_c, EG)
                    for q in range(2):
                        last = nc.tensor.transpose(PS[6 + b % 2][:, q * 128:(q + 1) * 128], gath[:, b, q], ident[:])
                    last.then_inc(gath_t, 1)

            @block.scalar
            def _(act):
                act.dma_start(aWN[:, 0, :], aW).then_inc(loaded, 16)
                act.dma_start(wihN[:], wih.rearrange("(a p) m -> p a m", p=128)).then_inc(loaded, 16)
                act.dma_start(gWN[:], gW.rearrange("l (a p) m -> p (l a) m", p=128)).then_inc(loaded, 16)
                act.dma_start(whhN[:], whh.rearrange("(a p) m -> p a m", p=128)).then_inc(loaded, 16)
                act.dma_start(l0N[:], l0w.rearrange("(a p) m -> p a m", p=128)).then_inc(loaded, 16)
                act.dma_start(l1N[:, 0, :], l1w).then_inc(loaded, 16)
                act.dma_start(w12N[:, 0, :], w1).then_inc(loaded, 16)
                act.dma_start(w12N[:, 1, :], w2).then_inc(loaded, 16)
                act.dma_start(acol[:], aA.rearrange("(h p) o -> p (h o)", p=128), allow_slow_non_contiguous=True).then_inc(loaded, 16)
                act.dma_start(xn[:], x.rearrange("(k p) d -> p k d", p=P)).then_inc(x_in, 16)
                for i, (nat, tr, b, a, m) in enumerate(jobs):
                    act.wait_ge(w_t, i + 1)
                    nc.scalar.copy(tr[:, b, a * 128:(a + m) * 128], PS[i % 6][:, 0:m * 128]).then_inc(w_c, 1)
                act.wait_ge(dve_did, VAR)
                act.wait_ge(made, 1)
                nc.scalar.activation(st[:, 1, :], st[:, 0, :], ACT.Sqrt, bias=eps[0:P, :], scale=1.0 / D).then_inc(root_r, 1)
                for i in range(4 * GL):
                    l, j = i // 4, i % 4
                    act.wait_ge(v_t, i + 1)
                    if l >= 2 and j == 0:
                        act.wait_ge(v_st, 16 * (l - 1))
                    nc.scalar.copy(V[:, l % 2, (j // 2) * GATES + (j % 2) * HALF:(j // 2) * GATES + (j % 2 + 1) * HALF],
                                   PS[1 + i % 4][:, 0:HALF]).then_inc(v_c, 1)
                    if j == 3:
                        act.wait_ge(v_c, i + 1)
                        if l:
                            act.wait_ge(v_st, 16 * l)
                        act.dma_start(VD[l], V[:, l % 2, :]).then_inc(v_st, 16)
                act.wait_ge(v_st, 16 * GL)

            @block.vector
            def _(dve):
                n = [0]

                def done(ins):
                    n[0] += 1
                    ins.then_inc(chain, 1)
                    dve.wait_ge(chain, n[0])
                V_ = nc.vector
                dve.wait_ge(loaded, 16 * 9)
                last = V_.tensor_copy(abc[:], acol[:, :, None].to_broadcast([128, 2, P]))
                last.then_inc(dve_did, 1)
                dve.wait_ge(eloaded, 16 * edge_dmas)
                done(V_.tensor_copy(ef[:], ei[:]))
                V_.scalar_tensor_tensor(key[:], ef[:, 0], float(N), ef[:, 1], ALU.mult, ALU.add).then_inc(dve_did, 1)
                dve.wait_ge(dve_did, EDGES)
                done(V_.tensor_scalar(part[:], ef[:, 0], -float(P // 2), 1.0 / P, ALU.add, ALU.mult))
                done(V_.tensor_scalar(part[:], part[:], ROUND, None, ALU.add))
                done(V_.tensor_scalar(part[:], part[:], -ROUND, None, ALU.add))
                V_.scalar_tensor_tensor(cs[:, :, 0, :], ef[:, 1], float(T), part[:], ALU.mult, ALU.add)
                V_.scalar_tensor_tensor(cs[:, :, 1, :], part[:], -float(P), ef[:, 0], ALU.mult, ALU.add).then_inc(dve_did, 1)
                done(V_.tensor_scalar(near[:], ef[:, 1], 0.0, 1e5, ALU.is_lt, ALU.mult))
                done(V_.tensor_tensor(near[:], near[:], ef[:, 1], ALU.add))
                V_.tensor_reduce(dmin[:], near[:], X, ALU.min)
                done(V_.tensor_reduce(dmax[:], ef[:, 1], X, ALU.max))
                done(V_.tensor_scalar(dmin[:], dmin[:], -float(WIN - 1), None, ALU.add))
                dve.wait_ge(made, 9)
                for g in range(EG):
                    done(V_.tensor_scalar(over[:, g, 1, :], base[:], dmax[:, g:g + 1], None, ALU.is_le))
                    done(V_.scalar_tensor_tensor(over[:, g, 0, :], base[:], dmin[:, g:g + 1], over[:, g, 1, :], ALU.is_ge, ALU.mult))
                    done(V_.tensor_scalar(over[:, g, 1, :], over[:, g, 0, :], tile_no[:, g:g + 1], None, ALU.mult))
                    V_.tensor_tensor(over[:, g, 2, :], over[:, g, 1, :], over[:, g, 0, :], ALU.add)
                    done(V_.scalar_tensor_tensor(over[:, g, 1, :], over[:, g, 0, :], -FAR, over[:, g, 1, :], ALU.mult, ALU.add))
                for g in range(1, EG):
                    a = (cand[:, 0, :], cand[:, 1, :]) if g > 1 else (over[:, 0, 1, :], over[:, 0, 2, :])
                    V_.tensor_tensor(cand[:, 0, :], a[0], over[:, g, 1, :], ALU.min)
                    done(V_.tensor_tensor(cand[:, 1, :], a[1], over[:, g, 2, :], ALU.max))
                V_.tensor_scalar(cand[:, 0, :], cand[:, 0, :], -1.0, None, ALU.mult).then_inc(dve_did, 1)
                dve.wait_ge(red_r, 1)
                V_.memset(nil[:], 0.0)
                done(V_.memset(start[:], 0.0))
                done(V_.tensor_scalar(start[:, 0:NW], red[:, 0, :], -1.0, FAR, ALU.mult, ALU.add))
                done(V_.tensor_scalar(start[:, 0:NW], start[:, 0:NW], float(ET - 1), None, ALU.min))
                done(V_.tensor_scalar(hit[:], near4[:], 0.0, None, ALU.is_ge))
                done(V_.scalar_tensor_tensor(hit[:], near4[:], 3.0, hit[:], ALU.is_le, ALU.mult))
                done(V_.tensor_tensor(near4[:], near4[:], hit[:], ALU.mult))
                done(V_.tensor_reduce(place[:], near4[:], X, ALU.add))
                done(V_.tensor_tensor(picked[:], start[:].rearrange("p (b j) -> p b j", j=32),
                                      hit[:, None, :].to_broadcast([128, SB, 32]), ALU.mult))
                done(V_.tensor_reduce(tile[:], picked[:], X, ALU.add))
                done(V_.tensor_scalar(tile[:], tile[:], place[:], None, ALU.add))
                V_.tensor_copy(tilei[:], tile[:]).then_inc(dve_did, 1)
                done(V_.tensor_scalar(place[:], place[:], -float(WC // 4), None, ALU.mult))
                done(V_.tensor_scalar(woff[:], woff[:], place[:], None, ALU.add))
                done(V_.tensor_scalar(vis[:, 0, :], start[0:1, 0:NW], float(SPAN), None, ALU.add))
                done(V_.tensor_tensor(vis[:, 1, :], red[0:1, 1, :], vis[:, 0, :], ALU.subtract))
                done(V_.scalar_tensor_tensor(vis[:, 2, :], vis[:, 1, :], 0.0, wno[:], ALU.is_gt, ALU.mult))
                done(V_.tensor_reduce(top[:], vis[:, 2, 0:NW - 1], X, ALU.max))
                done(V_.tensor_scalar(top[:], top[:], 1.0, None, ALU.max))
                done(V_.tensor_scalar(vis[:, 2, :], wno[:], top[:], None, ALU.is_le))
                done(V_.memset(vis[:, 2, NW - 1:NW], 1.0))
                done(V_.scalar_tensor_tensor(vis[:, 2, :], vis[:, 1, :], 1.0, vis[:, 2, :], ALU.max, ALU.mult))
                done(V_.tensor_tensor_scan(vis[:, 3, :], vis[:, 2, :], nil[:], 0.0, ALU.add, ALU.add))
                done(V_.tensor_tensor(vis[:, 4, :], vis[:, 3, :], vis[:, 2, :], ALU.subtract))
                done(V_.scalar_tensor_tensor(vis[:, 5, :], vis[:, 0, :], RAISE, vis[:, 4, :], ALU.add, ALU.subtract))
                V_.tensor_copy(visits[:, 0, 0:NW], vis[:, 4, :])
                V_.tensor_copy(visits[:, 1, 0:NW], vis[:, 3, :])
                V_.tensor_copy(visits[:, 3, 0:1], top[:])
                done(V_.tensor_copy(visits[:, 2, 0:NW], vis[:, 5, :]))
                for g in range(EG):
                    dve.wait_ge(edge_t, g + 1)
                    V_.tensor_copy(ecol[:, :, g * LANE:(g + 1) * LANE], PS[6][:].rearrange("p (a t) -> p a t", a=4)).then_inc(edge_c, 1)
                dve.wait_ge(edge_c, EG)
                w = ecol[:, 3]
                V_.tensor_copy(wp[:, :, 3], rank[:].bitcast(f32).to_broadcast([128, EG * LANE]))
                left = [a[:].rearrange("p g e -> p (g e)") for a in (near, part)]
                for q in range(3):
                    done(V_.tensor_copy(wp[:, :, q], w))
                    if q < 2:
                        done(V_.tensor_tensor(left[q], w, wp[:, :, q], ALU.subtract))
                        w = left[q]
                dve.wait_ge(gathered, 16 * SB)
                V_.tensor_tensor(gath[:, :, 0, :], gath[:, :, 0, :], woff[:, :, None].to_broadcast([128, SB, LANE]), ALU.subtract).then_inc(dve_did, 1)
                dve.wait_ge(x_in, 16)
                bc = lambda a: a[:, :, None].to_broadcast([P, T, D])
                done(V_.tensor_reduce(st[:, 2, :], xn[:], X, ALU.add))
                done(V_.tensor_scalar(st[:, 3, :], st[:, 2, :], 1.0 / D, None, ALU.mult))
                done(V_.tensor_tensor(xn[:], xn[:], bc(st[:, 3, :]), ALU.subtract))
                done(V_.tensor_tensor(sq[:], xn[:], xn[:], ALU.mult))
                V_.tensor_reduce(st[:, 0, :], sq[:], X, ALU.add).then_inc(dve_did, 1)
                dve.wait_ge(root_r, 1)
                done(V_.reciprocal(st[:, 2, :], st[:, 1, :]))
                done(V_.tensor_scalar(st[:, 0, :], st[:, 0, :], 1.0 / D, EPS, ALU.mult, ALU.add))
                newton(V_, done, st[:, 2, :], st[:, 0, :], st[:, 1, :])
                done(V_.tensor_tensor(xn[:], xn[:], bc(st[:, 2, :]), ALU.mult))
                done(V_.tensor_scalar(sq[:], xn[:], 0.0, None, ALU.max))
                done(V_.tensor_scalar(xn[:], sq[:], UP, None, ALU.mult))
                done(V_.tensor_copy(pair[:, :, 0, :], xn[:]))
                V_.tensor_tensor(pair[:, :, 1, :], xn[:], pair[:, :, 0, :], ALU.subtract).then_inc(dve_did, 1)
                dve.wait_ge(dve_did, PAIR)
                dve.wait_ge(u_t, 1)
                done(V_.tensor_copy(uT[:].rearrange("p h d -> p (h d)"), PS[0][0:P, 0:256]))
                for h, to in enumerate((scol, tcol)):
                    done(V_.tensor_tensor(xn[:], sq[:], uT[:, h:h + 1, :].to_broadcast([P, T, D]), ALU.mult))
                    done(V_.tensor_reduce(to[:], xn[:], X, ALU.add))
                for b in range(SB):
                    dve.wait_ge(gath_t, b + 1)
                    V_.tensor_copy(wcol[:, :, b * LANE:(b + 1) * LANE],
                                   PS[6 + b % 2][:, 0:256].rearrange("p (a r) -> p a r", a=2)).then_inc(gath_c, 1)


def counts(nc, sem, PS, banks, A, edges, keyD, scatD, WT, colD, rowD):
    with ExitStack() as c:
        def sb(name, shape, dt=f32):
            return c.enter_context(nc.sbuf_tensor(name, shape, dt))

        comb, sib, keyc, wc, wp, rank, wcol, visits, tcol, scol, ident = (
            edges[n] for n in ("comb", "sib", "keyc", "wc", "wp", "rank", "wcol", "visits", "tcol", "scol", "ident"))
        pairs = sb("pairs", [128, WC], f16)
        nodes = sb("nodes", [128, P], f16)
        first = sb("first", [128, NW])
        OHP = SPAN * WC
        wide = sb("wide", [128, OHP + 2 * BATCH * LANE])
        ohp = wide[:, 0:OHP].bitcast(f16).rearrange("p (h s n) -> p h s n", h=2, s=SPAN)
        krow = wide[:, OHP:].rearrange("p (h q e) -> p h q e", h=2, q=BATCH)
        acc = wide[0:P, 0:N]
        ohs = sb("ohs", [128, 2, SPAN, P], f16)
        gap = sb("gap", [128, BATCH, LANE])
        eq = sb("eq", [128, 2, BATCH, LANE], bf16)
        kcol = sb("kcol", [128, 2, BATCH])
        onef = sb("onef", [128, 1])
        oneh = sb("oneh", [P, 1], f16)
        dump = sb("dump", [128, 1])
        identh = sb("identh0", [128, 128], f16)
        far = sb("far", [128, 1])
        nzb = sb("nz", [128, SC, CH], f16)
        nz = nzb[0:P]
        zero = nzb[:].rearrange("p b n -> p (b n)").bitcast(f32)[:, 0:ZN].rearrange("p (o z) -> p o z", o=1)
        col = sb("col", [P, 4, T])
        root = sb("root", [P, 3, T])
        top = sb("top", [P, 3, T])
        srows = sb("srows", [T, 2, P])
        thr = sb("thr", [128, 1])
        scat = wcol[:].rearrange("p a r -> p (a r)").bitcast(i32)[:, 0:NBATCH * 2 * BATCH].rearrange("p (b k q) -> p b k q", k=2, q=BATCH)
        names = ("set", "oh_made", "win_r", "win_out", "x_made", "x_prod", "x_added", "k0", "k1", "gap_r", "eq_r",
                 "eq_used", "tp_r", "nz_r", "acc_r", "acc_x", "root_r", "outs", "chain",
                 "kcol_r", "zeros", "tick", "dve_did", "pe_did")
        (set_, oh_made, win_r, win_out, x_made, x_prod, x_added, k0, k1, gap_r, eq_r,
         eq_used, tp_r, nz_r, acc_r, acc_x, root_r,
         outs, chain, kcol_r, zeros, tick, dve_did, pe_did) = (sem("w_" + n) for n in names)
        k_in = (k0, k1)
        SCAT, TOPS, DEGREES, COLS, ROWS = 2, 3, 4, 5, 6
        DEG_T, ROWS_T = 1, SC + 2
        W = [CH] * NC + [N - NC * CH]
        NSET = 9
        sums = banks[:, 4:8, :].rearrange("p b (t k) -> p (b t) k", k=4)
        assert NBATCH * BATCH <= 512
        LAST = N - (NW - 1) * WIN

        def windows(eng, window, merge=None, ahead=0):
            for b in range(ahead):
                merge(0, b)
            with eng.Fori(0, MERGE) as i:
                for j in range(STEP):
                    window(i * STEP + j, WIN, j)
                    if merge and j % 2:
                        b = j // 2 + ahead
                        merge(i + b // 2, b % 2)
            window(NW - 1, LAST, 0)
            if merge:
                for h in range(ahead, 2):
                    merge(MERGE, h)

        def rest(eng, window):
            end = eng.value_load(visits[0:1, 3, 0:1], min_val=1, max_val=NW - 1)
            with eng.Fori(0, end) as w:
                window(w, WIN)
            window(NW - 1, LAST)

        def span(eng, w):
            at = bass.ds(w, 1)
            return (eng.value_load(visits[0:1, 0, at], min_val=0, max_val=(ET + 3) * NW),
                    eng.value_load(visits[0:1, 1, at], min_val=1, max_val=(ET + 3) * NW))

        with nc.Block() as block:
            @block.gpsimd
            def _(pool):
                g = nc.gpsimd
                g.iota(pairs[:], [[1, WC]], base=0, channel_multiplier=0, allow_small_or_imprecise_dtypes=True).then_inc(set_, 1)
                g.iota(nodes[:], [[1, P]], base=0, channel_multiplier=0, allow_small_or_imprecise_dtypes=True).then_inc(set_, 1)
                g.iota(first[:], [[-WC, NW]], base=0, channel_multiplier=0, allow_small_or_imprecise_dtypes=True).then_inc(set_, 1)
                g.iota(dump[:], [[0, 1]], base=DUMP, channel_multiplier=1, allow_small_or_imprecise_dtypes=True).then_inc(set_, 1)
                g.memset(onef[:], 1.0).then_inc(set_, 1)
                g.memset(oneh[:], 1.0).then_inc(set_, 1)
                g.memset(zero, 0.0).then_inc(set_, 1)
                g.memset(far[:], BIG).then_inc(set_, 1)
                g.memset(identh[:], 0.0).then_inc(set_, 1)
                pool.wait_ge(set_, NSET)
                g.affine_select(out=identh[:], in_=identh[:], compare_op=ALU.not_equal, fill=1.0,
                                base=0, pattern=[[-1, 128]], channel_multiplier=1).then_inc(set_, 1)
                pool.wait_ge(set_, NSET + 1)

            @block.sync
            def _(sp):
                sp.wait_ge(set_, NSET)
                def keys(b, h):
                    sp.wait_ge(gap_r, b + 1)
                    rows = keyD[bass.ds(b * BATCH, BATCH), :].rearrange("(o t) e -> o (t e)", o=1)
                    sp.dma_start(krow[:, h].rearrange("p t e -> p (t e)"), rows.to_broadcast([128, BATCH * LANE])).then_inc(k_in[h], 16)
                with sp.Fori(0, MERGE) as i:
                    for h in range(2):
                        keys(2 * i + h, h)
                    sp.dma_start(WT[bass.ds(i * (LANE * ZW), LANE * ZW), :].rearrange("(p a w) o -> p a (w o)", p=LANE, w=ZN),
                                 zero.to_broadcast([128, ZW // ZN, ZN])).then_inc(zeros, 16)
                for h in range(2):
                    keys(2 * MERGE + h, h)
                sp.wait_ge(dve_did, SCAT)
                sp.dma_start(scatD.rearrange("b p c -> p b c"), scat.rearrange("p b k q -> p b (k q)")).then_inc(outs, 16)
                sp.wait_ge(dve_did, COLS)
                sp.dma_start(colD, col[:].rearrange("p a t -> p (a t)")).then_inc(outs, 16)
                sp.wait_ge(dve_did, ROWS)
                sp.dma_start(rowD.rearrange("h (k p) -> k h p", p=P), srows[:]).then_inc(outs, 16)
                sp.wait_ge(outs, 48)
                sp.wait_ge(zeros, 16 * ZF)

            @block.vector
            def _(dve):
                V_ = nc.vector
                dve.wait_ge(set_, NSET + 1)

                def window(w, n, j):
                    dve.wait_ge(win_r, w + 1)
                    V_.tensor_tensor(ohs[:, j % 2], nodes[:, None, :].to_broadcast([128, SPAN, P]),
                                     wcol[:, 1, bass.ds(w * SPAN, SPAN)][:, :, None].to_broadcast([128, SPAN, P]), ALU.is_equal)
                    for k in range(SPAN):
                        last = V_.tensor_scalar(ohp[:, j % 2, k], pairs[:], wcol[:, 0, bass.ds(w * SPAN + k, 1)], None, ALU.is_equal)
                    last.then_inc(oh_made, 1)
                windows(dve, window)

                dve.wait_ge(win_out, NW + 4)
                dve.wait_ge(win_r, NW + 2)

                def more(w, n):
                    v0, v1 = span(dve, w)
                    off = dve.value_load(visits[0:1, 2, bass.ds(w, 1)], min_val=0, max_val=ET + SPAN + int(RAISE))
                    with dve.Fori(v0, v1) as v:
                        t = nc.s_assert_within(v + off - int(RAISE), 0, EG * LANE - 1, skip_runtime_bounds_check_because=
                                               "the table of visits keeps to the edge tiles")
                        V_.tensor_scalar(ohs[:, 0, 0], nodes[:], sib[:, bass.ds(t, 1)], None, ALU.is_equal)
                        V_.tensor_scalar(ohp[:, 0, 0], pairs[:], first[:, bass.ds(w, 1)], comb[:, bass.ds(t, 1)],
                                         ALU.subtract, ALU.is_equal).then_inc(x_made, 1)
                        dve.wait_ge(x_prod, v + 1)
                        dve.sem_inc(tick, 1)
                        part = A[:, :, bass.ds(w * WIN, n)]
                        V_.tensor_tensor(part, part, PS[0][0:P, 0:n * T].rearrange("p (n a) -> p a n", a=T), ALU.add).then_inc(x_added, 1)
                        dve.wait_ge(x_added, v + 1)
                rest(dve, more)
                n = [0]

                def done(ins):
                    n[0] += 1
                    ins.then_inc(chain, 1)
                    dve.wait_ge(chain, n[0])
                nt = NBATCH * BATCH
                dve.wait_ge(eq_used, NBATCH + 2)
                bq = lambda a: a.rearrange("p (b q) -> p b q", q=BATCH)
                V_.tensor_reduce(scat[:, :, 1, :].bitcast(f32), sums[:, 0:nt, 0:3].rearrange("p (b q) k -> p b q k", q=BATCH),
                                 X, ALU.add).then_inc(dve_did, 1)
                done(V_.tensor_scalar(thr[:], rank[:].bitcast(f32), 2.5, None, ALU.mult))
                done(V_.tensor_scalar(wc[:, 0:nt], keyc[:, 0:nt], dump[:], -1.0, ALU.subtract, ALU.mult))
                done(V_.scalar_tensor_tensor(wc[:, 0:nt], sums[:, 0:nt, 3], thr[:], wc[:, 0:nt], ALU.is_gt, ALU.mult))
                V_.tensor_tensor(scat[:, :, 0, :], bq(wc[:, 0:nt]), bq(keyc[:, 0:nt]), ALU.add).then_inc(dve_did, 1)
                dve.wait_ge(dve_did, SCAT)
                V_.memset(acc, 1e30).then_inc(acc_r, SC)
                with dve.Fori(0, T) as j:
                    for b in range(SC):
                        part = acc[:, b * CH:b * CH + W[b]]
                        dve.wait_ge(nz_r, SC * j + b + 1 + SC)
                        dve.wait_ge(acc_r, SC * j + b + 1)
                        V_.scalar_tensor_tensor(part, nz[:, b, 0:W[b]], tcol[:, bass.ds(j, 1)], part, ALU.subtract, ALU.min).then_inc(acc_r, 1)
                for b in range(SC):
                    dve.wait_ge(pe_did, 1 + b + 1)
                    k = W[b] // P
                    V_.tensor_reduce(top[:, 0, b * NQ:b * NQ + k], PS[b][0:P, 0:W[b]].rearrange("p (k q) -> p k q", k=k), X, ALU.min).then_inc(acc_x, 1)
                dve.wait_ge(acc_x, SC)
                done(V_.tensor_tensor(top[:, 1, :], scol[:], top[:, 0, :], ALU.subtract))
                done(V_.scalar_tensor_tensor(top[:, 2, :], top[:, 1, :], ALPHA, top[:, 1, :], ALU.mult, ALU.max))
                V_.tensor_tensor(top[:, 0, :], scol[:], top[:, 2, :], ALU.subtract)
                done(V_.scalar_tensor_tensor(top[:, 1, :], scol[:], ALPHA, top[:, 2, :], ALU.mult, ALU.subtract))
                V_.tensor_copy(col[:, 0, :], tcol[:]).then_inc(dve_did, 1)
                V_.tensor_scalar(col[:, 1, :], tcol[:], ALPHA, None, ALU.mult)
                dve.wait_ge(pe_did, DEG_T)
                done(V_.tensor_scalar(root[:, 0, :], PS[7][0:P, 0:T], 1.0, None, ALU.add))
                V_.tensor_copy(root[:, 1, :], root[:, 0, :]).then_inc(dve_did, 1)
                dve.wait_ge(root_r, 1)
                done(V_.reciprocal(root[:, 2, :], root[:, 1, :]))
                newton(V_, done, root[:, 2, :], root[:, 0, :], root[:, 1, :])
                V_.tensor_scalar(col[:, 3, :], root[:, 2, :], UP, None, ALU.mult)
                V_.tensor_copy(col[:, 2, :], root[:, 2, :]).then_inc(dve_did, 1)
                dve.wait_ge(pe_did, ROWS_T)
                V_.tensor_copy(srows[:], PS[0][0:T, 0:256].rearrange("p (h c) -> p h c", h=2)[:, :, 0:P]).then_inc(dve_did, 1)

            @block.scalar
            def _(act):
                act.wait_ge(set_, NSET + 1)
                act.sem_inc(win_out, 4)
                act.sem_inc(nz_r, SC)
                act.sem_inc(gap_r, 2)

                def window(w, n, j):
                    act.wait_ge(win_r, w + 3)
                    nc.scalar.copy(A[:, :, bass.ds(w * WIN, n)], PS[j][0:P, 0:n * T].rearrange("p (n a) -> p a n", a=T)).then_inc(win_out, 1)

                def merge(i, h):
                    b = 2 * i + h
                    nc.scalar.copy(kcol[:, h, :], keyc[:, bass.ds(b * BATCH, BATCH)]).then_inc(kcol_r, 1)
                    act.wait_ge(k_in[h], 16 * i + 16)
                    act.wait_ge(kcol_r, b + 1)
                    act.sem_inc(tick, 1)
                    for q in range(BATCH):
                        last = nc.scalar.activation(gap[:, q], krow[:, h, q], ACT.Square, bias=kcol[:, h, q:q + 1], scale=-1.0)
                    last.then_inc(gap_r, 1)
                    act.wait_ge(gap_r, b + 3)
                    act.wait_ge(eq_used, b + 1)
                    nc.scalar.activation(eq[:, h], gap[:], ACT.Relu, bias=onef[:], scale=-2.0).then_inc(eq_r, 1)
                windows(act, window, merge, ahead=1)
                act.wait_ge(zeros, 16 * ZF)
                with act.Fori(0, T) as j:
                    for b in range(SC):
                        act.wait_ge(tp_r, SC * j + b + 1)
                        act.wait_ge(acc_r, SC * j + b + 1)
                        nc.scalar.activation(nz[:, b, 0:W[b]], PS[b][0:P, 0:W[b]], ACT.Relu, scale=-BIG, bias=far[0:P, :]).then_inc(nz_r, 1)
                act.wait_ge(dve_did, DEGREES)
                nc.scalar.activation(root[:, 1, :], root[:, 1, :], ACT.Sqrt).then_inc(root_r, 1)

            @block.tensor
            def _(pe):
                pe.sem_inc(win_r, 2)
                pe.sem_inc(eq_used, 2)
                pe.wait_ge(set_, NSET + 1)

                def window(w, n, j):
                    pe.wait_ge(win_out, w + 1)
                    pe.wait_ge(oh_made, w + 1)
                    for k in range(SPAN):
                        last = nc.tensor.matmul(PS[j][0:P, 0:WC], ohs[:, j % 2, k], ohp[:, j % 2, k], start=(k == 0), stop=(k == SPAN - 1))
                    last.then_inc(win_r, 1)

                def merge(i, h):
                    b = 2 * i + h
                    pe.wait_ge(eq_r, b + 1)
                    for q in range(BATCH):
                        t = bass.ds(b * BATCH + q, 1)
                        last = nc.tensor.matmul(sums[:, t, :].rearrange("p o k -> p (o k)"), eq[:, h, q], wp[:, t, :].rearrange("p o k -> p (o k)"),
                                                start=True, stop=True)
                    last.then_inc(eq_used, 1)
                windows(pe, window, merge)

                def more(w, n):
                    v0, v1 = span(pe, w)
                    with pe.Fori(v0, v1) as v:
                        pe.wait_ge(x_made, v + 1)
                        nc.tensor.matmul(PS[0][0:P, 0:WC], ohs[:, 0, 0], ohp[:, 0, 0], start=True, stop=True).then_inc(x_prod, 1)
                rest(pe, more)
                pe.wait_ge(dve_did, SCAT)
                with pe.Fori(0, T) as j:
                    for b in range(SC):
                        pe.wait_ge(nz_r, SC * j + b + 1)
                        for q in range(W[b] // P):
                            a = b * NQ + q
                            tile = A[:, a, bass.ds(j * P, P)]
                            nc.tensor.matmul(PS[7][0:P, bass.ds(j, 1)], tile, oneh[:], start=(a == 0), stop=(a == T - 1))
                            last = nc.tensor.matmul(PS[b][0:P, q * P:(q + 1) * P], tile, identh[0:P, 0:P], start=True, stop=True)
                        last.then_inc(tp_r, 1)
                pe.sem_inc(pe_did, 1)
                pe.wait_ge(acc_r, SC * T + SC)
                for b in range(SC):
                    for k in range(W[b] // P):
                        last = nc.tensor.transpose(PS[b][0:P, k * P:(k + 1) * P], acc[:, b * CH + k * P:b * CH + (k + 1) * P], ident[0:P, 0:P])
                    last.then_inc(pe_did, 1)
                pe.wait_ge(dve_did, TOPS)
                for h in range(2):
                    last = nc.tensor.transpose(PS[0][0:T, h * 128:h * 128 + P], top[:, h, :], ident[0:P, 0:P])
                last.then_inc(pe_did, 1)


class Done:

    def __init__(self, eng, sem):
        self.eng, self.sem, self.n = eng, sem, 0

    def __call__(self, ins, start=None):
        self.n += 1
        ins.then_inc(self.sem, 1)
        self.eng.wait_ge(self.sem, self.n if start is None else start + self.n)


def scatter(nc, pool, sems, scat, scatD, WT, first, end):
    got, added, landed = sems
    with pool.Fori(first, end) as b:
        pool.dma_start(scat[:], scatD[bass.ds(b, 1)].rearrange("o p c -> (o p) c")).then_inc(got, 16)
        pool.wait_ge(got, 16 * b + 16)
        pool.sem_inc(landed, 1)
        for q in range(BATCH):
            nc.gpsimd.indirect_dma_start(out=WT, out_offset=bass.IndirectOffsetOnAxis(ap=scat[:, q:q + 1], axis=0),
                                         in_=scat[:, BATCH + q:BATCH + q + 1].bitcast(f32), in_offset=None,
                                         compute_op=ALU.add).then_inc(added, 16)
            pool.wait_ge(added, 16 * (BATCH * b + q + 1))
            pool.sem_inc(landed, 1)


def layers(nc, sem, PS, big, A, x, aW, cW, cB, bih, bhh, l0b, l1b, b1, b2, out, WT, scatD, VD, whhD, l0D, l1D, w12D,
           rowD, xhD, xh1D, x1D, x2D, colD, hnD, hTD, xhTD):
    with ExitStack() as c:
        def sb(name, shape, dt=f32):
            return c.enter_context(nc.sbuf_tensor(name, shape, dt))

        ident = sb("identf", [128, 128])
        identh = sb("identh", [128, 128], f16)
        col = sb("cols", [P, 4, T])
        scat = sb("scatp", [128, 2 * BATCH], i32)
        scat_sems = [sem("scat_" + n) for n in ("got", "added", "landed")]
        attention(nc, sem, PS, x, aW, rowD, xhD, xh1D, x1D, colD, A, ident, identh, col)
        convolutions(nc, sem, PS, cW, cB, scat, scat_sems, scatD, WT, xh1D, x1D, x2D, hnD, hTD, xhTD, A, ident, identh, col)
        gru(nc, sem, PS, bih, bhh, scat, scat_sems, scatD, WT, VD, whhD, hnD, hTD, A, ident)
    tail(nc, sem, PS, big, l0b, l1b, b1, b2, out, WT, l0D, l1D, w12D, x2D, hTD, xhTD)


def norm(V_, done, mid, y, xc, sq, st, relu_to):
    q = y.shape[1]
    bc = lambda a: a[:, :, None].to_broadcast([P, q, D])
    done(V_.tensor_reduce(st[:, 0, :], y, X, ALU.add))
    done(V_.tensor_scalar(st[:, 1, :], st[:, 0, :], 1.0 / D, None, ALU.mult))
    done(V_.tensor_tensor(xc, y, bc(st[:, 1, :]), ALU.subtract))
    done(V_.tensor_tensor(sq, xc, xc, ALU.mult))
    done(V_.tensor_reduce(st[:, 0, :], sq, X, ALU.add))
    mid(V_.tensor_scalar(st[:, 2, :], st[:, 0, :], 1.0 / D, EPS, ALU.mult, ALU.add))
    done(V_.reciprocal(st[:, 0, :], st[:, 3, :]))
    newton(V_, done, st[:, 0, :], st[:, 2, :], st[:, 3, :])
    if relu_to is None:
        done(V_.tensor_tensor(xc, xc, bc(st[:, 0, :]), ALU.mult))
    else:
        done(V_.tensor_tensor(xc, xc, bc(st[:, 0, :]), ALU.mult))
        done(V_.tensor_scalar(relu_to, xc, 0.0, None, ALU.max))


def attention(nc, sem, PS, x, aW, rowD, xhD, xh1D, x1D, colD, A, ident, identh, col):
    with ExitStack() as c:
        def sb(name, shape, dt=f32):
            return c.enter_context(nc.sbuf_tensor(name, shape, dt))

        UN = 5
        xh = sb("xh", [P, T, 2, D], f16)
        sr = sb("sr", [P, 2, CH])
        z = sb("z", [P, UN, CH])
        ph = sb("ph", [P, 3, 2, CH], f16)
        inv = sb("inv", [128, CH])
        hT = sb("hT", [128, CH])
        xin = sb("xin", [P, NQ, D])
        ya = sb("ya", [P, NQ, D])
        yb = sb("yb", [P, NQ, D])
        st = sb("sta", [P, 4, NQ])
        W = sb("aWs", [128, D])
        ones = sb("ones", [P, 128], f16)
        names = ("made", "loaded", "sr_in", "sr_free", "a_r", "z_r", "e_r", "p_r", "ph_r", "pl_r", "cell_r", "tr_r",
                 "sum_r", "hT_r", "out_r", "exp_r", "var_r", "root_r", "x_in", "x_out", "y_r", "chain", "sum_free")
        (made, loaded, sr_in, sr_free, a_r, z_r, e_r, p_r, ph_r, pl_r, cell_r, tr_r,
         sum_r, hT_r, out_r, exp_r, var_r, root_r, x_in, x_out, y_r, chain, sum_free) = (sem("a0_" + n) for n in names)
        xt = x.rearrange("(k p) d -> p k d", p=P)

        def chunks(eng, body):
            with eng.Fori(0, NC) as ch:
                body(ch, CH)
            body(NC, P)

        def cells(eng, ch, stages, lag):
            def step(g, i, first, upto=None):
                for n, stage in enumerate(stages):
                    if not (first and i < n) and (upto is None or upto <= n):
                        k = i - n
                        stage(ch * T + g * UN + k, g * UN + k, k % UN, g if k >= 0 else g - 1)
            for i in range(UN):
                step(0, i, True)
            with eng.Fori(1, T // UN) as g:
                for i in range(UN):
                    step(g, i, False)
            for n in range(1, lag + 1):
                for m in range(n, lag + 1):
                    k = UN - 1 + n - m
                    stages[m](ch * T + T - UN + k, T - UN + k, k, T // UN - 1)

        with nc.Block() as block:
            @block.sync
            def _(sp):
                sp.dma_start(xh[:], xhD).then_inc(loaded, 16)
                sp.dma_start(col[:], colD.rearrange("p (a t) -> p a t", a=4)).then_inc(loaded, 16)
                sp.dma_start(W[:], aW).then_inc(loaded, 16)

                def body(ch, w):
                    k = w // P
                    sp.wait_ge(sr_free, 2 * ch + 2)
                    sp.dma_start(sr[:, :, 0:w], rowD[:, bass.ds(ch * CH, w)].rearrange("(o h) n -> o h n", o=1).to_broadcast([P, 2, w])).then_inc(sr_in, 16)
                    sp.wait_ge(x_in, 16 * ch + 16)
                    sp.wait_ge(x_out, 32 * ch + 32)
                    sp.dma_start(xin[:, 0:k, :], xt[:, bass.ds(ch * NQ, k), :]).then_inc(x_in, 16)
                    sp.wait_ge(y_r, 2 * ch + 1)
                    sp.dma_start(x1D[:, bass.ds(ch * NQ, k), :], ya[:, 0:k, :]).then_inc(x_out, 16)
                    sp.wait_ge(y_r, 2 * ch + 2)
                    sp.dma_start(xh1D[:, bass.ds(ch * NQ, k), :], yb[:, 0:k, :]).then_inc(x_out, 16)
                sp.sem_inc(x_in, 16)
                sp.sem_inc(x_out, 32)
                chunks(sp, body)
                sp.wait_ge(x_out, 32 * (NC + 1) + 32)

            @block.gpsimd
            def _(pool):
                nc.gpsimd.memset(ones[:], 1.0).then_inc(made, 1)
                nc.gpsimd.memset(ident[:], 0.0).then_inc(made, 1)
                nc.gpsimd.memset(identh[:], 0.0).then_inc(made, 1)
                pool.wait_ge(made, 3)
                for m in (ident, identh):
                    nc.gpsimd.affine_select(out=m[:], in_=m[:], compare_op=ALU.not_equal, fill=1.0,
                                            base=0, pattern=[[-1, 128]], channel_multiplier=1).then_inc(made, 1)
                pool.sem_inc(pl_r, UN)

                def body(ch, w):
                    def low(m, j, i, g):
                        pool.wait_ge(ph_r, m + 1)
                        nc.gpsimd.tensor_tensor(ph[:, i % 3, 1, 0:w], z[:, i, 0:w], ph[:, i % 3, 0, 0:w], ALU.subtract).then_inc(pl_r, 1)
                    cells(pool, ch, [low], 0)
                chunks(pool, body)

            @block.scalar
            def _(act):
                act.wait_ge(loaded, 48)

                def body(ch, w):
                    k = w // P
                    act.wait_ge(sr_in, 16 * ch + 16)

                    def lift(m, j, i, g):
                        act.wait_ge(pl_r, m + 1)
                        nc.scalar.activation(z[:, i, 0:w], sr[:, 1, 0:w], ACT.Identity, bias=col[:, 1, bass.ds(j, 1)]).then_inc(a_r, 1)

                    def expo(m, j, i, g):
                        act.wait_ge(z_r, m + 1)
                        nc.scalar.activation(z[:, i, 0:w], z[:, i, 0:w], ACT.Exp).then_inc(e_r, 1)

                    def high(m, j, i, g):
                        act.wait_ge(p_r, m + 1 + 2 * UN)
                        act.wait_ge(cell_r, m - 1 + 2 * UN)
                        nc.scalar.copy(ph[:, i % 3, 0, 0:w], z[:, i, 0:w]).then_inc(ph_r, 1)
                    cells(act, ch, [lift, expo, high], 2)
                    act.sem_inc(sr_free, 1)
                    act.wait_ge(out_r, ch + 1)
                    nc.scalar.activation(yb[:, 0:k, :].rearrange("p k d -> p (k d)"), PS[5][0:P, 0:k * D], ACT.Exp).then_inc(exp_r, 1)
                    act.wait_ge(var_r, ch + 1)
                    nc.scalar.activation(st[:, 3, 0:k], st[:, 2, 0:k], ACT.Sqrt).then_inc(root_r, 1)
                chunks(act, body)

            @block.tensor
            def _(pe):
                pe.wait_ge(made, 5)
                pe.wait_ge(loaded, 48)
                pe.sem_inc(cell_r, 2 * UN)

                def body(ch, w):
                    k = w // P
                    pe.wait_ge(sum_free, ch + 1)

                    def turn(m, j, i, g):
                        pe.wait_ge(p_r, m - 1 + 2 * UN)
                        for q in range(k):
                            last = nc.tensor.matmul(PS[2 + i % 3][0:P, q * P:(q + 1) * P],
                                                    A[:, bass.ds(ch * NQ + q, 1), bass.ds(j * P, P)].rearrange("p o n -> p (o n)"),
                                                    identh[0:P, 0:P], start=True, stop=True)
                        last.then_inc(tr_r, 1)

                    def idle(m, j, i, g):
                        pass

                    def cell(m, j, i, g):
                        start, stop = (isinstance(j, int) and j == n for n in (0, T - 1))
                        hi, lo = ph[:, i % 3, 0, 0:w], ph[:, i % 3, 1, 0:w]
                        xhi = xh[:, bass.ds(j, 1), 0, :].rearrange("p o d -> p (o d)")
                        xlo = xh[:, bass.ds(j, 1), 1, :].rearrange("p o d -> p (o d)")
                        pe.wait_ge(ph_r, m + 1)
                        nc.tensor.matmul(PS[0][:, 0:w], xhi, hi, start=start, stop=False)
                        nc.tensor.matmul(PS[0][:, 0:w], xlo, hi, start=False, stop=False)
                        nc.tensor.matmul(PS[1][:, 0:w], ones[:], hi, start=start, stop=False)
                        pe.wait_ge(pl_r, m + 1 + UN)
                        nc.tensor.matmul(PS[0][:, 0:w], xhi, lo, start=False, stop=stop)
                        nc.tensor.matmul(PS[1][:, 0:w], ones[:], lo, start=False, stop=stop).then_inc(cell_r, 1)
                    cells(pe, ch, [turn, idle, cell], 2)
                    pe.wait_ge(hT_r, ch + 1)
                    for q in range(k):
                        last = nc.tensor.matmul(PS[5][0:P, q * D:(q + 1) * D], hT[:, q * P:(q + 1) * P], W[:], start=True, stop=True)
                    last.then_inc(out_r, 1)
                chunks(pe, body)

            @block.vector
            def _(dve):
                V_ = nc.vector
                dve.wait_ge(loaded, 48)
                dve.sem_inc(sr_free, 2)
                dve.sem_inc(p_r, 2 * UN)
                dve.sem_inc(sum_free, 1)

                def body(ch, w):
                    k = w // P
                    dve.wait_ge(sr_in, 16 * ch + 16)

                    def logit(m, j, i, g):
                        dve.wait_ge(a_r, m + 1)
                        V_.scalar_tensor_tensor(z[:, i, 0:w], sr[:, 0, 0:w], col[:, 0, bass.ds(j, 1)], z[:, i, 0:w], ALU.add, ALU.max).then_inc(z_r, 1)

                    def weigh(m, j, i, g):
                        dve.wait_ge(e_r, m + 1)
                        dve.wait_ge(tr_r, m + 1)
                        V_.scalar_tensor_tensor(z[:, i, 0:w], z[:, i, 0:w], 1.0, PS[2 + i % 3][0:P, 0:w], ALU.min, ALU.mult).then_inc(p_r, 1)
                    cells(dve, ch, [logit, weigh], 1)
                    dve.sem_inc(sr_free, 1)
                    dve.wait_ge(cell_r, ch * T + T + 2 * UN)
                    K_ = 17
                    n0 = done.n

                    def dn(ins):
                        done.n += 1
                        ins.then_inc(chain, 1)
                        dve.wait_ge(chain, ch * K_ + done.n - n0)
                    dn(V_.tensor_scalar(inv[:, 0:w], PS[1][:, 0:w], 1e-8, None, ALU.max))
                    dn(V_.reciprocal(inv[:, 0:w], inv[:, 0:w]))
                    V_.scalar_tensor_tensor(hT[:, 0:w], PS[0][:, 0:w], 1.0 / UP, inv[:, 0:w], ALU.mult, ALU.mult).then_inc(hT_r, 1)
                    dve.wait_ge(hT_r, ch + 1)
                    dve.sem_inc(sum_free, 1)
                    o = PS[5][0:P, 0:k * D].rearrange("p (k d) -> p k d", d=D)
                    y, t = ya[:, 0:k, :], yb[:, 0:k, :]
                    dve.wait_ge(exp_r, ch + 1)
                    dn(V_.tensor_scalar(t, t, 1.0, -1.0, ALU.min, ALU.add))
                    dn(V_.scalar_tensor_tensor(t, o, 0.0, t, ALU.max, ALU.add))
                    dve.wait_ge(x_in, 16 * ch + 32)
                    dn(V_.tensor_tensor(y, t, xin[:, 0:k, :], ALU.add))
                    dve.sem_inc(y_r, 1)

                    def mid(ins):
                        ins.then_inc(var_r, 1)
                        dve.wait_ge(root_r, ch + 1)
                    norm(V_, dn, mid, y, t, xin[:, 0:k, :], st[:, :, 0:k], t)
                    dve.sem_inc(y_r, 1)
                    dve.wait_ge(x_out, 32 * ch + 64)
                    assert done.n - n0 == K_, done.n - n0
                done = Done(dve, chain)
                chunks(dve, body)


def convolutions(nc, sem, PS, cW, cB, scat, scat_sems, scatD, WT, xh1D, x1D, x2D, hnD, hTD, xhTD, A, ident, identh, col):
    with ExitStack() as c:
        def sb(name, shape, dt=f32):
            return c.enter_context(nc.sbuf_tensor(name, shape, dt))

        xr = sb("xr", [P, T, D])
        G = sb("G1", [P, 2, T, 2, D], f16)
        F = G[:].rearrange("p a t h d -> p (a t h d)").bitcast(f32).rearrange("p (a t d) -> p a t d", a=2, t=T)
        x2 = F[:, 1]
        assert CL % 2 == 1
        pair = xr[:].rearrange("p t d -> p (t d)").bitcast(f16).rearrange("p (t h d) -> p t h d", t=T, h=2)
        aT = sb("aT1", [128, CH])
        W = sb("cWs", [128, CL, D])
        bias = sb("cBs", [P, CL, D])
        ya = sb("y1a", [P, NQ, D])
        yb = sb("y1b", [P, NQ, D])
        yc = sb("y1c", [P, NQ, D])
        st = sb("st1", [P, 4, NQ])
        hs = sb("hs1", [128, 2, CH])
        zt = sb("zt1", [128, 1, P])
        names = ("loaded", "g_r", "agg_r", "aT_r", "o_r", "var_r", "root_r", "chain", "y_free", "x1_in", "x2_r",
                 "x2_out", "pair_r", "pair_out", "tr_r", "hs_r", "hs_out0", "hs_out1", "zset", "z_out", "var2", "root2", "chain2")
        (loaded, g_r, agg_r, aT_r, o_r, var_r, root_r, chain, y_free, x1_in, x2_r,
         x2_out, pair_r, pair_out, tr_r, hs_r, hs_out0, hs_out1, zset, z_out, var2, root2, chain2) = (sem("c_" + n) for n in names)
        hs_out = (hs_out0, hs_out1)

        def steps(eng, body):
            with eng.Fori(0, CL - 1) as l:
                with eng.Fori(0, NC) as ch:
                    body(l, ch, CH, l * SC + ch)
                body(l, NC, P, l * SC + NC)

        def last(eng, body, after):
            body(0, CH)
            with eng.Fori(0, NC // 2 - 1) as c:
                for q in range(2):
                    body(2 * c + q + 1, CH)
                    after(2 * c + q, CH, q, c)
            body(NC - 1, CH)
            after(NC - 2, CH, 0, NC // 2 - 1)
            body(NC, P)
            after(NC - 1, CH, 1, NC // 2 - 1)
            after(NC, P, 0, NC // 2)

        with nc.Block() as block:
            @block.gpsimd
            def _(pool):
                nc.gpsimd.memset(zt[:], 0.0).then_inc(zset, 1)
                scatter(nc, pool, scat_sems, scat, scatD, WT, 0, SPLIT)

            @block.sync
            def _(sp):
                sp.dma_start(xr[:], xh1D).then_inc(loaded, 16)
                sp.dma_start(W[:], cW.rearrange("l p d -> p l d")).then_inc(loaded, 16)
                sp.dma_start(bias[:], cB.rearrange("(o l) d -> o l d", o=1).to_broadcast([P, CL, D])).then_inc(loaded, 16)
                sp.wait_ge(zset, 1)
                sp.dma_start(hTD[:, 1, :].rearrange("p (t n) -> p t n", n=P), zt[:].to_broadcast([128, T, P])).then_inc(z_out, 16)
                sp.wait_ge(agg_r, (CL - 1) * SC)
                sp.dma_start(x2, x1D).then_inc(x1_in, 16)
                for s_, n in ((hs_out0, 32), (hs_out1, 32)):
                    sp.sem_inc(s_, n)

                def body(ch, w):
                    tiles = bass.ds(ch * NQ, w // P)
                    sp.wait_ge(x2_r, ch + 1)
                    sp.dma_start(x2D[:, tiles, :], x2[:, tiles, :]).then_inc(x2_out, 16)
                    sp.wait_ge(pair_r, ch + 1)
                    sp.dma_start(hnD[:, tiles, :, 0:D], pair[:, tiles]).then_inc(pair_out, 16)

                def after(ch, w, par, c):
                    sp.wait_ge(hs_r, ch + 3)
                    for to in (hTD[:, 0, bass.ds(ch * CH, w)], xhTD[:, bass.ds(ch * CH, w)]):
                        sp.dma_start(to, hs[:, par, 0:w]).then_inc(hs_out[par], 16)
                last(sp, body, after)
                for s_, n in ((x2_out, 16 * SC), (pair_out, 16 * SC), (hs_out0, 32 * (SC - SC // 2) + 32),
                              (hs_out1, 32 * (SC // 2) + 32), (z_out, 16)):
                    sp.wait_ge(s_, n)

            @block.tensor
            def _(pe):
                pe.wait_ge(loaded, 48)
                pe.sem_inc(o_r, 1)

                def step(l, ch, w, s):
                    k = w // P
                    half = bass.ds(l % 2, 1)
                    pe.wait_ge(g_r, l * SC + SC)
                    for j in range(T):
                        cols = A[:, j, bass.ds(ch * CH, w)]
                        for part in range(2):
                            nc.tensor.matmul(PS[0][:, 0:w], G[:, half, j, part, :].rearrange("p o d -> p (o d)"), cols,
                                             start=(j == 0 and part == 0), stop=False)
                    for q in range(k):
                        for part in range(2):
                            last = nc.tensor.matmul(PS[0][:, q * P:(q + 1) * P],
                                                    G[:, half, bass.ds(ch * NQ + q, 1), part, :].rearrange("p o a d -> p (o a d)"),
                                                    identh[0:P, 0:P], start=False, stop=(q == k - 1 and part == 1))
                    last.then_inc(agg_r, 1)
                    pe.wait_ge(aT_r, s + 1)
                    pe.wait_ge(y_free, s + 1)
                    for q in range(k):
                        last = nc.tensor.matmul(PS[1][0:P, q * D:(q + 1) * D], aT[:, q * P:(q + 1) * P],
                                                W[:, bass.ds(l, 1), :].rearrange("p o d -> p (o d)"), start=True, stop=True)
                    last.then_inc(o_r, 1)
                steps(pe, step)
                pe.sem_inc(tr_r, 1)

                def after(ch, w, par, c):
                    pe.wait_ge(pair_r, ch + 1)
                    pe.wait_ge(hs_r, ch + 1)
                    for q in range(w // P):
                        last_ = nc.tensor.transpose(PS[2 + par][:, q * P:(q + 1) * P], yb[:, q, :], ident[0:P, 0:P])
                    last_.then_inc(tr_r, 1)
                last(pe, lambda ch, w: step(CL - 1, ch, w, (CL - 1) * SC + ch), after)

            @block.scalar
            def _(act):
                def step(l, ch, w, s):
                    k = w // P
                    act.wait_ge(agg_r, s + 1)
                    act.wait_ge(o_r, s + 1)
                    nc.scalar.activation(aT[:, 0:w], PS[0][:, 0:w], ACT.Copy, scale=1.0 / UP).then_inc(aT_r, 1)
                    act.wait_ge(var_r, s + 1)
                    nc.scalar.activation(st[:, 3, 0:k], st[:, 2, 0:k], ACT.Sqrt).then_inc(root_r, 1)
                steps(act, step)
                act.sem_inc(hs_r, 2)

                def body(ch, w):
                    step(CL - 1, ch, w, (CL - 1) * SC + ch)
                    act.wait_ge(var2, ch + 1)
                    nc.scalar.activation(st[:, 3, 0:w // P], st[:, 2, 0:w // P], ACT.Sqrt).then_inc(root2, 1)

                def after(ch, w, par, c):
                    act.wait_ge(tr_r, ch + 2)
                    act.wait_ge(hs_out[par], 32 * c + 32)
                    nc.scalar.copy(hs[:, par, 0:w], PS[2 + par][:, 0:w]).then_inc(hs_r, 1)
                last(act, body, after)

            @block.vector
            def _(dve):
                V_ = nc.vector
                dve.wait_ge(loaded, 48)
                dve.sem_inc(y_free, 1)
                dn2 = Done(dve, chain2)
                wide = lambda a: a[:, :, None].to_broadcast([P, T, D])
                dn2(V_.tensor_tensor(F[:, 1], xr[:], wide(col[:, 3, :]), ALU.mult))
                dn2(V_.tensor_copy(G[:, 0, :, 0, :], F[:, 1]))
                dn2(V_.tensor_tensor(G[:, 0, :, 1, :], F[:, 1], G[:, 0, :, 0, :], ALU.subtract))
                dve.sem_inc(g_r, SC)
                done = Done(dve, chain)

                def conv(dn, l, ch, w, s):
                    k = w // P
                    tiles = bass.ds(ch * NQ, k)
                    y, xc, sq = ya[:, 0:k, :], yb[:, 0:k, :], yc[:, 0:k, :]
                    dve.wait_ge(o_r, s + 2)
                    dn(V_.tensor_tensor(y, PS[1][0:P, 0:k * D].rearrange("p (k d) -> p k d", d=D),
                                        col[:, 2, tiles][:, :, None].to_broadcast([P, k, D]), ALU.mult))
                    dve.sem_inc(y_free, 1)
                    dn(V_.tensor_tensor(y, y, bias[:, bass.ds(l, 1), :].to_broadcast([P, k, D]), ALU.add))
                    dn(V_.tensor_scalar(y, y, 0.0, None, ALU.max))

                    def mid(ins):
                        ins.then_inc(var_r, 1)
                        dve.wait_ge(root_r, s + 1)
                    norm(V_, dn, mid, y, xc, sq, st[:, :, 0:k], None)
                    dn(V_.tensor_tensor(xr[:, tiles, :], xr[:, tiles, :], xc, ALU.add))

                def counted(step, start, chain_, each):
                    n = [0]

                    def dn(ins):
                        n[0] += 1
                        ins.then_inc(chain_, 1)
                        dve.wait_ge(chain_, start + step * each + n[0])
                    return dn, n

                def step(l, ch, w, s):
                    k = w // P
                    dn, n = counted(s, 0, chain, K_)
                    tiles = bass.ds(ch * NQ, k)
                    y = ya[:, 0:k, :]
                    conv(dn, l, ch, w, s)
                    dn(V_.tensor_tensor(y, xr[:, tiles, :], col[:, 3, tiles][:, :, None].to_broadcast([P, k, D]), ALU.mult))
                    nxt = bass.ds((l + 1) % 2, 1)
                    dn(V_.tensor_copy(G[:, nxt, tiles, 0, :].rearrange("p o k d -> p (o k) d"), y))
                    V_.tensor_tensor(G[:, nxt, tiles, 1, :].rearrange("p o k d -> p (o k) d"), y,
                                     G[:, nxt, tiles, 0, :].rearrange("p o k d -> p (o k) d"), ALU.subtract).then_inc(g_r, 1)
                    dve.wait_ge(g_r, s + 1 + SC)
                    assert n[0] == K_, n[0]
                K_, KL = 17, 31
                steps(dve, step)

                def body(ch, w):
                    k = w // P
                    dn, n = counted(ch, dn2.n, chain2, KL)
                    tiles = bass.ds(ch * NQ, k)
                    y, sq, h, x2t = ya[:, 0:k, :], yc[:, 0:k, :], yb[:, 0:k, :], x2[:, tiles, :]
                    dve.wait_ge(tr_r, ch + 1)
                    conv(dn, CL - 1, ch, w, (CL - 1) * SC + ch)
                    dve.wait_ge(x1_in, 16)
                    dn(V_.tensor_tensor(x2t, x2t, xr[:, tiles, :], ALU.add))
                    dve.sem_inc(x2_r, 1)

                    def mid(ins):
                        ins.then_inc(var2, 1)
                        dve.wait_ge(root2, ch + 1)
                    norm(V_, dn, mid, x2t, y, sq, st[:, :, 0:k], h)
                    dn(V_.tensor_scalar(y, h, UP, None, ALU.mult))
                    dn(V_.tensor_copy(pair[:, tiles, 0, :], y))
                    dn(V_.tensor_tensor(pair[:, tiles, 1, :], y, pair[:, tiles, 0, :], ALU.subtract))
                    dve.sem_inc(pair_r, 1)
                    assert n[0] == KL, n[0]
                last(dve, body, lambda *a: None)


def gru(nc, sem, PS, bih, bhh, scat, scat_sems, scatD, WT, VD, whhD, hnD, hTD, A, ident):
    with ExitStack() as c:
        def sb(name, shape, dt=f32):
            return c.enter_context(nc.sbuf_tensor(name, shape, dt))

        G = sb("G2", [P, T, 2, S2], f16)
        V = sb("V2", [128, 2, GATES])
        U = sb("U2", [128, 2, GATES])
        aT = sb("aT2", [128, 2, CH])
        H = sb("H2", [128, 2, CH])
        HL = sb("HL2", [128, 2, P])
        HN = sb("HN2", [128, 2, CH])
        stg = sb("stg2", [P, NQ, 2, 128], f16)
        bi = sb("bi2", [128, 6])
        bh = sb("bh2", [128, 6])
        bs = sb("bs2", [128, 4])
        names = ("loaded", "G_in", "V_in", "H_in", "HL_in", "agg_r", "aT_r", "r_g", "h_g", "i_g", "z_g", "r_r", "z_r", "n_r", "u1", "u2",
                 "d_r", "dz_r", "hn_r", "hn_out", "tr_r", "hi_r", "lo_r", "st_out", "bs_r", "tick")
        (loaded, G_in, V_in, H_in, HL_in, agg_r, aT_r, r_g, h_g, i_g, z_g, r_r, z_r, n_r, u1, u2,
         d_r, dz_r, hn_r, hn_out, tr_r, hi_r, lo_r, st_out, bs_r, tick) = (sem("g_" + n) for n in names)

        KEPT = (NC - 1) * NQ
        assert NC % 2 == 0

        def run(eng, sums, gates, late, copy=lambda *a: None, end=lambda l: None):
            def layer(l, halves):
                s = l * SC
                sums(l, 0, CH, s, halves, 0)
                copy(l, 0, CH, s, halves, 0)
                sums(l, 1, CH, s + 1, halves, 1)
                gates(l, 0, CH, s, halves, 0)
                copy(l, 1, CH, s + 1, halves, 1)
                with eng.Fori(1, NC // 2) as c:
                    for q in range(2):
                        ch = 2 * c + q
                        sums(l, ch, CH, s + ch, halves, q)
                        late(l, ch - 2, CH, s + ch - 2)
                        gates(l, ch - 1, CH, s + ch - 1, halves, 1 - q)
                        copy(l, ch, CH, s + ch, halves, q)
                sums(l, NC, P, s + NC, halves, 0)
                late(l, NC - 2, CH, s + NC - 2)
                gates(l, NC - 1, CH, s + NC - 1, halves, 1)
                copy(l, NC, P, s + NC, halves, 0)
                late(l, NC - 1, CH, s + NC - 1)
                gates(l, NC, P, s + NC, halves, 0)
                end(l)
            layer(0, 1)
            with eng.Fori(1, GL) as l:
                layer(l, 2)
            late(GL - 1, NC, P, GL * SC - 1)

        SUMS = ((PS[0], PS[1]), (PS[7], PS[1]))

        def direct(ch):
            return isinstance(ch, int) and ch >= NC - 1

        def stored(l, ch, hf):
            return 2 * (NC - 1) * l + 2 * ch + hf

        with nc.Block() as block:
            @block.gpsimd
            def _(pool):
                scatter(nc, pool, scat_sems, scat, scatD, WT, SPLIT, NBATCH)

            @block.sync
            def _(sp):
                for t in (slice(0, KEPT), slice(KEPT, T)):
                    sp.dma_start(G[:, t, :, 0:D], hnD[:, t, :, 0:D]).then_inc(G_in, 16)
                sp.dma_start(V[:], VD[0].rearrange("p (a g) -> p a g", a=2)).then_inc(V_in, 16)
                sp.dma_start(U[:], whhD.rearrange("p (a g) -> p a g", a=2)).then_inc(loaded, 16)
                sp.dma_start(bi[:], bih.rearrange("(c p) -> p c", p=128), allow_slow_non_contiguous=True).then_inc(loaded, 16)
                sp.dma_start(bh[:], bhh.rearrange("(c p) -> p c", p=128), allow_slow_non_contiguous=True).then_inc(loaded, 16)

                def store(l, ch, k, s, hf):
                    if direct(ch):
                        return
                    sp.wait_ge(lo_r, 2 * s + hf + 3)
                    sp.dma_start(hnD[:, bass.ds(ch * NQ, k), :, hf * 128:(hf + 1) * 128], stg[:, 0:k]).then_inc(st_out, 16)

                def state(ch, s):
                    sp.wait_ge(hn_r, 2 * s + 1)
                    sp.sem_inc(tick, 1)
                    sp.wait_ge(z_g, 2 * s + 3)
                    sp.wait_ge(hn_out, 32 * s + 32)
                    sp.dma_start(H[:], hTD[:, :, bass.ds(ch * CH, CH)]).then_inc(H_in, 16)

                def sums(l, ch, w, s, halves, par):
                    if not (isinstance(ch, int) and ch == 0):
                        state(ch - 1, s - 1)
                    if w != CH:
                        sp.dma_start(HL[:], hTD[:, :, NC * CH:N]).then_inc(HL_in, 16)
                        sp.wait_ge(agg_r, s + 1)
                        sp.wait_ge(st_out, 16 * stored(l, NC - 2, 0) + 16)
                        sp.dma_start(G[:, 0:KEPT - NQ], hnD[:, 0:KEPT - NQ]).then_inc(G_in, 16)

                def gates(l, ch, w, s, halves, par):
                    for hf in range(2):
                        sp.wait_ge(hn_r, 2 * s + hf + 2)
                        sp.dma_start(hTD[:, hf, bass.ds(ch * CH, w)], HN[:, hf, 0:w]).then_inc(hn_out, 16)
                    store(l, ch, w // P, s, 0)

                def late(l, ch, w, s):
                    store(l, ch, w // P, s, 1)
                    if isinstance(ch, int) and ch == NC - 2:
                        sp.wait_ge(st_out, 16 * stored(l, NC - 1, 0) + 16)
                        sp.dma_start(G[:, KEPT - NQ:KEPT], hnD[:, KEPT - NQ:KEPT]).then_inc(G_in, 16)

                def end(l):
                    nxt = (l + 1) % GL
                    sp.wait_ge(z_g, 2 * SC * l + 2 * SC + 3)
                    sp.dma_start(V[:].rearrange("p a g -> p (a g)"), VD[bass.ds(nxt, 1)].rearrange("o p g -> (o p) g")).then_inc(V_in, 16)
                sp.sem_inc(st_out, 16)
                sp.sem_inc(hn_out, 32)
                run(sp, sums, gates, late, end=end)
                sp.wait_ge(G_in, 32 * GL + 32)
                sp.wait_ge(V_in, 16 * GL + 16)
                sp.wait_ge(hn_out, 32 * SC * GL + 32)

            @block.tensor
            def _(pe):
                pe.sem_inc(z_g, 3)
                pe.sem_inc(tr_r, 1)
                pe.wait_ge(loaded, 48)

                def turn(e, hf, k):
                    pe.wait_ge(hn_r, e + 2)
                    pe.wait_ge(lo_r, e + 2)
                    for q in range(k):
                        last = nc.tensor.transpose(PS[6][0:P, q * 128:(q + 1) * 128], HN[:, hf, q * P:(q + 1) * P], ident[:])
                    last.then_inc(tr_r, 1)

                def sums(l, ch, w, s, halves, par):
                    first = isinstance(ch, int) and ch == 0
                    pe.wait_ge(aT_r, 2 * s + 2 if first else 2 * s + 1)
                    pe.wait_ge(G_in, 32 * l + 32)
                    for lo, hi in ((0, KEPT), (KEPT, T)) if first and halves == 2 else ((0, T),):
                        if lo:
                            late(l, NC, P, s - 1)
                            pe.wait_ge(lo_r, 2 * s + 2)
                        for half in range(halves):
                            if half and not lo:
                                pe.wait_ge(aT_r, 2 * s + 2)
                            for j in range(lo, hi):
                                for part in range(2):
                                    last = nc.tensor.matmul(SUMS[par][half][:, 0:w], G[:, j, part, half * 128:(half + 1) * 128],
                                                            A[:, j, bass.ds(ch * CH, w)],
                                                            start=(j == 0 and part == 0), stop=(j == T - 1 and part == 1))
                    last.then_inc(agg_r, 1)

                def gates(l, ch, w, s, halves, par):
                    h = H if w == CH else HL
                    pe.wait_ge(aT_r, 2 * s + 4)
                    if w == CH:
                        pe.wait_ge(H_in, 16 * (NC * l + ch) + 16)
                    else:
                        pe.wait_ge(HL_in, 16 * l + 16)
                    pe.wait_ge(V_in, 16 * l + 16)
                    for hf in range(2):
                        m = 2 * s + hf

                        def gate(bank, free, ready, g, terms):
                            pe.wait_ge(free, m + 1)
                            terms = [(wt, a, kt) for wt, a in terms for kt in range(halves)]
                            for n, (wt, a, kt) in enumerate(terms):
                                last = nc.tensor.matmul(PS[bank][:, 0:w], wt[:, kt, g:g + 128], a[:, kt, 0:w],
                                                        start=(n == 0), stop=(n == len(terms) - 1))
                            last.then_inc(ready, 1)
                        gate(3, u1, h_g, 2 * S2 + hf * 128, ((U, h),))
                        gate(2, r_r, r_g, hf * 128, ((U, h), (V, aT)))
                        gate(4, hn_r, i_g, 2 * S2 + hf * 128, ((V, aT),))
                        gate(5, dz_r, z_g, S2 + hf * 128, ((V, aT), (U, h)))
                    turn(2 * s, 0, w // P)

                def late(l, ch, w, s):
                    turn(2 * s + 1, 1, w // P)
                run(pe, sums, gates, late)

            @block.scalar
            def _(act):
                act.wait_ge(bs_r, 1)
                act.sem_inc(r_r, 1)

                def high(l, ch, w, s, hf):
                    e, k = 2 * s + hf, w // P
                    act.wait_ge(tr_r, e + 2)
                    if direct(ch):
                        act.wait_ge(agg_r, l * SC + SC)
                        to = G[:, ch * NQ:ch * NQ + k, 0, hf * 128:(hf + 1) * 128]
                    else:
                        act.wait_ge(st_out, 16 * stored(l, ch, hf) + 16)
                        to = stg[:, 0:k, 0, :]
                    nc.scalar.activation(to, PS[6][0:P, 0:k * 128].rearrange("p (k d) -> p k d", k=k),
                                         ACT.Copy, scale=UP).then_inc(hi_r, 1)

                def copy(l, ch, w, s, halves, par):
                    first = isinstance(ch, int) and ch == 0
                    if first and halves == 2:
                        late(l - 1, NC, P, s - 1)
                    act.wait_ge(agg_r, s + 1)
                    act.wait_ge(z_g, 2 * s + 3)
                    for half in range(halves):
                        nc.scalar.activation(aT[:, half, 0:w], SUMS[par][half][:, 0:w], ACT.Copy, scale=1.0 / UP).then_inc(aT_r, 2 // halves)

                def gates(l, ch, w, s, halves, par):
                    act.wait_ge(hn_out, 32 * s + 32)
                    act.wait_ge(tr_r, 2 * s + 1)
                    for hf in range(2):
                        m = 2 * s + hf
                        act.wait_ge(r_g, m + 1)
                        nc.scalar.activation(HN[:, hf, 0:w], PS[2][:, 0:w], ACT.Sigmoid, bias=bs[:, hf:hf + 1]).then_inc(r_r, 1)
                        act.wait_ge(z_g, m + 4)
                        nc.scalar.activation(PS[5][:, 0:w], PS[5][:, 0:w], ACT.Sigmoid, bias=bs[:, 2 + hf:3 + hf]).then_inc(z_r, 1)
                        act.wait_ge(u2, m + 1)
                        nc.scalar.activation(HN[:, hf, 0:w], HN[:, hf, 0:w], ACT.Tanh, bias=bi[:, 4 + hf:5 + hf]).then_inc(n_r, 1)
                    high(l, ch, w, s, 0)

                def late(l, ch, w, s):
                    high(l, ch, w, s, 1)
                act.sem_inc(aT_r, 2)
                run(act, lambda *a: None, gates, late, copy)

            @block.vector
            def _(dve):
                V_ = nc.vector
                dve.wait_ge(loaded, 48)
                V_.tensor_tensor(bs[:], bi[:, 0:4], bh[:, 0:4], ALU.add).then_inc(bs_r, 1)
                for s_, n in ((u1, 1), (dz_r, 1), (hn_r, 1), (lo_r, 2)):
                    dve.sem_inc(s_, n)

                def low(l, ch, w, s, hf):
                    e, k = 2 * s + hf, w // P
                    dve.wait_ge(hi_r, e + 1)
                    if direct(ch):
                        high, to = (G[:, ch * NQ:ch * NQ + k, part, hf * 128:(hf + 1) * 128] for part in range(2))
                    else:
                        high, to = stg[:, 0:k, 0, :], stg[:, 0:k, 1, :]
                    V_.scalar_tensor_tensor(to, PS[6][0:P, 0:k * 128].rearrange("p (k d) -> p k d", k=k), UP,
                                            high, ALU.mult, ALU.subtract).then_inc(lo_r, 1)

                def sums(l, ch, w, s, halves, par):
                    if isinstance(ch, int) and ch == 0 and halves == 2:
                        late(l - 1, NC, P, s - 1)

                def gates(l, ch, w, s, halves, par):
                    h = H if w == CH else HL
                    if w == CH:
                        dve.wait_ge(H_in, 16 * (NC * l + ch) + 16)
                    else:
                        dve.wait_ge(HL_in, 16 * l + 16)
                    for hf in range(2):
                        m = 2 * s + hf
                        dve.wait_ge(r_r, m + 2)
                        dve.wait_ge(h_g, m + 1)
                        n, d = HN[:, hf, 0:w], PS[4][:, 0:w]
                        V_.scalar_tensor_tensor(n, PS[3][:, 0:w], bh[:, 4 + hf:5 + hf], n, ALU.add, ALU.mult).then_inc(u1, 1)
                        dve.wait_ge(u1, m + 2)
                        dve.wait_ge(i_g, m + 1)
                        V_.tensor_tensor(n, n, PS[4][:, 0:w], ALU.add).then_inc(u2, 1)
                        dve.wait_ge(u2, m + 1)
                        dve.wait_ge(z_r, m + 1)
                        V_.tensor_tensor(d, PS[5][:, 0:w], h[:, hf, 0:w], ALU.mult).then_inc(d_r, 1)
                        dve.wait_ge(n_r, m + 1)
                        V_.scalar_tensor_tensor(n, PS[5][:, 0:w], -1.0, n, ALU.add, ALU.mult).then_inc(dz_r, 1)
                        dve.wait_ge(d_r, m + 1)
                        dve.wait_ge(dz_r, m + 2)
                        V_.tensor_tensor(n, d, n, ALU.subtract).then_inc(hn_r, 1)
                    low(l, ch, w, s, 0)

                def late(l, ch, w, s):
                    low(l, ch, w, s, 1)
                run(dve, sums, gates, late)


def tail(nc, sem, PS, big, l0b, l1b, b1, b2, out, WT, l0D, l1D, w12D, x2D, hTD, xhTD):
    with ExitStack() as c:
        sb = pieces(big)
        RING = 5
        wt = sb("wt", [128, RING, N])
        hT = sb("hT3", [128, 2, 2, CH])
        xT = sb("xT3", [128, 2, CH])
        x3 = sb("x3", [P, T, D])
        xc = sb("xc3", [P, T, D])
        sq = sb("sq3", [P, T, D])
        st = sb("st3", [P, 4, T])
        x3T = sb("x3T", [128, N])
        y0 = sb("y0", [128, 2, CH])
        y1 = sb("y1", [128, CH])
        a = sb("a3", [128, 2, CH])
        b = sb("b3", [128, 2, CH])
        o = sb("o3", [P, 2, NQ, D])
        L0, L1, W = sb("L0", [128, 3, 256]), sb("L1", [128, 2, 128]), sb("W3", [128, 2, D])
        bl0, bl1 = sb("bl0", [128, 2]), sb("bl1", [128, 1])
        bb = sb("bb", [P, 2, D])
        ident = sb("ident3", [128, 128])
        names = ("made", "loaded", "h0", "h1", "m0", "a0", "m1", "a1", "tr", "x_r", "var_r", "root_r", "chain", "xh_r", "t2", "t2c",
                 "agg", "a_r", "b_r", "o_g", "o_r", "out0", "out1", "bias_r", "w_used", "o1", "o2")
        (made, loaded, h0, h1, m0, a0, m1, a1, tr, x_r, var_r, root_r, chain, xh_r, t2, t2c,
         agg, a_r, b_r, o_g, o_r, out0, out1, bias_r, w_used, o1, o2) = (sem("t_" + n) for n in names)
        w_in = [sem(f"t_w{i}") for i in range(RING)]
        outs = (out0, out1)
        h_in = (h0, h1)
        wid = lambda ch: min(CH, N - ch * CH)
        ot = out.rearrange("(k p) d -> p k d", p=P)

        with nc.Block() as block:
            @block.gpsimd
            def _(pool):
                nc.gpsimd.memset(ident[:], 0.0).then_inc(made, 1)
                pool.wait_ge(made, 1)
                nc.gpsimd.affine_select(out=ident[:], in_=ident[:], compare_op=ALU.not_equal, fill=1.0,
                                        base=0, pattern=[[-1, 128]], channel_multiplier=1).then_inc(made, 1)

            @block.sync
            def _(sp):
                for to, frm in ((L0, l0D), (L1, l1D), (W, w12D)):
                    sp.dma_start(to[:].rearrange("p a b -> p (a b)"), frm).then_inc(loaded, 16)
                sp.dma_start(bl0[:], l0b.rearrange("(c p) -> p c", p=128), allow_slow_non_contiguous=True).then_inc(loaded, 16)
                sp.dma_start(bl1[:], l1b.rearrange("(c p) -> p c", p=128), allow_slow_non_contiguous=True).then_inc(loaded, 16)
                for n, v in enumerate((b1, b2)):
                    sp.dma_start(bb[:, n, :], v.rearrange("(o d) -> o d", o=1).to_broadcast([P, D])).then_inc(loaded, 16)
                sp.dma_start(x3[:], x2D).then_inc(loaded, 16)
                for ch in range(SC):
                    w = wid(ch)
                    if ch >= 2:
                        sp.wait_ge(m0, ch - 1)
                    sp.dma_start(hT[:, ch % 2, :, 0:w], hTD[:, :, ch * CH:ch * CH + w]).then_inc(h_in[ch % 2], 16)
                    sp.dma_start(xT[:, ch % 2, 0:w], xhTD[:, ch * CH:ch * CH + w]).then_inc(h_in[ch % 2], 16)
                for ch in range(SC):
                    sp.wait_ge(o_r, ch + 1)
                    k = wid(ch) // P
                    sp.dma_start(ot[:, ch * NQ:ch * NQ + k, :], o[:, ch % 2, 0:k, :]).then_inc(outs[ch % 2], 16)
                sp.wait_ge(out0, 16 * (SC - SC // 2))
                sp.wait_ge(out1, 16 * (SC // 2))

            @block.scalar
            def _(act):
                rows = WT.rearrange("n o -> (n o)")

                def load(g, i):
                    act.dma_start(wt[:, i, :], rows[bass.ds((g * RING + i) * P * N, 128 * N)].rearrange("(p n) -> p n", n=N)).then_inc(w_in[i], 16)
                act.wait_ge(loaded, 16 * 8)

                def root(ch):
                    act.wait_ge(var_r, ch + 1)
                    tiles = slice(ch * NQ, ch * NQ + wid(ch) // P)
                    nc.scalar.activation(st[:, 3, tiles], st[:, 2, tiles], ACT.Sqrt).then_inc(root_r, 1)

                def copy(ch):
                    w = wid(ch)
                    act.wait_ge(t2, ch + 1)
                    nc.scalar.copy(x3T[:, ch * CH:ch * CH + w], PS[6 + ch % 2][:, 0:w]).then_inc(t2c, 1)
                for ch in range(SC):
                    w = wid(ch)
                    act.wait_ge(m0, ch + 1)
                    if ch:
                        act.wait_ge(m1, ch)
                    for h in range(2):
                        last = nc.scalar.activation(y0[:, h, 0:w], PS[h][:, 0:w], ACT.Relu, bias=bl0[:, h:h + 1])
                    last.then_inc(a0, 1)
                    if ch:
                        root(ch - 1)
                    act.wait_ge(m1, ch + 1)
                    if ch:
                        act.wait_ge(tr, ch)
                    nc.scalar.activation(y1[:, 0:w], PS[2][:, 0:w], ACT.Relu, bias=bl1[:, 0:1]).then_inc(a1, 1)
                    if ch:
                        copy(ch - 1)
                    if ch < RING:
                        load(0, ch)
                root(SC - 1)
                copy(SC - 1)
                with act.Fori(1, T // RING) as g:
                    for i in range(RING):
                        act.wait_ge(w_used, g * RING + i - (RING - 1))
                        load(g, i)

            @block.tensor
            def _(pe):
                pe.wait_ge(made, 2)
                pe.wait_ge(loaded, 16 * 8)

                def turn(ch):
                    pe.wait_ge(xh_r, ch + 1)
                    if ch >= 2:
                        pe.wait_ge(t2c, ch - 1)
                    for q in range(wid(ch) // P):
                        last = nc.tensor.transpose(PS[6 + ch % 2][:, q * P:(q + 1) * P], xc[:, ch * NQ + q, :], ident[0:P, 0:P])
                    last.then_inc(t2, 1)
                for ch in range(SC):
                    w = wid(ch)
                    pe.wait_ge(h_in[ch % 2], 32 * (ch // 2) + 32)
                    if ch:
                        pe.wait_ge(a0, ch)
                    for h in range(2):
                        for kt, v in enumerate((hT[:, ch % 2, 0, 0:w], hT[:, ch % 2, 1, 0:w], xT[:, ch % 2, 0:w])):
                            last = nc.tensor.matmul(PS[h][:, 0:w], L0[:, kt, h * 128:(h + 1) * 128], v, start=(kt == 0), stop=(kt == 2))
                    last.then_inc(m0, 1)
                    pe.wait_ge(a0, ch + 1)
                    if ch:
                        pe.wait_ge(a1, ch)
                    for kt in range(2):
                        last = nc.tensor.matmul(PS[2][:, 0:w], L1[:, kt, :], y0[:, kt, 0:w], start=(kt == 0), stop=(kt == 1))
                    last.then_inc(m1, 1)
                    pe.wait_ge(a1, ch + 1)
                    if ch:
                        pe.wait_ge(x_r, ch)
                    for q in range(w // P):
                        last = nc.tensor.transpose(PS[3][0:P, q * 128:(q + 1) * 128], y1[:, q * P:(q + 1) * P], ident[:])
                    last.then_inc(tr, 1)
                    if ch:
                        turn(ch - 1)
                turn(SC - 1)
                pe.wait_ge(t2c, SC)

                def tile(g, i, start=False, stop=False):
                    pe.wait_ge(w_in[i], 16 * g + 16)
                    for ch in range(SC):
                        w = wid(ch)
                        last = nc.tensor.matmul(PS[ch][:, 0:w], xc[:, g * RING + i, :], wt[0:P, i, ch * CH:ch * CH + w], start=start, stop=stop)
                    last.then_inc(w_used, 1)
                for g in range(T // RING):
                    for i in range(RING):
                        tile(g, i, start=(g == 0 and i == 0), stop=(g == T // RING - 1 and i == RING - 1))
                for ch in range(SC):
                    k = wid(ch) // P
                    pe.wait_ge(a_r, ch + 1)
                    pe.wait_ge(b_r, ch + 1)
                    for q in range(k):
                        for n, v in enumerate((a, b)):
                            last = nc.tensor.matmul(PS[ch][0:P, q * D:(q + 1) * D], v[:, ch % 2, q * P:(q + 1) * P], W[:, n, :], start=(n == 0), stop=(n == 1))
                    last.then_inc(o_g, 1)

            @block.vector
            def _(dve):
                V_ = nc.vector
                dn = Done(dve, chain)
                dve.wait_ge(loaded, 16 * 8)
                dn(V_.tensor_tensor(bb[:, 0, :], bb[:, 0, :], bb[:, 1, :], ALU.add))
                for ch in range(SC):
                    k = wid(ch) // P
                    dve.wait_ge(tr, ch + 1)
                    v = x3[:, ch * NQ:ch * NQ + k, :]
                    V_.tensor_tensor(v, v, PS[3][0:P, 0:k * D].rearrange("p (k d) -> p k d", d=D), ALU.add).then_inc(x_r, 1)
                    dve.wait_ge(x_r, ch + 1)

                    def mid(ins):
                        ins.then_inc(var_r, 1)
                        dve.wait_ge(root_r, ch + 1)
                    t = slice(ch * NQ, ch * NQ + k)
                    norm(V_, dn, mid, v, xc[:, t, :], sq[:, t, :], st[:, :, t], xc[:, t, :])
                    dve.sem_inc(xh_r, 1)
                dve.wait_ge(w_used, T)
                dve.wait_ge(t2c, SC)

                def finish(ch):
                    k = wid(ch) // P
                    dve.wait_ge(o_g, ch + 1)
                    if ch >= 2:
                        dve.wait_ge(outs[ch % 2], 16 * (ch // 2))
                    v = o[:, ch % 2, 0:k, :]
                    V_.tensor_tensor(v, PS[ch][0:P, 0:k * D].rearrange("p (k d) -> p k d", d=D), bb[:, 0:1, :].to_broadcast([P, k, D]), ALU.add).then_inc(o1, 1)
                    dve.wait_ge(o1, ch + 1)
                    V_.scalar_tensor_tensor(v, v, ALPHA, v, ALU.mult, ALU.max).then_inc(o2, 1)
                    dve.wait_ge(o2, ch + 1)
                    V_.tensor_tensor(v, v, x3[:, ch * NQ:ch * NQ + k, :], ALU.add).then_inc(o_r, 1)
                for ch in range(SC):
                    w = wid(ch)
                    if ch >= 2:
                        dve.wait_ge(o_g, ch - 1)
                    t = x3T[:, ch * CH:ch * CH + w]
                    V_.tensor_tensor(a[:, ch % 2, 0:w], PS[ch][:, 0:w], t, ALU.add).then_inc(a_r, 1)
                    V_.tensor_tensor(b[:, ch % 2, 0:w], PS[ch][:, 0:w], t, ALU.mult).then_inc(b_r, 1)
                    if ch:
                        finish(ch - 1)
                finish(SC - 1)


_INS = ['x', 'src', 'dst', 'edge_weight', 'L0_gnn_W', 'L0_gnn_a', 'L1_gnn_W', 'L1_gnn_b', 'L2_gnn_W',
        'L2_gnn_w_ih', 'L2_gnn_w_hh', 'L2_gnn_b_ih', 'L2_gnn_b_hh', 'L2_gnn_l0_w', 'L2_gnn_l0_b',
        'L2_gnn_l1_w', 'L2_gnn_l1_b', 'L3_gnn_W1', 'L3_gnn_b1', 'L3_gnn_W2', 'L3_gnn_b2']


def kernel(**inputs):
    import numpy as _np
    import concourse.bacc as _bacc
    from concourse import mybir as _mybir
    from concourse.bass_utils import run_bass_kernel_spmd as _run

    nc = _bacc.Bacc("TRN2", target_bir_lowering=False, num_devices=1)
    arrays, args = {}, []
    for name in _INS:
        a = _np.ascontiguousarray(inputs[name])
        arrays[f"in_{name}_dram"] = a
        args.append(nc.dram_tensor(f"in_{name}_dram", a.shape, _mybir.dt.from_np(a.dtype), kind="ExternalInput").ap())
    args.append(nc.dram_tensor("out_0_dram", (N, D), f32, kind="ExternalOutput").ap())
    gnn_kernel(nc, *args)
    r = _run(nc, [arrays], core_ids=[0])
    return r.results[0]["out_0_dram"]
```
